# Optimizing a Trainium2 kernel written in Bass

```python
import numpy as np
import jax
import jax.numpy as jnp

def _softmax(x, axis=-1):
    return jax.nn.softmax(x, axis=axis)

def _gelu(x):
    return jax.nn.gelu(x, approximate=True)

def _silu(x):
    return jax.nn.silu(x)

def _sigmoid(x):
    return jax.nn.sigmoid(x)

def _layernorm(x, axis=-1, eps=1e-05):
    m = jnp.mean(x, axis=axis, keepdims=True)
    v = jnp.var(x, axis=axis, keepdims=True)
    return (x - m) / jnp.sqrt(v + eps)

def _scatter_add(tgt, idx, src, axis=0):
    return tgt.at[idx].add(src)

def _segment_sum(src, seg, n):
    return jax.ops.segment_sum(src, seg, n)
kernel_name = 'mk_hybrid_d1_jaxref_r4_6315c4'

def setup_inputs(seed: int=0):
    np.random.seed(seed)
    _w = jnp.asarray

    def _L0_attn_a_setup():
        import jax, jax.numpy as jnp
        import numpy as np
        import math
        B, S, H, NH = (2, 512, 256, 16)
        DK = H // NH
        key = jax.random.key(seed)
        k1, k2, k3 = jax.random.split(key, 3)
        scale = 1.0 / math.sqrt(H)
        return {'x': jax.random.normal(k1, (B, S, H), dtype=jnp.float32), 'w_attn': jax.random.normal(k2, (H, 3 * H), dtype=jnp.float32) * scale, 'b_attn': jnp.zeros((3 * H,), dtype=jnp.float32), 'w_proj': jax.random.normal(k3, (H, H), dtype=jnp.float32) * scale, 'b_proj': jnp.zeros((H,), dtype=jnp.float32)}
    _L0_attn_a_in = _L0_attn_a_setup()

    def _L0_attn_b_setup():
        import jax, jax.numpy as jnp
        import numpy as np
        B, T, C, H = (2, 512, 256, 16)
        D = C // H
        RW, RA, RG = (64, 64, 128)
        EPS = 1e-05

        def _rwkv7_scan(r, log_w, k, v, a, b):
            Bn, Tn, Hn, Dn = r.shape

            def step(S, xs):
                r_t, w_t, k_t, v_t, a_t, b_t = xs
                sa = jnp.einsum('bhij,bhj->bhi', S, a_t)
                S = S * jnp.exp(w_t)[:, :, None, :] + sa[..., None] * b_t[:, :, None, :] + v_t[..., None] * k_t[:, :, None, :]
                o_t = jnp.einsum('bhij,bhj->bhi', S, r_t)
                return (S, o_t)
            S0 = jnp.zeros((Bn, Hn, Dn, Dn), r.dtype)
            xs = tuple((jnp.swapaxes(x, 0, 1) for x in (r, log_w, k, v, a, b)))
            _, o = jax.lax.scan(step, S0, xs)
            return jnp.swapaxes(o, 0, 1)
        key = jax.random.key(seed)
        ks = iter(jax.random.split(key, 40))
        n = lambda s, sc=0.02: jax.random.normal(next(ks), s, jnp.float32) * sc
        u = lambda s: jax.random.uniform(next(ks), s, jnp.float32)
        return dict(hidden_states=jax.random.normal(next(ks), (B, T, C), jnp.float32), x_r=u((C,)), x_w=u((C,)), x_k=u((C,)), x_v=u((C,)), x_a=u((C,)), x_g=u((C,)), k_k=u((C,)), k_a=u((C,)), r_k=n((H, D), 0.1), W_r=n((C, C)), W_k=n((C, C)), W_v=n((C, C)), W_o=n((C, C)), w_lora_a=n((C, RW)), w_lora_b=n((RW, C)), w_lora_bias=n((C,), 0.1), a_lora_a=n((C, RA)), a_lora_b=n((RA, C)), a_lora_bias=jnp.zeros((C,), jnp.float32), g_lora_a=n((C, RG)), g_lora_b=n((RG, C)), g_lora_bias=jnp.zeros((C,), jnp.float32), gn_weight=jnp.ones((C,), jnp.float32), gn_bias=jnp.zeros((C,), jnp.float32))
    _L0_attn_b_in = _L0_attn_b_setup()

    def _L0_ffn_setup():
        import jax, jax.numpy as jnp
        import numpy as np
        B, L, H, E, I = (4, 512, 256, 8, 1024)
        S = B * L
        CAP_FACTOR_EVAL = 2.0
        MIN_CAP = 4
        _cap = int(np.floor(CAP_FACTOR_EVAL * S / E))
        _cap += _cap % 2
        CAPACITY = max(_cap, MIN_CAP)

        def _layer_norm(x, g, b, eps=1e-05):
            mu = x.mean(-1, keepdims=True)
            var = ((x - mu) ** 2).mean(-1, keepdims=True)
            return (x - mu) * jax.lax.rsqrt(var + eps) * g + b
        key = jax.random.key(seed)
        ks = jax.random.split(key, 8)
        gate_std = float(np.sqrt(0.1 / H))
        return {'inputs': jax.random.normal(ks[0], (B, L, H), jnp.float32), 'gate_weight': jax.random.normal(ks[1], (E, H), jnp.float32) * gate_std, 'ln_gamma': jnp.ones((H,), jnp.float32), 'ln_beta': jnp.zeros((H,), jnp.float32), 'wi': jax.random.normal(ks[2], (E, H, I), jnp.float32) * float(1.0 / np.sqrt(H)), 'wo': jax.random.normal(ks[3], (E, I, H), jnp.float32) * float(1.0 / np.sqrt(I)), 'conf_w1': jax.random.normal(ks[4], (H // 2, H), jnp.float32) * float(np.sqrt(2.0 / (H + H // 2))), 'conf_b1': -jnp.ones((H // 2,), jnp.float32), 'conf_w2': jax.random.normal(ks[5], (1, H // 2), jnp.float32) * float(np.sqrt(2.0 / (1 + H // 2))), 'conf_b2': -jnp.ones((1,), jnp.float32), 'comp_w': jax.random.normal(ks[6], (1, H), jnp.float32) * float(1.0 / np.sqrt(H)), 'comp_b': jnp.zeros((1,), jnp.float32)}
    _L0_ffn_in = _L0_ffn_setup()
    _d = {'L0_attn_a_x': _L0_attn_a_in['x'], 'L0_attn_a_w_attn': _L0_attn_a_in['w_attn'], 'L0_attn_a_b_attn': _L0_attn_a_in['b_attn'], 'L0_attn_a_w_proj': _L0_attn_a_in['w_proj'], 'L0_attn_a_b_proj': _L0_attn_a_in['b_proj'], 'L0_attn_b_x_r': _L0_attn_b_in['x_r'], 'L0_attn_b_x_w': _L0_attn_b_in['x_w'], 'L0_attn_b_x_k': _L0_attn_b_in['x_k'], 'L0_attn_b_x_v': _L0_attn_b_in['x_v'], 'L0_attn_b_x_a': _L0_attn_b_in['x_a'], 'L0_attn_b_x_g': _L0_attn_b_in['x_g'], 'L0_attn_b_k_k': _L0_attn_b_in['k_k'], 'L0_attn_b_k_a': _L0_attn_b_in['k_a'], 'L0_attn_b_r_k': _L0_attn_b_in['r_k'], 'L0_attn_b_W_r': _L0_attn_b_in['W_r'], 'L0_attn_b_W_k': _L0_attn_b_in['W_k'], 'L0_attn_b_W_v': _L0_attn_b_in['W_v'], 'L0_attn_b_W_o': _L0_attn_b_in['W_o'], 'L0_attn_b_w_lora_a': _L0_attn_b_in['w_lora_a'], 'L0_attn_b_w_lora_b': _L0_attn_b_in['w_lora_b'], 'L0_attn_b_w_lora_bias': _L0_attn_b_in['w_lora_bias'], 'L0_attn_b_a_lora_a': _L0_attn_b_in['a_lora_a'], 'L0_attn_b_a_lora_b': _L0_attn_b_in['a_lora_b'], 'L0_attn_b_a_lora_bias': _L0_attn_b_in['a_lora_bias'], 'L0_attn_b_g_lora_a': _L0_attn_b_in['g_lora_a'], 'L0_attn_b_g_lora_b': _L0_attn_b_in['g_lora_b'], 'L0_attn_b_g_lora_bias': _L0_attn_b_in['g_lora_bias'], 'L0_attn_b_gn_weight': _L0_attn_b_in['gn_weight'], 'L0_attn_b_gn_bias': _L0_attn_b_in['gn_bias'], 'L0_ffn_gate_weight': _L0_ffn_in['gate_weight'], 'L0_ffn_ln_gamma': _L0_ffn_in['ln_gamma'], 'L0_ffn_ln_beta': _L0_ffn_in['ln_beta'], 'L0_ffn_wi': _L0_ffn_in['wi'], 'L0_ffn_wo': _L0_ffn_in['wo'], 'L0_ffn_conf_w1': _L0_ffn_in['conf_w1'], 'L0_ffn_conf_b1': _L0_ffn_in['conf_b1'], 'L0_ffn_conf_w2': _L0_ffn_in['conf_w2'], 'L0_ffn_conf_b2': _L0_ffn_in['conf_b2'], 'L0_ffn_comp_w': _L0_ffn_in['comp_w'], 'L0_ffn_comp_b': _L0_ffn_in['comp_b']}
    _x0 = _d['L0_attn_a_x']
    _d['L0_attn_a_x'] = jax.random.normal(jax.random.fold_in(jax.random.key(seed), 1), (8, 1024, 256), dtype=_x0.dtype)
    del _x0
    return _d

def reference(L0_attn_a_x, L0_attn_a_w_attn, L0_attn_a_b_attn, L0_attn_a_w_proj, L0_attn_a_b_proj, L0_attn_b_x_r, L0_attn_b_x_w, L0_attn_b_x_k, L0_attn_b_x_v, L0_attn_b_x_a, L0_attn_b_x_g, L0_attn_b_k_k, L0_attn_b_k_a, L0_attn_b_r_k, L0_attn_b_W_r, L0_attn_b_W_k, L0_attn_b_W_v, L0_attn_b_W_o, L0_attn_b_w_lora_a, L0_attn_b_w_lora_b, L0_attn_b_w_lora_bias, L0_attn_b_a_lora_a, L0_attn_b_a_lora_b, L0_attn_b_a_lora_bias, L0_attn_b_g_lora_a, L0_attn_b_g_lora_b, L0_attn_b_g_lora_bias, L0_attn_b_gn_weight, L0_attn_b_gn_bias, L0_ffn_gate_weight, L0_ffn_ln_gamma, L0_ffn_ln_beta, L0_ffn_wi, L0_ffn_wo, L0_ffn_conf_w1, L0_ffn_conf_b1, L0_ffn_conf_w2, L0_ffn_conf_b2, L0_ffn_comp_w, L0_ffn_comp_b):

    def _L0_attn_a_ref(x, w_attn, b_attn, w_proj, b_proj):
        import jax, jax.numpy as jnp
        import numpy as np
        import math
        B, S, H, NH = (2, 512, 256, 16)
        DK = H // NH
        bs, seq_len, hidden = x.shape
        qkv = x @ w_attn + b_attn
        q, k, v = jnp.split(qkv, 3, axis=-1)

        def heads(t):
            return t.reshape(bs, seq_len, NH, DK).transpose(0, 2, 1, 3)
        q, k, v = (heads(q), heads(k), heads(v))
        scores = jnp.einsum('bhqd,bhkd->bhqk', q, k) / math.sqrt(DK)
        causal = jnp.tril(jnp.ones((seq_len, seq_len), dtype=bool))
        scores = jnp.where(causal[None, None], scores, -jnp.inf)
        attn = jax.nn.softmax(scores, axis=-1)
        out = jnp.einsum('bhqk,bhkd->bhqd', attn, v)
        out = out.transpose(0, 2, 1, 3).reshape(bs, seq_len, hidden)
        return out @ w_proj + b_proj

    def _L0_attn_b_ref(hidden_states, x_r, x_w, x_k, x_v, x_a, x_g, k_k, k_a, r_k, W_r, W_k, W_v, W_o, w_lora_a, w_lora_b, w_lora_bias, a_lora_a, a_lora_b, a_lora_bias, g_lora_a, g_lora_b, g_lora_bias, gn_weight, gn_bias):
        import jax, jax.numpy as jnp
        import numpy as np
        B, T, C, H = (2, 512, 256, 16)
        D = C // H
        RW, RA, RG = (64, 64, 128)
        EPS = 1e-05

        def _rwkv7_scan(r, log_w, k, v, a, b):
            Bn, Tn, Hn, Dn = r.shape

            def step(S, xs):
                r_t, w_t, k_t, v_t, a_t, b_t = xs
                sa = jnp.einsum('bhij,bhj->bhi', S, a_t)
                S = S * jnp.exp(w_t)[:, :, None, :] + sa[..., None] * b_t[:, :, None, :] + v_t[..., None] * k_t[:, :, None, :]
                o_t = jnp.einsum('bhij,bhj->bhi', S, r_t)
                return (S, o_t)
            S0 = jnp.zeros((Bn, Hn, Dn, Dn), r.dtype)
            xs = tuple((jnp.swapaxes(x, 0, 1) for x in (r, log_w, k, v, a, b)))
            _, o = jax.lax.scan(step, S0, xs)
            return jnp.swapaxes(o, 0, 1)
        Bn, Tn, Cn = hidden_states.shape
        shifted = jnp.concatenate([jnp.zeros_like(hidden_states[:, :1]), hidden_states[:, :-1]], axis=1)
        delta = shifted - hidden_states
        xr = hidden_states + delta * x_r
        xw = hidden_states + delta * x_w
        xk = hidden_states + delta * x_k
        xv = hidden_states + delta * x_v
        xa = hidden_states + delta * x_a
        r = xr @ W_r
        log_w = -jax.nn.softplus(-(jnp.tanh(xw @ w_lora_a) @ w_lora_b + w_lora_bias)) - 0.5
        k = xk @ W_k
        v = xv @ W_v
        a = jax.nn.sigmoid(xa @ a_lora_a @ a_lora_b + a_lora_bias)
        g = jax.nn.sigmoid(r @ g_lora_a) @ g_lora_b + g_lora_bias
        kk = (k * k_k).reshape(Bn, Tn, H, D)
        kk = kk / jnp.maximum(jnp.linalg.norm(kk, axis=-1, keepdims=True), 1e-12)
        k = k * (1.0 + (a - 1.0) * k_a)
        rh = r.reshape(Bn, Tn, H, D)
        wh = log_w.reshape(Bn, Tn, H, D)
        kh = k.reshape(Bn, Tn, H, D)
        vh = v.reshape(Bn, Tn, H, D)
        ah = a.reshape(Bn, Tn, H, D)
        o = _rwkv7_scan(rh, wh, kh, vh, -kk, kk * ah)
        mu = o.mean(-1, keepdims=True)
        var = ((o - mu) ** 2).mean(-1, keepdims=True)
        o_flat = ((o - mu) * jax.lax.rsqrt(var + EPS)).reshape(Bn, Tn, C) * gn_weight + gn_bias
        bonus = ((rh * kh * r_k).sum(-1, keepdims=True) * vh).reshape(Bn, Tn, C)
        o_flat = o_flat + bonus
        return o_flat * g @ W_o

    def _L0_ffn_ref(inputs, gate_weight, ln_gamma, ln_beta, wi, wo, conf_w1, conf_b1, conf_w2, conf_b2, comp_w, comp_b):
        import jax, jax.numpy as jnp
        import numpy as np
        B, L, H, E, I = (4, 512, 256, 8, 1024)
        S = B * L
        CAP_FACTOR_EVAL = 2.0
        MIN_CAP = 4
        _cap = int(np.floor(CAP_FACTOR_EVAL * S / E))
        _cap += _cap % 2
        CAPACITY = max(_cap, MIN_CAP)

        def _layer_norm(x, g, b, eps=1e-05):
            mu = x.mean(-1, keepdims=True)
            var = ((x - mu) ** 2).mean(-1, keepdims=True)
            return (x - mu) * jax.lax.rsqrt(var + eps) * g + b
        tokens = inputs.reshape(-1, H)
        residual = tokens
        tokens = _layer_norm(tokens, ln_gamma, ln_beta)
        complexity_score = jax.nn.sigmoid(tokens @ comp_w.T + comp_b).mean()
        hdn = jax.nn.relu(tokens @ conf_w1.T + conf_b1)
        confidence_score = jax.nn.sigmoid(hdn @ conf_w2.T + conf_b2).mean()
        logits = tokens.astype(jnp.float32) @ gate_weight.astype(jnp.float32).T
        probs = jax.nn.softmax(logits, axis=-1)
        top1 = jnp.argmax(logits, axis=-1)
        onehot = jax.nn.one_hot(top1, E, dtype=jnp.int32)
        rank_e = jnp.cumsum(onehot, axis=0) - onehot
        rank = jnp.sum(rank_e * onehot, axis=-1)
        keep = rank < CAPACITY
        weight = jnp.take_along_axis(probs, top1[:, None], axis=-1)[:, 0]
        weight = (weight * keep).astype(tokens.dtype)
        slot = jnp.where(keep, rank, 0)
        dispatch = jnp.zeros((E, CAPACITY, H), tokens.dtype)
        dispatch = dispatch.at[top1, slot].add(tokens * keep[:, None])
        h = jax.nn.gelu(jnp.einsum('ech,ehi->eci', dispatch, wi), approximate=False)
        expert_out = jnp.einsum('eci,eih->ech', h, wo)
        combined = weight[:, None] * expert_out[top1, slot]
        out = (residual + combined).reshape(inputs.shape)
        return out
    x = L0_attn_a_x
    x = x + _L0_attn_a_ref(_layernorm(x, axis=-1), L0_attn_a_w_attn, L0_attn_a_b_attn, L0_attn_a_w_proj, L0_attn_a_b_proj)
    x = x + _L0_ffn_ref(_layernorm(x, axis=-1), L0_ffn_gate_weight, L0_ffn_ln_gamma, L0_ffn_ln_beta, L0_ffn_wi, L0_ffn_wo, L0_ffn_conf_w1, L0_ffn_conf_b1, L0_ffn_conf_w2, L0_ffn_conf_b2, L0_ffn_comp_w, L0_ffn_comp_b)
    x = x + _L0_attn_b_ref(_layernorm(x, axis=-1), L0_attn_b_x_r, L0_attn_b_x_w, L0_attn_b_x_k, L0_attn_b_x_v, L0_attn_b_x_a, L0_attn_b_x_g, L0_attn_b_k_k, L0_attn_b_k_a, L0_attn_b_r_k, L0_attn_b_W_r, L0_attn_b_W_k, L0_attn_b_W_v, L0_attn_b_W_o, L0_attn_b_w_lora_a, L0_attn_b_w_lora_b, L0_attn_b_w_lora_bias, L0_attn_b_a_lora_a, L0_attn_b_a_lora_b, L0_attn_b_a_lora_bias, L0_attn_b_g_lora_a, L0_attn_b_g_lora_b, L0_attn_b_g_lora_bias, L0_attn_b_gn_weight, L0_attn_b_gn_bias)
    x = x + _L0_ffn_ref(_layernorm(x, axis=-1), L0_ffn_gate_weight, L0_ffn_ln_gamma, L0_ffn_ln_beta, L0_ffn_wi, L0_ffn_wo, L0_ffn_conf_w1, L0_ffn_conf_b1, L0_ffn_conf_w2, L0_ffn_conf_b2, L0_ffn_comp_w, L0_ffn_comp_b)
    return x

_drawn_inputs = setup_inputs


def setup_inputs(seed=0):
    import zlib

    import numpy as np

    out = dict(_drawn_inputs(seed))
    spreads = {'L0_attn_a_b_attn': (0.0, 0.1),
     'L0_attn_a_b_proj': (0.0, 0.1),
     'L0_attn_b_a_lora_bias': (0.0, 0.8),
     'L0_attn_b_g_lora_bias': (0.0, 0.48),
     'L0_attn_b_gn_weight': (1.0, 0.6),
     'L0_attn_b_gn_bias': (0.0, 0.8),
     'L0_ffn_ln_gamma': (1.0, 0.2),
     'L0_ffn_ln_beta': (0.0, 0.1),
     'L0_ffn_conf_b1': (-1.0, 0.2)}
    factors = {'L0_attn_b_x_r': 3.625,
     'L0_attn_b_x_w': 8.0,
     'L0_attn_b_x_k': 3.83,
     'L0_attn_b_x_v': 4.246,
     'L0_attn_b_x_a': 8.0,
     'L0_attn_b_k_k': 8.0,
     'L0_attn_b_k_a': 7.696,
     'L0_attn_b_r_k': 8.0,
     'L0_attn_b_w_lora_a': 8.0,
     'L0_attn_b_w_lora_b': 8.0,
     'L0_attn_b_w_lora_bias': 8.0,
     'L0_attn_b_a_lora_a': 8.0,
     'L0_attn_b_a_lora_b': 8.0,
     'L0_attn_b_g_lora_a': 8.0,
     'L0_attn_b_g_lora_b': 2.883}
    for name, (base, spread) in spreads.items():
        noise = np.random.default_rng([zlib.crc32(name.encode()), seed]).standard_normal(out[name].shape)
        drawn = base * np.exp(spread * noise) if base else spread * noise
        out[name] = jnp.asarray(drawn.astype(out[name].dtype))
    for name, factor in factors.items():
        out[name] = (out[name] * factor).astype(out[name].dtype)
    return out
```

```python
from contextlib import ExitStack, contextmanager

import numpy as np

import concourse.bass as bass
from concourse import mybir

F32 = mybir.dt.float32
BF16 = mybir.dt.bfloat16
I32 = mybir.dt.int32
U32 = mybir.dt.uint32
ALU = mybir.AluOpType
ACT = mybir.ActivationFunctionType
AX = mybir.AxisListType

P = 128
BATCH, T, C = 8, 1024, 256
TILES = T // P
NT = BATCH * TILES
KC = C // P
HEADS, D = 16, 16
GROUP = 4
PAD = 32
BANK = 512
SLOTS = 3
LN_EPS = 1e-5
MASKED = -1e30


class Tally:

    def __init__(self, eng, sem, base=0):
        self.eng, self.sem, self.base, self.n = eng, sem, base, 0

    def up(self, ins):
        self.n += 1
        return ins.then_inc(self.sem, 1)

    def done(self):
        self.eng.wait_ge(self.sem, self.base + self.n)

    def link(self, ins):
        self.up(ins)
        self.done()


def spread(row, parts=P):
    return bass.AP(tensor=row.tensor, offset=row.offset, ap=[[0, parts], *row.ap])


@contextmanager
def semaphores(nc, prefix):
    made = []

    def sem(name):
        made.append(nc.alloc_semaphore(name=prefix + name))
        return made[-1]

    yield sem
    nc.clear_and_free_semaphores(made)
    nc.all_engine_barrier()


def causal_rows(q_tile):
    return (q_tile + 1) * P


def attention_plan():
    plan = [("turn_x", c) for c in range(KC)]
    plan += [("project_qk", oc) for oc in range(2 * KC)]
    plan += [("project_v", half) for half in range(2)]

    def maxima(g):
        return [("maxima", (h, qt)) for qt in range(TILES) for h in range(GROUP * g, GROUP * g + GROUP)]

    def weights(g):
        return [("weights", (h, kt)) for kt in range(TILES) for h in range(GROUP * g, GROUP * g + GROUP)]

    plan += maxima(0) + [("turn_max", 0)]
    for g in range(HEADS // GROUP):
        ahead = maxima(g + 1) if g + 1 < HEADS // GROUP else []
        for n, job in enumerate(weights(g)):
            plan.append(job)
            if ahead:
                plan.append(ahead[n])
        if ahead:
            plan.append(("turn_max", g + 1))
        plan.append(("turn_out", g))
    plan += [("turn_o", c) for c in range(KC)]
    plan += [("project_o", half) for half in range(2)]
    return plan


SLOT_USER = {"turn_x": "act", "project_qk": "act", "project_v": "dve", "maxima": "dve", "turn_max": "act",
             "weights": "act", "turn_out": "dve", "turn_o": "act", "project_o": "dve"}


def with_slots(plan, slots=SLOTS):
    uses, out, place = [0] * slots, [], {}
    for n, (stage, what) in enumerate(plan):
        s = n % slots
        out.append((stage, what, s, uses[s]))
        place[stage, what] = (s, uses[s])
        uses[s] += 1
    return out, uses, place


def attention(nc, x_in, w_attn, b_attn, w_proj, b_proj, x_out):
    plan, slot_uses, place = with_slots(attention_plan())
    groups = HEADS // GROUP
    with ExitStack() as ctx:
        def sb(name, shape, dt=F32):
            return ctx.enter_context(nc.sbuf_tensor("at_" + name, shape, dt))

        sem = ctx.enter_context(semaphores(nc, "at_"))

        slot = [ctx.enter_context(nc.psum_tensor(f"at_slot{s}", [P, 2 * BANK], F32)) for s in range(SLOTS)]
        values = ctx.enter_context(nc.psum_tensor("at_values", [P, T], F32))

        w_qkv = sb("w_qkv", [P, KC, 3 * C])
        w_o = sb("w_o", [P, KC, C])
        bias_qk = sb("bias_qk", [P, 2 * KC])
        bias_v = sb("bias_v", [P, C])
        bias_o = sb("bias_o", [P, C])
        ident = sb("ident", [P, P])
        ident_bf = sb("ident_bf", [P, P], BF16)
        mask_q = sb("mask_q", [P, P], BF16)
        mask_k = sb("mask_k", [P, P], BF16)
        x = sb("x", [P, TILES, C])
        xn = sb("xn", [P, TILES, C])
        stats = sb("stats", [P, TILES, 6])
        mean_var = sb("mean_var", [P, TILES, 2])
        std = sb("std", [P, TILES])
        rstd = sb("rstd", [P, TILES])
        turned = sb("turned", [P, KC, T])
        qk = sb("qk", [P, 2, T])
        part = [sb(f"part{k}", [P, 2 * KC, T], BF16) for k in range(3)]
        rest = sb("rest", [P, 2, T])
        q_stack = sb("q_stack", [P, HEADS, T], BF16)
        k_stack = sb("k_stack", [P, HEADS, T], BF16)
        v_rows = sb("v_rows", [P, TILES, HEADS, PAD])
        neg_max = sb("neg_max", [P, TILES, HEADS])
        max_rest = sb("max_rest", [P, TILES, GROUP])
        max_part = sb("max_part", [P, TILES, 3, GROUP], BF16)
        max_rows = sb("max_rows", [3 * GROUP, T], BF16)
        NPROB = 2 * GROUP
        prob = sb("prob", [P, NPROB, T])
        out_t = sb("out_t", [P, T])
        inv_sum = sb("inv_sum", [P, TILES, GROUP])

        consts = sem("consts")
        w_in = sem("w_in")
        x_loaded = sem("x_loaded")
        var_ready = sem("var_ready")
        std_ready = sem("std_ready")
        xn_ready = sem("xn_ready")
        dve_chain = sem("dve_chain")
        act_chain = sem("act_chain")
        filled = [sem(f"filled{s}") for s in range(SLOTS)]
        emptied = [sem(f"emptied{s}") for s in range(SLOTS)]
        qk_ready = sem("qk_ready")
        rest_ready = sem("rest_ready")
        part2_ready = sem("part2_ready")
        part3_ready = sem("part3_ready")
        stacked = sem("stacked")
        max_ready = sem("max_ready")
        max_stacked = sem("max_stacked")
        prob_used = sem("prob_used")
        out_t_ready = sem("out_t_ready")
        stored = sem("stored")

        ctx.enter_context(nc.allow_non_contiguous_dma(reason="bias columns"))
        block = ctx.enter_context(nc.Block())
        STACK_DMAS = 2 * KC * 8 * 6

        def read_out(eng, b, *uses):
            latest = {}
            for stage, what in uses:
                s, use = place[stage, what]
                latest[s] = max(latest.get(s, 0), use + 1)
            for s, use in latest.items():
                eng.wait_ge(emptied[s], b * slot_uses[s] + use)

        @block.gpsimd
        def _(pool):
            own = Tally(pool, consts)
            own.up(pool.memset(ident[:], 0.0))
            own.up(pool.memset(mask_q[:], 0.0))
            own.up(pool.memset(mask_k[:], 0.0))
            own.up(pool.memset(v_rows[:], 0.0))
            own.up(pool.memset(k_stack[:], 1.0))
            own.done()
            own.up(pool.affine_select(out=ident[:], in_=ident[:], compare_op=ALU.not_equal, fill=1.0, base=0,
                                      pattern=[[-1, P]], channel_multiplier=1))
            own.up(pool.affine_select(out=mask_q[:], in_=mask_q[:], compare_op=ALU.is_ge, fill=MASKED, base=0,
                                      pattern=[[-1, P]], channel_multiplier=1))
            own.up(pool.affine_select(out=mask_k[:], in_=mask_k[:], compare_op=ALU.is_ge, fill=MASKED, base=0,
                                      pattern=[[1, P]], channel_multiplier=-1))
            own.up(pool.memset(v_rows[:, :, :, D], 1.0))
            own.done()
            own.up(pool.tensor_copy(ident_bf[:], ident[:]))
            assert own.n == 10
            with pool.Fori(0, BATCH) as b:
                for oc in range(2 * KC):
                    pool.wait_ge(rest_ready, b * 2 * KC + oc + 1)
                    pool.nop(nofuse=True)
                    pool.tensor_copy(part[1][:, oc, :], rest[:, oc % 2, :]).then_inc(part2_ready, 1)

        @block.sync
        def _(sp):
            sp.dma_start(w_qkv[:], w_attn.rearrange("(k p) n -> p k n", p=P)).then_inc(w_in, 16)
            sp.dma_start(w_o[:], w_proj.rearrange("(k p) n -> p k n", p=P)).then_inc(w_in, 16)
            sp.dma_start(bias_qk[:], b_attn[0:2 * C].rearrange("(k p) -> p k", p=P)).then_inc(w_in, 16)
            sp.dma_start(bias_v[:], spread(b_attn[2 * C:3 * C])).then_inc(w_in, 16)
            sp.dma_start(bias_o[:], spread(b_proj)).then_inc(w_in, 16)
            sp.wait_ge(consts, 5)
            with sp.Fori(0, BATCH) as b:
                sp.wait_ge(stored, b * 32)
                sp.dma_start(x[:], x_in[bass.ds(b * TILES, TILES)].rearrange("n p c -> p n c")).then_inc(x_loaded, 16)
                for oc in range(2 * KC):
                    sp.wait_ge(part3_ready, b * 2 * KC + oc + 1)
                    is_k = oc // KC
                    order = (0, 1, 2, 0, 1, 0) if is_k else (0, 0, 0, 1, 1, 2)
                    stack = k_stack if is_k else q_stack
                    for h8 in range(8):
                        for blk, k in enumerate(order):
                            sp.dma_start(stack[blk * D:(blk + 1) * D, (oc % KC) * 8 + h8, :],
                                         part[k][h8 * D:(h8 + 1) * D, oc, :]).then_inc(stacked, 16)
                for g in range(groups):
                    read_out(sp, b, ("turn_max", g))
                    for k in range(3):
                        sp.dma_start(q_stack[96 + k:97 + k, GROUP * g:GROUP * g + GROUP, :],
                                     max_rows[GROUP * k:GROUP * k + GROUP, :]).then_inc(max_stacked, 16)
                for half in range(2):
                    read_out(sp, b, ("project_o", half))
                    n = TILES // 2
                    sp.dma_start(x_out[bass.ds(b * TILES + half * n, n)].rearrange("n p c -> p n c"),
                                 xn[:, half * n:half * n + n, :]).then_inc(stored, 16)
            sp.wait_ge(stored, 16 * 2 * BATCH)

        @block.tensor
        def _(pe):
            pe.wait_ge(consts, 10)
            pe.wait_ge(w_in, 16 * 5)
            with pe.Fori(0, BATCH) as b:
                def value_product(g, kt):
                    read_out(pe, b, *[("weights", (GROUP * g + j, kt)) for j in range(GROUP)])
                    if kt == 0:
                        pe.wait_ge(out_t_ready, b * groups + g)
                    for q0 in range(0, T, BANK):
                        q1 = q0 + BANK
                        if q1 <= kt * P:
                            continue
                        lo = max(q0, kt * P)
                        for j in range(GROUP):
                            n = (g * TILES + kt) * GROUP + j
                            last = pe.matmul(values[PAD * j:PAD * j + PAD, lo:q1],
                                             v_rows[:, kt, GROUP * g + j, :], prob[:, n % NPROB, lo:q1],
                                             start=(kt == 0), stop=(q1 == (kt + 1) * P), tile_position=(0, PAD * j))
                    last.then_inc(prob_used, 1)

                for n_job, (stage, what, s, use) in enumerate(plan):
                    if stage == "turn_out":
                        value_product(what, TILES - 1)
                    ps = slot[s]
                    pe.wait_ge(emptied[s], b * slot_uses[s] + use)
                    if stage == "turn_x":
                        if what == 0:
                            pe.wait_ge(xn_ready, (b + 1) * TILES)
                        for t in range(TILES):
                            last = pe.transpose(ps[:, t * P:(t + 1) * P], xn[:, t, what * P:(what + 1) * P], ident[:])
                    elif stage == "project_qk":
                        if what == 0:
                            read_out(pe, b, ("turn_x", 0), ("turn_x", 1))
                        for half in range(2):
                            for k in range(KC):
                                last = pe.matmul(ps[:, half * BANK:(half + 1) * BANK],
                                                 w_qkv[:, k, what * P:(what + 1) * P],
                                                 turned[:, k, half * BANK:(half + 1) * BANK],
                                                 start=(k == 0), stop=(k == KC - 1))
                    elif stage == "project_v":
                        for n in range(4):
                            t = 4 * what + n
                            for k in range(KC):
                                last = pe.matmul(ps[:, n * C:(n + 1) * C], turned[:, k, t * P:(t + 1) * P],
                                                 w_qkv[:, k, 2 * C:3 * C], start=(k == 0), stop=(k == KC - 1))
                    elif stage == "maxima":
                        h, qt = what
                        if (h, qt) == (0, 0):
                            pe.wait_ge(stacked, (b + 1) * 16 * STACK_DMAS)
                            read_out(pe, b, ("project_v", 0), ("project_v", 1))
                        keys = causal_rows(qt)
                        for k0 in range(0, keys, BANK):
                            k1 = min(k0 + BANK, keys)
                            pe.matmul(ps[:, k0:k1], q_stack[0:96, h, qt * P:(qt + 1) * P], k_stack[0:96, h, k0:k1],
                                      start=True, stop=True)
                        last = pe.matmul(ps[:, keys - P:keys], ident_bf[:], mask_q[:], start=False, stop=True,
                                         skip_group_check=True)
                    elif stage == "turn_max":
                        pe.wait_ge(max_ready, b * groups + what + 1)
                        rows = ps[:].bitcast(BF16)
                        for t in range(TILES):
                            last = pe.transpose(rows[0:3 * GROUP, t * P:(t + 1) * P],
                                                max_part[:, t, :, :].rearrange("p k g -> p (k g)"), ident_bf[:])
                    elif stage == "weights":
                        h, kt = what
                        if (h % GROUP, kt) == (0, 0):
                            pe.wait_ge(max_stacked, (b * groups + h // GROUP + 1) * 48)
                        q_from = kt * P
                        for q0 in range(0, T, BANK):
                            if q0 + BANK <= q_from:
                                continue
                            lo = max(q0, q_from)
                            last = pe.matmul(ps[:, lo:q0 + BANK], k_stack[0:99, h, kt * P:(kt + 1) * P],
                                             q_stack[0:99, h, lo:q0 + BANK], start=True, stop=True)
                            if lo == q_from:
                                last = pe.matmul(ps[:, lo:lo + P], ident_bf[:], mask_k[:], start=False, stop=True,
                                                 skip_group_check=True)
                    elif stage == "turn_out":
                        pe.wait_ge(out_t_ready, b * groups + what + 1)
                        for t in range(TILES):
                            last = pe.transpose(ps[:, t * P:(t + 1) * P], out_t[:, t * P:(t + 1) * P], ident[:])
                    elif stage == "turn_o":
                        if what == 0:
                            read_out(pe, b, *[("turn_out", g) for g in range(groups)])
                        for t in range(TILES):
                            last = pe.transpose(ps[:, t * P:(t + 1) * P], xn[:, t, what * P:(what + 1) * P], ident[:])
                    elif stage == "project_o":
                        if what == 0:
                            read_out(pe, b, ("turn_o", 0), ("turn_o", 1))
                        for n in range(4):
                            t = 4 * what + n
                            for k in range(KC):
                                last = pe.matmul(ps[:, n * C:(n + 1) * C], turned[:, k, t * P:(t + 1) * P],
                                                 w_o[:, k, :], start=(k == 0), stop=(k == KC - 1))
                    last.then_inc(filled[s], 1)
                    if stage == "weights" and what[0] % GROUP == GROUP - 1 and what[1] >= 1:
                        value_product(what[0] // GROUP, what[1] - 1)

        @block.scalar
        def _(act):
            act.wait_ge(w_in, 16 * 5)
            act.wait_ge(consts, 10)
            act.activation(bias_qk[:, 0:KC], bias_qk[:, 0:KC], ACT.Copy, scale=D ** -0.5).then_inc(act_chain, 1)
            act.wait_ge(act_chain, 1)
            with act.Fori(0, BATCH) as b:
                act.wait_ge(var_ready, b + 1)
                act.activation(std[:], mean_var[:, :, 1], ACT.Sqrt).then_inc(std_ready, 1)
                for stage, what, s, use in plan:
                    ps = slot[s]
                    if stage == "turn_out":
                        act.wait_ge(prob_used, (b * groups + what + 1) * TILES)
                        if what:
                            read_out(act, b, ("turn_out", what - 1))
                        act.activation(out_t[:], values[:], ACT.Copy).then_inc(out_t_ready, 1)
                    if SLOT_USER[stage] != "act":
                        continue
                    act.wait_ge(filled[s], b * slot_uses[s] + use + 1)
                    if stage in ("turn_x", "turn_o"):
                        act.activation(turned[:, what, :], ps[:], ACT.Copy).then_inc(emptied[s], 1)
                    elif stage == "project_qk":
                        if what == 0:
                            act.wait_ge(stacked, b * 16 * STACK_DMAS)
                        if what >= 2:
                            act.wait_ge(part3_ready, b * 2 * KC + what - 1)
                        act.activation(qk[:, what % 2, :], ps[:], ACT.Identity, bias=bias_qk[:, what:what + 1],
                                       scale=D ** -0.5 if what < KC else 1.0)\
                           .then_inc(emptied[s], 1)
                        read_out(act, b, (stage, what))
                        act.activation(part[0][:, what, :], qk[:, what % 2, :], ACT.Copy).then_inc(qk_ready, 1)
                    elif stage == "turn_max":
                        act.wait_ge(max_stacked, (b * groups + what) * 48)
                        act.activation(max_rows[:], ps[:].bitcast(BF16)[0:3 * GROUP, 0:T], ACT.Copy)\
                           .then_inc(emptied[s], 1)
                    elif stage == "weights":
                        h, kt = what
                        n = ((h // GROUP) * TILES + kt) * GROUP + h % GROUP
                        if n % GROUP == 0:
                            if n >= NPROB:
                                act.wait_ge(prob_used, b * groups * TILES + n // GROUP - 1)
                            else:
                                act.wait_ge(prob_used, b * groups * TILES)
                        act.activation(prob[:, n % NPROB, kt * P:T], ps[:, kt * P:T], ACT.Exp).then_inc(emptied[s], 1)

        @block.vector
        def _(dve):
            dve.wait_ge(consts, 10)
            dve.wait_ge(w_in, 16 * 5)
            CHAIN = 2 * TILES + 2 + groups * 4
            with dve.Fori(0, BATCH) as b:
                own = Tally(dve, dve_chain, b * CHAIN)
                dve.wait_ge(x_loaded, (b + 1) * 16)
                dve.wait_ge(stored, b * 32)
                for t in range(TILES):
                    own.up(dve.bn_stats(stats[:, t, :], x[:, t, :]))
                own.done()
                dve.nop(nofuse=True)
                for t in range(TILES):
                    own.up(dve.bn_aggr(mean_var[:, t, :], stats[:, t, :]))
                own.done()
                dve.tensor_scalar(mean_var[:, :, 1], mean_var[:, :, 1], LN_EPS, None, ALU.add).then_inc(var_ready, 1)
                dve.wait_ge(std_ready, b + 1)
                own.link(dve.reciprocal(rstd[:], std[:]))
                for t in range(TILES):
                    dve.tensor_scalar(xn[:, t, :], x[:, t, :], mean_var[:, t, 0:1], rstd[:, t:t + 1],
                                      ALU.subtract, ALU.mult).then_inc(xn_ready, 1)
                dve.wait_ge(xn_ready, (b + 1) * TILES)
                own.up(dve.tensor_tensor(x[:], x[:], bias_o[:].unsqueeze(1).broadcast_to([P, TILES, C]), ALU.add))

                def split_rest(oc):
                    dve.wait_ge(qk_ready, b * 2 * KC + oc + 1)
                    dve.wait_ge(stacked, b * 16 * STACK_DMAS)
                    dve.tensor_tensor(rest[:, oc % 2, :], qk[:, oc % 2, :], part[0][:, oc, :], ALU.subtract)\
                       .then_inc(rest_ready, 1)

                def third(oc):
                    dve.wait_ge(part2_ready, b * 2 * KC + oc + 1)
                    dve.tensor_tensor(part[2][:, oc, :], rest[:, oc % 2, :], part[1][:, oc, :], ALU.subtract)\
                       .then_inc(part3_ready, 1)

                for oc in range(2 * KC):
                    split_rest(oc)
                    third(oc)
                for stage, what, s, use in plan:
                    if SLOT_USER[stage] != "dve":
                        if stage == "turn_max":
                            heads = slice(GROUP * what, GROUP * what + GROUP)
                            read_out(dve, b, *[("maxima", (h, TILES - 1)) for h in range(heads.start, heads.stop)],
                                     *[("turn_max", what - 1)][:what])
                            own.link(dve.tensor_copy(max_part[:, :, 0, :], neg_max[:, :, heads]))
                            own.link(dve.tensor_tensor(max_rest[:], neg_max[:, :, heads], max_part[:, :, 0, :],
                                                       ALU.subtract))
                            own.link(dve.tensor_copy(max_part[:, :, 1, :], max_rest[:]))
                            dve.tensor_tensor(max_part[:, :, 2, :], max_rest[:], max_part[:, :, 1, :],
                                              ALU.subtract).then_inc(max_ready, 1)
                        continue
                    ps = slot[s]
                    dve.wait_ge(filled[s], b * slot_uses[s] + use + 1)
                    if stage == "project_v":
                        for n in range(4):
                            ins = dve.tensor_tensor(
                                v_rows[:, 4 * what + n, :, 0:D],
                                ps[:, n * C:(n + 1) * C].rearrange("p (h d) -> p h d", d=D),
                                bias_v[:].rearrange("p (h d) -> p h d", d=D), ALU.add)
                        ins.then_inc(emptied[s], 1)
                    elif stage == "maxima":
                        h, qt = what
                        keys = causal_rows(qt)
                        dve.tensor_reduce(neg_max[:, qt, h:h + 1], ps[:, 0:keys], AX.X, ALU.max, negate=True)\
                           .then_inc(emptied[s], 1)
                    elif stage == "turn_out":
                        rows = ps[:].rearrange("p (t h d) -> p t h d", t=TILES, d=PAD)
                        own.link(dve.reciprocal(inv_sum[:], rows[:, :, :, D]))
                        dve.tensor_tensor(
                            xn[:].rearrange("p t (h d) -> p t h d", d=D)[:, :, GROUP * what:GROUP * what + GROUP, :],
                            rows[:, :, :, 0:D], inv_sum[:].unsqueeze(3).broadcast_to([P, TILES, GROUP, D]),
                            ALU.mult).then_inc(emptied[s], 1)
                    elif stage == "project_o":
                        own.done()
                        dve.tensor_tensor(xn[:, 4 * what:4 * what + 4, :], ps[:].rearrange("p (n c) -> p n c", c=C),
                                          x[:, 4 * what:4 * what + 4, :], ALU.add).then_inc(emptied[s], 1)
                assert own.n == CHAIN, (own.n, CHAIN)


EXPERTS, HIDDEN, CAPACITY = 8, 1024, 512
KEPT = EXPERTS * CAPACITY
HC = HIDDEN // P
ST = CAPACITY // P


def mixture(nc, n, x_in, gate_w, gamma, beta, w_in, w_out, slots_dram, results_dram, x_out, clear_slots):
    with ExitStack() as outer:
        def sb(name, shape, dt=F32, ctx=outer):
            return ctx.enter_context(nc.sbuf_tensor(f"f{n}_{name}", shape, dt))

        def psum(ctx, name, shape, dt=F32):
            return ctx.enter_context(nc.psum_tensor(f"f{n}_{name}", shape, dt))

        sem = outer.enter_context(semaphores(nc, f"f{n}_"))

        outer.enter_context(nc.allow_non_contiguous_dma(reason="gate weights by channel"))
        base = sb("base", [P, NT, C])
        weight = sb("weight", [P, NT])
        fetch_at = sb("fetch_at", [P, NT], I32)
        send_to = sb("send_to", [P, NT], I32)
        ident = sb("ident", [P, P])
        consts = sem("consts")

        with ExitStack() as ctx:
            tokens = sb("tokens", [P, NT, C], ctx=ctx)
            u = sb("u", [P, TILES, C], ctx=ctx)
            tok = sb("tok", [P, TILES, C], ctx=ctx)
            turned = sb("turned", [P, KC, T], ctx=ctx)
            gate = sb("gate", [P, KC, EXPERTS], ctx=ctx)
            gamma_b = sb("gamma_b", [P, C], ctx=ctx)
            beta_b = sb("beta_b", [P, C], ctx=ctx)
            stats = sb("stats", [P, TILES, 6], ctx=ctx)
            mean_var = sb("mean_var", [P, 2, TILES, 2], ctx=ctx)
            std = sb("std", [P, 2, TILES], ctx=ctx)
            rstd = sb("rstd", [P, 2, TILES], ctx=ctx)
            logits = sb("logits", [P, NT, EXPERTS], ctx=ctx)
            before = sb("before", [P, P], ctx=ctx)
            ones = sb("ones", [P, P], ctx=ctx)
            order = sb("order", [P, EXPERTS], ctx=ctx)
            onehot = sb("onehot", [P, NT, EXPERTS], ctx=ctx)
            work = sb("work", [P, NT, EXPERTS], ctx=ctx)
            tops = sb("tops", [P, NT], ctx=ctx)
            first = sb("first", [P, NT], ctx=ctx)
            total = sb("total", [P, NT], ctx=ctx)
            rank = sb("rank", [P, NT], ctx=ctx)
            keep = sb("keep", [P, NT], ctx=ctx)
            place = sb("place", [P, NT], ctx=ctx)
            totals = sb("totals", [P, NT, EXPERTS], ctx=ctx)
            earlier = sb("earlier", [P, NT, EXPERTS], ctx=ctx)
            zeros = sb("zeros", [P, 1024], ctx=ctx)
            ps_turn = [psum(ctx, f"turn{k}", [P, T]) for k in range(KC)]
            ps_gate = psum(ctx, "ps_gate", [P, TILES * EXPERTS])
            ps_before = psum(ctx, "ps_before", [P, NT * EXPERTS])
            ps_total = psum(ctx, "ps_total", [P, NT * EXPERTS])

            x_loaded = sem("x_loaded")
            loaded = sem("loaded")
            cleared = sem("cleared")
            chain = sem("chain")
            var_ready = sem("var_ready")
            std_ready = sem("std_ready")
            scaled = sem("scaled")
            tok_ready = sem("tok_ready")
            base_ready = sem("base_ready")
            turn_ready = sem("turn_ready")
            turned_ready = sem("turned_ready")
            kept = sem("kept")
            gate_ready = sem("gate_ready")
            logits_ready = sem("logits_ready")
            shifted = sem("shifted")
            exp_ready = sem("exp_ready")
            onehot_ready = sem("onehot_ready")
            counts_ready = sem("counts_ready")
            routed = sem("routed")
            sent = sem("sent")

            block = ctx.enter_context(nc.Block())

            @block.sync
            def _(sp):
                for k in range(KC):
                    sp.dma_start(gate[:, k, :], gate_w[:, k * P:(k + 1) * P].rearrange("e p -> p e")).then_inc(loaded, 16)
                sp.dma_start(gamma_b[:], spread(gamma)).then_inc(loaded, 16)
                sp.dma_start(beta_b[:], spread(beta)).then_inc(loaded, 16)
                with sp.Fori(0, BATCH) as b:
                    sp.wait_ge(x_loaded, b * 16)
                    sp.dma_start(base[:, bass.ds(b * TILES, TILES), :],
                                 x_in[bass.ds(b * TILES, TILES)].rearrange("n p c -> p n c")).then_inc(x_loaded, 16)
                if clear_slots:
                    sp.wait_ge(consts, 1)
                    zero_rows = KEPT // 8
                    for k in range(8):
                        sp.dma_start(slots_dram[k * zero_rows:(k + 1) * zero_rows, :]
                                     .rearrange("(p r) c -> p (r c)", p=P), zeros[:]).then_inc(cleared, 16)

            @block.gpsimd
            def _(pool):
                own = Tally(pool, consts)
                own.up(pool.memset(zeros[:], 0.0))
                own.up(pool.memset(ident[:], 0.0))
                own.up(pool.memset(before[:], 1.0))
                own.up(pool.memset(ones[:], 1.0))
                own.up(pool.iota(fetch_at[:, 0:EXPERTS], pattern=[[-1, EXPERTS]], base=EXPERTS, channel_multiplier=0))
                own.done()
                own.up(pool.affine_select(out=ident[:], in_=ident[:], compare_op=ALU.not_equal, fill=1.0, base=0,
                                          pattern=[[-1, P]], channel_multiplier=1))
                own.up(pool.affine_select(out=before[:], in_=before[:], compare_op=ALU.is_gt, fill=0.0, base=0,
                                          pattern=[[1, P]], channel_multiplier=-1))
                own.up(pool.tensor_copy(order[:], fetch_at[:, 0:EXPERTS]))
                own.done()
                assert own.n == 8
                pool.wait_ge(loaded, 64)
                beta_wide = beta_b[:].unsqueeze(1).broadcast_to([P, TILES, C])
                with pool.Fori(0, BATCH) as b:
                    pool.wait_ge(scaled, b + 1)
                    pool.wait_ge(kept, b)
                    pool.tensor_tensor(tok[:], tok[:], beta_wide, ALU.add).then_inc(tok_ready, 1)
                    span = base[:, bass.ds(b * TILES, TILES), :]
                    pool.tensor_tensor(span, span, u[:], ALU.add).then_inc(base_ready, 1)
                pool.wait_ge(routed, 1)
                pool.wait_ge(kept, BATCH)
                if clear_slots:
                    pool.wait_ge(cleared, 8 * 16)
                for t in range(NT):
                    pool.indirect_dma_start(
                        out=slots_dram, out_offset=bass.IndirectOffsetOnAxis(ap=send_to[:, t:t + 1].bitcast(U32), axis=0),
                        in_=tokens[:, t, :], in_offset=None, bounds_check=KEPT - 1, oob_is_err=False)\
                        .then_inc(sent, 16)
                pool.wait_ge(sent, 16 * NT)

            @block.tensor
            def _(pe):
                pe.wait_ge(consts, 8)
                pe.wait_ge(loaded, 64)
                with pe.Fori(0, BATCH) as b:
                    pe.wait_ge(tok_ready, b + 1)
                    pe.wait_ge(turned_ready, b * KC)
                    for k in range(KC):
                        for t in range(TILES):
                            last = pe.transpose(ps_turn[k][:, t * P:(t + 1) * P], tok[:, t, k * P:(k + 1) * P],
                                                ident[:])
                        last.then_inc(turn_ready, 1)
                    pe.wait_ge(turned_ready, b * KC + KC)
                    pe.wait_ge(logits_ready, b)
                    for t in range(TILES):
                        for k in range(KC):
                            last = pe.matmul(ps_gate[:, t * EXPERTS:(t + 1) * EXPERTS],
                                             turned[:, k, t * P:(t + 1) * P], gate[:, k, :],
                                             start=(k == 0), stop=(k == KC - 1))
                    last.then_inc(gate_ready, 1)
                pe.wait_ge(onehot_ready, 1)
                chosen = onehot[:].rearrange("p t e -> p (t e)")
                pe.matmul(ps_before[:], before[:], chosen, start=True, stop=True)
                pe.matmul(ps_total[:], ones[:], chosen, start=True, stop=True).then_inc(counts_ready, 1)

            @block.scalar
            def _(act):
                with act.Fori(0, BATCH) as b:
                    for k in range(2):
                        act.wait_ge(var_ready, b * 2 + k + 1)
                        act.activation(std[:, k, :], mean_var[:, k, :, 1], ACT.Sqrt).then_inc(std_ready, 1)
                    act.wait_ge(gate_ready, b)
                    for k in range(KC):
                        act.wait_ge(turn_ready, b * KC + k + 1)
                        act.activation(turned[:, k, :], ps_turn[k][:], ACT.Copy).then_inc(turned_ready, 1)
                    act.activation(tokens[:, bass.ds(b * TILES, TILES), :], tok[:], ACT.Copy).then_inc(kept, 1)
                act.wait_ge(shifted, 1)
                act.activation(work[:], work[:], ACT.Exp).then_inc(exp_ready, 1)

            @block.vector
            def _(dve):
                dve.wait_ge(consts, 8)
                dve.wait_ge(loaded, 64)
                gamma_wide = gamma_b[:].unsqueeze(1).broadcast_to([P, TILES, C])
                TURN = 2 * (2 * TILES + 1) + 2 * TILES
                with dve.Fori(0, BATCH) as b:
                    own = Tally(dve, chain, b * TURN)
                    dve.wait_ge(x_loaded, (b + 1) * 16)
                    for k in range(2):
                        for t in range(TILES):
                            src = u[:, t, :] if k else base[:, bass.ds(b * TILES + t, 1), :].rearrange("p a c -> p (a c)")
                            own.up(dve.bn_stats(stats[:, t, :], src))
                        own.done()
                        dve.nop(nofuse=True)
                        for t in range(TILES):
                            own.up(dve.bn_aggr(mean_var[:, k, t, :], stats[:, t, :]))
                        own.done()
                        dve.tensor_scalar(mean_var[:, k, :, 1], mean_var[:, k, :, 1], LN_EPS, None, ALU.add)\
                           .then_inc(var_ready, 1)
                        dve.wait_ge(std_ready, b * 2 + k + 1)
                        own.link(dve.reciprocal(rstd[:, k, :], std[:, k, :]))
                        if k == 0:
                            dve.wait_ge(base_ready, b)
                        else:
                            dve.wait_ge(kept, b)
                            dve.wait_ge(turn_ready, b * KC)
                        for t in range(TILES):
                            src = u[:, t, :] if k else base[:, bass.ds(b * TILES + t, 1), :].rearrange("p a c -> p (a c)")
                            dst = tok[:, t, :] if k else u[:, t, :]
                            own.up(dve.tensor_scalar(dst, src, mean_var[:, k, t, 0:1], rstd[:, k, t:t + 1],
                                                     ALU.subtract, ALU.mult))
                        own.done()
                    dve.tensor_tensor(tok[:], tok[:], gamma_wide, ALU.mult).then_inc(scaled, 1)
                    dve.wait_ge(gate_ready, b + 1)
                    dve.tensor_copy(logits[:, bass.ds(b * TILES, TILES), :],
                                    ps_gate[:].rearrange("p (t e) -> p t e", e=EXPERTS)).then_inc(logits_ready, 1)
                    assert own.n == TURN, own.n
                own = Tally(dve, chain, BATCH * TURN)
                wide = [P, NT, EXPERTS]
                dve.wait_ge(logits_ready, BATCH)
                own.link(dve.tensor_reduce(tops[:], logits[:], AX.X, ALU.max))
                tops_wide = tops[:].unsqueeze(2).broadcast_to(wide)
                dve.tensor_tensor(work[:], logits[:], tops_wide, ALU.subtract).then_inc(shifted, 1)
                own.link(dve.tensor_tensor(onehot[:], logits[:], tops_wide, ALU.is_equal))
                own.link(dve.tensor_tensor(onehot[:], onehot[:], order[:].unsqueeze(1).broadcast_to(wide), ALU.mult))
                own.link(dve.tensor_reduce(first[:], onehot[:], AX.X, ALU.max))
                dve.tensor_tensor(onehot[:], onehot[:], first[:].unsqueeze(2).broadcast_to(wide), ALU.is_equal)\
                   .then_inc(onehot_ready, 1)
                dve.wait_ge(exp_ready, 1)
                own.link(dve.tensor_reduce(total[:], work[:], AX.X, ALU.add))
                own.link(dve.reciprocal(weight[:], total[:]))
                dve.wait_ge(counts_ready, 1)
                own.link(dve.tensor_copy(totals[:], ps_total[:].rearrange("p (t e) -> p t e", e=EXPERTS)))
                for e in range(EXPERTS):
                    own.up(dve.tensor_tensor_scan(earlier[:, :, e], ones[:, 0:NT], totals[:, :, e], 0.0,
                                                  ALU.mult, ALU.add))
                own.done()
                own.link(dve.tensor_tensor(earlier[:], earlier[:], totals[:], ALU.subtract))
                own.link(dve.tensor_tensor(earlier[:], earlier[:], ps_before[:].rearrange("p (t e) -> p t e", e=EXPERTS),
                                           ALU.add))
                dve.wait_ge(onehot_ready, 1)
                own.link(dve.tensor_tensor(earlier[:], earlier[:], onehot[:], ALU.mult))
                own.link(dve.tensor_reduce(rank[:], earlier[:], AX.X, ALU.add))
                own.link(dve.tensor_scalar(keep[:], rank[:], float(CAPACITY), None, ALU.is_lt))
                own.link(dve.tensor_scalar(place[:], first[:], -float(CAPACITY), float(EXPERTS * CAPACITY), ALU.mult, ALU.add))
                own.link(dve.tensor_tensor(place[:], place[:], rank[:], ALU.add))
                own.link(dve.tensor_tensor(place[:], place[:], keep[:], ALU.mult))
                own.link(dve.tensor_tensor(weight[:], weight[:], keep[:], ALU.mult))
                own.link(dve.tensor_copy(fetch_at[:], place[:]))
                own.link(dve.tensor_scalar(keep[:], keep[:], -float(KEPT), float(KEPT), ALU.mult, ALU.add))
                own.link(dve.tensor_tensor(place[:], place[:], keep[:], ALU.add))
                dve.tensor_copy(send_to[:], place[:]).then_inc(routed, 1)

        with ExitStack() as ctx:
            up_w = [sb(f"up_w{k}", [P, KC, HIDDEN], ctx=ctx) for k in range(2)]
            down_w = [sb(f"down_w{k}", [P, HC, C], ctx=ctx) for k in range(2)]
            rows = [sb(f"rows{k}", [P, ST, C], ctx=ctx) for k in range(2)]
            cols = [sb(f"cols{k}", [P, KC, CAPACITY], ctx=ctx) for k in range(2)]
            hidden = [sb(f"hidden{k}", [P, HC, CAPACITY], ctx=ctx) for k in range(2)]
            result = [sb(f"result{k}", [P, ST, C], ctx=ctx) for k in range(2)]
            ps_cols = psum(ctx, "ps_cols", [P, KC * CAPACITY])
            ps_hid = [psum(ctx, f"ps_hid{k}", [P, 2 * CAPACITY]) for k in range(2)]
            ps_res = psum(ctx, "ps_res", [P, ST * C])

            weights_in = [sem(f"weights_in{k}") for k in range(2)]
            rows_in = [sem(f"rows_in{k}") for k in range(2)]
            cols_turned = sem("cols_turned")
            cols_ready = sem("cols_ready")
            hid_made = sem("hid_made")
            hid_ready = sem("hid_ready")
            res_made = sem("res_made")
            res_ready = sem("res_ready")
            res_stored = sem("res_stored")

            block = ctx.enter_context(nc.Block())

            @block.sync
            def _(sp):
                with sp.Fori(0, EXPERTS // 2) as turn:
                    for k in range(2):
                        e = turn * 2 + k
                        sp.wait_ge(res_stored, turn * 32)
                        sp.dma_start(rows[k][:], slots_dram.rearrange("(e s p) c -> e p s c", s=ST, p=P)
                                     [bass.ds(e, 1)].rearrange("a p s c -> (a p) s c")).then_inc(rows_in[k], 16)
                        sp.dma_start(up_w[k][:], w_in[bass.ds(e, 1)].rearrange("a (k p) n -> (a p) k n", p=P))\
                          .then_inc(weights_in[k], 16)
                        sp.dma_start(down_w[k][:], w_out[bass.ds(e, 1)].rearrange("a (k p) n -> (a p) k n", p=P))\
                          .then_inc(weights_in[k], 16)

            @block.scalar
            def _(act):
                with act.Fori(0, EXPERTS // 2) as turn:
                    for k in range(2):
                        e = turn * 2 + k
                        for pair in range(HC // 2):
                            act.wait_ge(hid_made, e * (HC // 2) + pair + 1)
                            act.activation(hidden[k][:, 2 * pair:2 * pair + 2, :],
                                           ps_hid[pair % 2][:].rearrange("p (a s) -> p a s", a=2), ACT.Gelu)\
                               .then_inc(hid_ready, 1)
                        act.wait_ge(res_ready, e + 1)
                        act.dma_start(results_dram.rearrange("(e s p) c -> e p s c", s=ST, p=P)
                                      [bass.ds(e, 1)].rearrange("a p s c -> (a p) s c"), result[k][:])\
                           .then_inc(res_stored, 16)
                act.wait_ge(res_stored, 16 * EXPERTS)

            @block.vector
            def _(dve):
                with dve.Fori(0, EXPERTS // 2) as turn:
                    for k in range(2):
                        e = turn * 2 + k
                        dve.wait_ge(cols_turned, e + 1)
                        dve.tensor_copy(cols[k][:].rearrange("p k s -> p (k s)"), ps_cols[:]).then_inc(cols_ready, 1)
                        dve.wait_ge(res_made, e + 1)
                        dve.wait_ge(res_stored, turn * 32)
                        dve.tensor_copy(result[k][:].rearrange("p s c -> p (s c)"), ps_res[:]).then_inc(res_ready, 1)

            @block.tensor
            def _(pe):
                with pe.Fori(0, EXPERTS // 2) as turn:
                    for k in range(2):
                        e = turn * 2 + k
                        pe.wait_ge(rows_in[k], (turn + 1) * 16)
                        pe.wait_ge(cols_ready, e)
                        for c in range(KC):
                            for s in range(ST):
                                last = pe.transpose(ps_cols[:, c * CAPACITY + s * P:c * CAPACITY + (s + 1) * P],
                                                    rows[k][:, s, c * P:(c + 1) * P], ident[:])
                        last.then_inc(cols_turned, 1)
                        pe.wait_ge(cols_ready, e + 1)
                        pe.wait_ge(weights_in[k], (turn + 1) * 32)
                        for pair in range(HC // 2):
                            if pair >= 2:
                                pe.wait_ge(hid_ready, e * (HC // 2) + pair - 1)
                            else:
                                pe.wait_ge(hid_ready, e * (HC // 2))
                            for m in range(2):
                                for c in range(KC):
                                    last = pe.matmul(ps_hid[pair % 2][:, m * CAPACITY:(m + 1) * CAPACITY],
                                                     up_w[k][:, c, (2 * pair + m) * P:(2 * pair + m + 1) * P],
                                                     cols[k][:, c, :], start=(c == 0), stop=(c == KC - 1))
                            last.then_inc(hid_made, 1)
                        pe.wait_ge(hid_ready, (e + 1) * (HC // 2))
                        pe.wait_ge(res_ready, e)
                        for s in range(ST):
                            for m in range(HC):
                                last = pe.matmul(ps_res[:, s * C:(s + 1) * C], hidden[k][:, m, s * P:(s + 1) * P],
                                                 down_w[k][:, m, :], start=(m == 0), stop=(m == HC - 1))
                        last.then_inc(res_made, 1)

        with ExitStack() as ctx:
            RING = 8
            got = sb("got", [P, RING, C], ctx=ctx)
            fetched = [sem(f"fetched{k}") for k in range(RING)]
            added = sem("added")
            stored = sem("stored")
            block = ctx.enter_context(nc.Block())

            @block.gpsimd
            def _(pool):
                for t in range(NT):
                    if t >= RING:
                        pool.wait_ge(added, t - RING + 1)
                    pool.indirect_dma_start(
                        out=got[:, t % RING, :], out_offset=None, in_=results_dram,
                        in_offset=bass.IndirectOffsetOnAxis(ap=fetch_at[:, t:t + 1].bitcast(U32), axis=0),
                        bounds_check=KEPT - 1, oob_is_err=False).then_inc(fetched[t % RING], 16)

            @block.vector
            def _(dve):
                for t in range(NT):
                    dve.wait_ge(fetched[t % RING], 16 * (t // RING + 1))
                    dve.scalar_tensor_tensor(out=base[:, t, :], in0=got[:, t % RING, :], scalar=weight[:, t:t + 1],
                                             in1=base[:, t, :], op0=ALU.mult, op1=ALU.add).then_inc(added, 1)

            @block.sync
            def _(sp):
                with sp.Fori(0, BATCH) as b:
                    sp.wait_ge(added, (b + 1) * TILES)
                    sp.dma_start(x_out[bass.ds(b * TILES, TILES)].rearrange("n p c -> p n c"),
                                 base[:, bass.ds(b * TILES, TILES), :]).then_inc(stored, 16)
                sp.wait_ge(stored, 16 * BATCH)


FIELDS = 6
FA, FB, FW, FK, FV, FR = range(FIELDS)
PACK = FIELDS * D
STEPS = 16
BATCHED = 8
COPIED = 4
STATE = D * D
RING = 8


def recurrence(nc, packed, o_out):
    with ExitStack() as ctx:
        def sb(name, shape, dt=F32):
            return ctx.enter_context(nc.sbuf_tensor("sc_" + name, shape, dt))

        def psum(name, shape):
            return ctx.enter_context(nc.psum_tensor("sc_" + name, shape, F32))

        sem = ctx.enter_context(semaphores(nc, "sc_"))

        pack = [sb(f"pack{h}", [P, STEPS, PACK]) for h in range(2)]
        outer = [sb(f"outer{h}", [P, STEPS, STATE]) for h in range(2)]
        seen = [sb(f"seen{h}", [P, STEPS, STATE]) for h in range(2)]
        o_buf = [sb(f"o_buf{h}", [P, STEPS * D]) for h in range(2)]
        ident = sb("ident", [P, P])
        sa = sb("sa", [P, D])
        rank1 = sb("rank1", [P, STATE])
        state = psum("state", [P, RING, STATE])
        prod = psum("prod", [P, STATE])
        kept = psum("kept", [P, STATE])
        ps_o = [psum(f"ps_o{h}", [P, STEPS * D]) for h in range(2)]

        OPS = 6
        HALF = OPS * STEPS
        chain = sem("chain")
        consts = sem("consts")
        packed_in = [sem(f"packed_in{h}") for h in range(2)]
        outer_made = [sem(f"outer_made{h}") for h in range(2)]
        copied = [sem(f"copied{k}") for k in range(2)]
        times_r = [sem(f"times_r{h}") for h in range(2)]
        o_made = [sem(f"o_made{h}") for h in range(2)]
        o_copied = [sem(f"o_copied{h}") for h in range(2)]
        o_stored = [sem(f"o_stored{h}") for h in range(2)]
        HALVES = T // STEPS
        TURNS = HALVES // 2
        PARTS = STEPS // BATCHED
        QUARTERS = STEPS // COPIED

        block = ctx.enter_context(nc.Block())

        def field(h, t, f):
            return pack[h][:, t, f * D:(f + 1) * D]

        @block.sync
        def _(sp):
            with sp.Fori(0, TURNS) as i:
                for h in range(2):
                    sp.wait_ge(chain, (i * 2 + h) * HALF)
                    sp.wait_ge(times_r[h], i * PARTS)
                    for b in range(BATCH):
                        sp.dma_start(pack[h][b * HEADS:(b + 1) * HEADS, :, :],
                                     packed[b, bass.ds(i * 2 * STEPS + h * STEPS, STEPS)]
                                     .rearrange("t h f -> h t f")).then_inc(packed_in[h], 16)

        @block.gpsimd
        def _(pool):
            own = Tally(pool, consts)
            own.link(pool.memset(ident[:], 0.0))
            own.up(pool.affine_select(out=ident[:], in_=ident[:], compare_op=ALU.not_equal, fill=1.0, base=0,
                                      pattern=[[-1, P]], channel_multiplier=1))

            def outers(i, h):
                pool.wait_ge(packed_in[h], (i + 1) * 16 * BATCH)
                pool.wait_ge(chain, (i * 2 + h) * HALF)
                for part in range(PARTS):
                    t = slice(part * BATCHED, (part + 1) * BATCHED)
                    shape = [P, BATCHED, D, D]
                    pool.tensor_tensor(
                        outer[h][:, t, :].rearrange("p t (i j) -> p t i j", j=D),
                        pack[h][:, t, FV * D:(FV + 1) * D].unsqueeze(3).broadcast_to(shape),
                        pack[h][:, t, FK * D:(FK + 1) * D].unsqueeze(2).broadcast_to(shape), ALU.mult)\
                        .then_inc(outer_made[h], 1)

            def read_states(i, h):
                for part in range(PARTS):
                    t = slice(part * BATCHED, (part + 1) * BATCHED)
                    shape = [P, BATCHED, D, D]
                    for k in range(2):
                        pool.wait_ge(copied[k], i * QUARTERS + h * QUARTERS // 2 + part + 1)
                    states = seen[h][:, t, :].rearrange("p t (i j) -> p t i j", j=D)
                    pool.tensor_tensor(states, states,
                                       pack[h][:, t, FR * D:(FR + 1) * D].unsqueeze(2).broadcast_to(shape),
                                       ALU.mult).then_inc(times_r[h], 1)

            outers(0, 0)
            with pool.Fori(0, TURNS - 1) as i:
                outers(i, 1)
                read_states(i, 0)
                outers(i + 1, 0)
                read_states(i, 1)
            outers(TURNS - 1, 1)
            read_states(TURNS - 1, 0)
            read_states(TURNS - 1, 1)

        @block.vector
        def _(dve):
            dve.memset(state[:, RING - 1, :], 0.0).then_inc(chain, HALF)
            square = [P, D, D]
            with dve.Fori(0, TURNS) as i:
                for h in range(2):
                    for t in range(STEPS):
                        n = h * STEPS + t
                        base = HALF + i * (2 * HALF) + n * OPS
                        old = state[:, (n - 1) % RING, :].rearrange("p (i j) -> p i j", j=D)
                        new = state[:, n % RING, :].rearrange("p (i j) -> p i j", j=D)
                        kept_s = kept[:].rearrange("p (i j) -> p i j", j=D)
                        prod_s = prod[:].rearrange("p (i j) -> p i j", j=D)
                        rank1_s = rank1[:].rearrange("p (i j) -> p i j", j=D)
                        if t == 0:
                            dve.wait_ge(packed_in[h], (i + 1) * 16 * BATCH)
                        dve.wait_ge(chain, base)
                        dve.tensor_tensor(prod_s, old, field(h, t, FA).unsqueeze(1).broadcast_to(square), ALU.mult)\
                           .then_inc(chain, 1)
                        dve.tensor_tensor(kept_s, old, field(h, t, FW).unsqueeze(1).broadcast_to(square), ALU.mult)\
                           .then_inc(chain, 1)
                        dve.wait_ge(chain, base + 1)
                        dve.tensor_reduce(sa[:], prod_s, AX.X, ALU.add).then_inc(chain, 1)
                        if t % BATCHED == 0:
                            dve.wait_ge(outer_made[h], i * PARTS + t // BATCHED + 1)
                        dve.wait_ge(chain, base + 2)
                        dve.tensor_tensor(kept[:], kept[:], outer[h][:, t, :], ALU.add).then_inc(chain, 1)
                        dve.wait_ge(chain, base + 3)
                        dve.tensor_tensor(rank1_s, sa[:].unsqueeze(2).broadcast_to(square),
                                          field(h, t, FB).unsqueeze(1).broadcast_to(square), ALU.mult)\
                           .then_inc(chain, 1)
                        if n % COPIED == 0:
                            m = n // COPIED
                            dve.wait_ge(copied[m % 2], i * QUARTERS + m // 2)
                        dve.wait_ge(chain, base + 5)
                        dve.tensor_tensor(new, kept_s, rank1_s, ALU.add).then_inc(chain, 1)
            dve.wait_ge(chain, HALF + TURNS * 2 * HALF)
            dve.memset(rank1[:], 0.0).then_inc(chain, 2)

        @block.scalar
        def _(act):
            def bring(i, h, q):
                n = h * STEPS + q * COPIED
                m = n // COPIED
                if q == 0:
                    act.wait_ge(o_made[h], i)
                act.wait_ge(chain, HALF + i * (2 * HALF) + (n + COPIED) * OPS + 2)
                act.activation(seen[h][:, q * COPIED:(q + 1) * COPIED, :],
                               state[:, n % RING:n % RING + COPIED, :], ACT.Copy).then_inc(copied[m % 2], 1)

            def finish(i, h):
                act.wait_ge(o_made[h], i + 1)
                act.wait_ge(o_stored[h], i * 16 * BATCH)
                act.activation(o_buf[h][:], ps_o[h][:], ACT.Copy).then_inc(o_copied[h], 1)
                act.wait_ge(o_copied[h], i + 1)
                for b in range(BATCH):
                    act.dma_start(o_out[b, bass.ds(i * 2 * STEPS + h * STEPS, STEPS)].rearrange("t h d -> h t d"),
                                  o_buf[h][b * HEADS:(b + 1) * HEADS, :].rearrange("p (t d) -> p t d", d=D))\
                       .then_inc(o_stored[h], 16)

            for q in range(QUARTERS):
                bring(0, 0, q)
            for q in range(QUARTERS):
                bring(0, 1, q)
                if q == 2:
                    finish(0, 0)
            with act.Fori(1, TURNS) as i:
                for h in range(2):
                    for q in range(QUARTERS):
                        bring(i, h, q)
                        if q == 2:
                            finish(i - 1 + h, 1 - h)
            finish(TURNS - 1, 1)
            for h in range(2):
                act.wait_ge(o_stored[h], TURNS * 16 * BATCH)

        @block.tensor
        def _(pe):
            pe.wait_ge(consts, 2)
            with pe.Fori(0, TURNS) as i:
                for h in range(2):
                    pe.wait_ge(times_r[h], (i + 1) * PARTS)
                    pe.wait_ge(o_copied[h], i)
                    terms = seen[h][:].rearrange("p t (i j) -> p (t i) j", j=D)
                    for j in range(D):
                        last = pe.matmul(ps_o[h][:], ident[:], terms[:, :, j], start=(j == 0), stop=(j == D - 1))
                    last.then_inc(o_made[h], 1)


RW, RG = 64, 128
HALF_TILES = TILES // 2
MIXES = ("r", "w", "a", "k", "v")


def preparation_plan():
    plan = [("turn_x", c) for c in range(KC)]
    plan += [("r", 0), ("r", 1), ("turn_r", 0), ("turn_r", 1), ("w_inner", 0), ("g_inner", 0), ("w", 0), ("w", 1),
             ("a_inner", 0), ("g", 0), ("g", 1), ("a", 0), ("a", 1), ("k", 0), ("k", 1), ("v", 0), ("v", 1)]
    return plan


PREPARATION_USER = {"turn_x": "act", "r": "act", "turn_r": "act", "w_inner": "act", "g_inner": "act", "w": "dve",
                    "a_inner": "act", "g": "dve", "a": "dve", "k": "dve", "v": "act"}


def prepare(nc, x_in, mixes, k_k, k_a, r_k, weights, w_a, w_b, w_bias, a_a, a_b, a_bias, g_a, g_b, g_bias,
            packed, gate_out, bonus_out):
    plan, slot_uses, place = with_slots(preparation_plan())
    with ExitStack() as ctx:
        def sb(name, shape, dt=F32):
            return ctx.enter_context(nc.sbuf_tensor("pr_" + name, shape, dt))

        sem = ctx.enter_context(semaphores(nc, "pr_"))

        ctx.enter_context(nc.allow_non_contiguous_dma(reason="mixing columns"))
        slot = [ctx.enter_context(nc.psum_tensor(f"pr_slot{s}", [P, 2 * BANK], F32)) for s in range(SLOTS)]
        big = {m: sb("big_" + m, [P, KC, C]) for m in "rkv"}
        mu = {m: sb("mu_" + m, [P, KC]) for m in MIXES}
        inner_a = {"w": sb("w_inner_a", [P, KC, RW]), "a": sb("a_inner_a", [P, KC, RW]), "g": sb("g_inner_a", [P, KC, RG])}
        inner_b = {"w": sb("w_inner_b", [RW, C]), "a": sb("a_inner_b", [RW, C]), "g": sb("g_inner_b", [RG, C])}
        wide = {m: sb("wide_" + m, [P, C]) for m in ("k_k", "k_a", "r_k", "w", "a", "g")}
        ident = sb("ident", [P, P])
        x = sb("x", [P, TILES, C])
        xn = sb("xn", [P, TILES, C])
        stats = sb("stats", [P, TILES, 6])
        mean_var = sb("mean_var", [P, TILES, 2])
        std = sb("std", [P, TILES])
        rstd = sb("rstd", [P, TILES])
        turned = sb("turned", [P, KC, T + 1])
        delta = sb("delta", [P, KC, T])
        mixed = [sb(f"mixed{k}", [P, KC, T]) for k in range(2)]
        pack = [sb(f"pack{h}", [P, HALF_TILES * HEADS, PACK]) for h in range(2)]
        r_turned = sb("r_turned", [P, KC, T])
        inner = {"w": sb("w_inner", [RW, T]), "a": sb("a_inner", [RW, T]), "g": sb("g_inner", [RG, T])}
        HW = HALF_TILES * C
        r_rows = [sb(f"r_rows{h}", [P, HW]) for h in range(2)]
        gate_sb = sb("gate_sb", [P, HW])
        z = sb("z", [P, HW])
        a_sig = [sb(f"a_sig{h}", [P, HW]) for h in range(2)]
        scaled = sb("scaled", [P, HW])
        kk = sb("kk", [P, HW])
        squares = sb("squares", [P, HW])
        norm = sb("norm", [P, HALF_TILES * HEADS])
        rr = sb("rr", [P, HW])
        dots = sb("dots", [P, HALF_TILES * HEADS])
        bonus = sb("bonus", [P, HW])

        loaded = sem("loaded")
        consts = sem("consts")
        x_loaded = sem("x_loaded")
        var_ready = sem("var_ready")
        std_ready = sem("std_ready")
        xn_ready = sem("xn_ready")
        chain = sem("chain")
        mix_ready = sem("mix_ready")
        filled = [sem(f"filled{s}") for s in range(SLOTS)]
        emptied = [sem(f"emptied{s}") for s in range(SLOTS)]
        r_copied = sem("r_copied")
        z_used = sem("z_used")
        w_packed = sem("w_packed")
        kk_ready = sem("kk_ready")
        squared = sem("squared")
        norm2_ready = sem("norm2_ready")
        norm_ready = sem("norm_ready")
        rr_ready = sem("rr_ready")
        bonus_ready = sem("bonus_ready")
        pack_stored = sem("pack_stored")
        gate_stored = sem("gate_stored")
        bonus_stored = sem("bonus_stored")
        N_LOADS = 3 + len(MIXES) + 6 + 6

        def read_out(eng, b, *uses):
            latest = {}
            for stage, what in uses:
                s, use = place[stage, what]
                latest[s] = max(latest.get(s, 0), use + 1)
            for s, use in latest.items():
                eng.wait_ge(emptied[s], b * slot_uses[s] + use)

        def field(h, f):
            return pack[h][:, :, f * D:(f + 1) * D]

        def by_head(ap):
            return ap.rearrange("p (n d) -> p n d", d=D)

        block = ctx.enter_context(nc.Block())

        @block.sync
        def _(sp):
            loads = [(big[m][:], weights[m].rearrange("(k p) n -> p k n", p=P)) for m in "rkv"]
            loads += [(mu[m][:], mixes[m].rearrange("(k p) -> p k", p=P)) for m in MIXES]
            loads += [(inner_a[m][:], src.rearrange("(k p) n -> p k n", p=P)) for m, src in
                      (("w", w_a), ("a", a_a), ("g", g_a))]
            loads += [(inner_b[m][:], src) for m, src in (("w", w_b), ("a", a_b), ("g", g_b))]
            loads += [(wide[m][:], spread(src)) for m, src in
                      (("k_k", k_k), ("k_a", k_a), ("r_k", r_k), ("w", w_bias), ("a", a_bias), ("g", g_bias))]
            assert len(loads) == N_LOADS
            for dst, src in loads:
                sp.dma_start(dst, src).then_inc(loaded, 16)
            with sp.Fori(0, BATCH) as b:
                sp.wait_ge(xn_ready, b * TILES)
                sp.dma_start(x[:], x_in[bass.ds(b * TILES, TILES)].rearrange("n p c -> p n c")).then_inc(x_loaded, 16)
                for h in range(2):
                    rows = bass.ds(b * TILES + h * HALF_TILES, HALF_TILES)
                    read_out(sp, b, ("g", h))
                    sp.dma_start(gate_out[rows].rearrange("n p c -> p n c"),
                                 gate_sb[:].rearrange("p (n c) -> p n c", c=C)).then_inc(gate_stored, 16)
                for h in range(2):
                    rows = bass.ds(b * TILES + h * HALF_TILES, HALF_TILES)
                    sp.wait_ge(bonus_ready, b * 2 + h + 1)
                    sp.dma_start(bonus_out[rows].rearrange("n p c -> p n c"),
                                 bonus[:].rearrange("p (n c) -> p n c", c=C)).then_inc(bonus_stored, 16)
                    sp.wait_ge(w_packed, b * 2 + h + 1)
                    sp.dma_start(packed[rows].rearrange("n p f -> p n f"),
                                 pack[h][:].rearrange("p (n h) f -> p n (h f)", h=HEADS)).then_inc(pack_stored, 16)
            sp.wait_ge(gate_stored, BATCH * 32)
            sp.wait_ge(bonus_stored, BATCH * 32)
            sp.wait_ge(pack_stored, BATCH * 32)

        @block.gpsimd
        def _(pool):
            own = Tally(pool, consts)
            own.up(pool.memset(turned[:], 0.0))
            own.link(pool.memset(ident[:], 0.0))
            own.up(pool.affine_select(out=ident[:], in_=ident[:], compare_op=ALU.not_equal, fill=1.0, base=0,
                                      pattern=[[-1, P]], channel_multiplier=1))
            pool.wait_ge(loaded, 16 * N_LOADS)
            r_k_wide = wide["r_k"][:].unsqueeze(1).broadcast_to([P, HALF_TILES, C])\
                .rearrange("p n (h d) -> p n h d", d=D)
            with pool.Fori(0, BATCH) as b:
                for h in range(2):
                    read_out(pool, b, ("r", h))
                    pool.wait_ge(bonus_ready, b * 2 + h)
                    pool.tensor_tensor(rr[:].rearrange("p (n h d) -> p n h d", d=D, h=HEADS),
                                       field(h, FR).rearrange("p (n h) d -> p n h d", h=HEADS), r_k_wide, ALU.mult)\
                        .then_inc(rr_ready, 1)
                    read_out(pool, b, ("k", h))
                    pool.wait_ge(rr_ready, b * 4 + h * 2 + 1)
                    pool.tensor_tensor(by_head(rr[:]), by_head(rr[:]), field(h, FK), ALU.mult).then_inc(rr_ready, 1)

        @block.tensor
        def _(pe):
            pe.wait_ge(consts, 3)
            pe.wait_ge(loaded, 16 * N_LOADS)
            mixed_of = {m: (mixed[n % 2], n) for n, m in enumerate(MIXES)}
            with pe.Fori(0, BATCH) as b:
                for stage, what, s, use in plan:
                    ps = slot[s]
                    pe.wait_ge(emptied[s], b * slot_uses[s] + use)
                    if stage == "turn_x":
                        if what == 0:
                            pe.wait_ge(xn_ready, (b + 1) * TILES)
                        for t in range(TILES):
                            last = pe.transpose(ps[:, t * P:(t + 1) * P], xn[:, t, what * P:(what + 1) * P], ident[:])
                    elif stage in ("r", "k", "v"):
                        src, n = mixed_of[stage]
                        if what == 0:
                            pe.wait_ge(mix_ready, b * len(MIXES) + n + 1)
                        for n in range(HALF_TILES):
                            t = HALF_TILES * what + n
                            for k in range(KC):
                                last = pe.matmul(ps[:, n * C:(n + 1) * C], src[:, k, t * P:(t + 1) * P],
                                                 big[stage][:, k, :], start=(k == 0), stop=(k == KC - 1))
                    elif stage == "turn_r":
                        if what == 0:
                            read_out(pe, b, ("r", 0), ("r", 1))
                        for t in range(TILES):
                            n = (t % HALF_TILES) * C + what * P
                            last = pe.transpose(ps[:, t * P:(t + 1) * P], r_rows[t // HALF_TILES][:, n:n + P],
                                                ident[:])
                    elif stage in ("w_inner", "a_inner", "g_inner"):
                        m = stage[0]
                        if m == "g":
                            read_out(pe, b, ("turn_r", 0), ("turn_r", 1))
                            src = r_turned
                        else:
                            src, n = mixed_of[m]
                            pe.wait_ge(mix_ready, b * len(MIXES) + n + 1)
                        width = inner_a[m].shape[2]
                        for half in range(2):
                            for k in range(KC):
                                last = pe.matmul(ps[0:width, half * BANK:(half + 1) * BANK], inner_a[m][:, k, :],
                                                 src[:, k, half * BANK:(half + 1) * BANK],
                                                 start=(k == 0), stop=(k == KC - 1))
                    else:
                        if what == 0:
                            read_out(pe, b, (stage + "_inner", 0))
                        for n in range(HALF_TILES):
                            t = HALF_TILES * what + n
                            last = pe.matmul(ps[:, n * C:(n + 1) * C], inner[stage][:, t * P:(t + 1) * P],
                                             inner_b[stage][:], start=True, stop=True)
                    last.then_inc(filled[s], 1)

        @block.scalar
        def _(act):
            act.wait_ge(consts, 3)
            with act.Fori(0, BATCH) as b:
                act.wait_ge(var_ready, b + 1)
                act.activation(std[:], mean_var[:, :, 1], ACT.Sqrt).then_inc(std_ready, 1)
                for stage, what, s, use in plan:
                    ps = slot[s]
                    if PREPARATION_USER[stage] == "act":
                        act.wait_ge(filled[s], b * slot_uses[s] + use + 1)
                    if stage == "turn_x":
                        if what == 0:
                            act.wait_ge(mix_ready, b * len(MIXES))
                        act.activation(turned[:, what, 1:T + 1], ps[:], ACT.Copy).then_inc(emptied[s], 1)
                    elif stage in ("r", "v"):
                        f = FR if stage == "r" else FV
                        if stage == "r":
                            act.wait_ge(pack_stored, b * 32)
                            act.activation(r_rows[what][:], ps[:], ACT.Copy).then_inc(r_copied, 1)
                            act.wait_ge(r_copied, b * 2 + what + 1)
                        act.activation(field(what, f), by_head(ps[:]), ACT.Copy).then_inc(emptied[s], 1)
                    elif stage == "turn_r":
                        act.activation(r_turned[:, what, :], ps[:], ACT.Copy).then_inc(emptied[s], 1)
                    elif stage in ("w_inner", "a_inner", "g_inner"):
                        m = stage[0]
                        width = inner_a[m].shape[2]
                        act.activation(inner[m][:], ps[0:width, :],
                                       {"w": ACT.Tanh, "a": ACT.Copy, "g": ACT.Sigmoid}[m]).then_inc(emptied[s], 1)
                    elif stage == "w":
                        read_out(act, b, (stage, what))
                        act.activation(z[:], z[:], ACT.Sigmoid).then_inc(z_used, 1)
                        act.wait_ge(z_used, b * 4 + what + 1)
                        act.activation(field(what, FW), by_head(z[:]), ACT.Copy, scale=float(np.exp(-0.5)))\
                           .then_inc(w_packed, 1)
                    elif stage == "a":
                        read_out(act, b, (stage, what))
                        act.wait_ge(bonus_ready, b * 2)
                        act.activation(a_sig[what][:], z[:], ACT.Sigmoid).then_inc(z_used, 1)
                    elif stage == "k":
                        act.wait_ge(kk_ready, b * 2 + what + 1)
                        act.activation(squares[:], kk[:], ACT.Square).then_inc(squared, 1)
                        act.wait_ge(norm2_ready, b * 2 + what + 1)
                        act.activation(norm[:], norm[:], ACT.Sqrt).then_inc(norm_ready, 1)

        @block.vector
        def _(dve):
            dve.wait_ge(consts, 3)
            dve.wait_ge(loaded, 16 * N_LOADS)
            TURN = 2 * TILES + 1 + KC + 2 * 6
            with dve.Fori(0, BATCH) as b:
                own = Tally(dve, chain, b * TURN)
                dve.wait_ge(x_loaded, (b + 1) * 16)
                for t in range(TILES):
                    own.up(dve.bn_stats(stats[:, t, :], x[:, t, :]))
                own.done()
                dve.nop(nofuse=True)
                for t in range(TILES):
                    own.up(dve.bn_aggr(mean_var[:, t, :], stats[:, t, :]))
                own.done()
                dve.tensor_scalar(mean_var[:, :, 1], mean_var[:, :, 1], LN_EPS, None, ALU.add).then_inc(var_ready, 1)
                dve.wait_ge(std_ready, b + 1)
                own.link(dve.reciprocal(rstd[:], std[:]))
                for t in range(TILES):
                    dve.tensor_scalar(xn[:, t, :], x[:, t, :], mean_var[:, t, 0:1], rstd[:, t:t + 1],
                                      ALU.subtract, ALU.mult).then_inc(xn_ready, 1)
                read_out(dve, b, ("turn_x", 0), ("turn_x", 1))
                for k in range(KC):
                    own.up(dve.tensor_tensor(delta[:, k, :], turned[:, k, 0:T], turned[:, k, 1:T + 1], ALU.subtract))
                own.done()

                def mix(m):
                    n = MIXES.index(m)
                    if n >= 2:
                        before = MIXES[n - 2]
                        read_out(dve, b, *{"r": [("r", 1)], "w": [("w_inner", 0)], "a": [("a_inner", 0)]}[before])
                    for k in range(KC):
                        ins = dve.scalar_tensor_tensor(out=mixed[n % 2][:, k, :], in0=delta[:, k, :],
                                                       scalar=mu[m][:, k:k + 1], in1=turned[:, k, 1:T + 1],
                                                       op0=ALU.mult, op1=ALU.add)
                    ins.then_inc(mix_ready, 1)

                mix("r")
                mix("w")
                for stage, what, s, use in plan:
                    ps = slot[s]
                    if stage == "w" and what == 0:
                        mix("a")
                    if stage == "g" and what == 0:
                        mix("k")
                    if stage == "k" and what == 0:
                        mix("v")
                    if PREPARATION_USER[stage] != "dve":
                        continue
                    wide_of = {m: wide[m][:].unsqueeze(1).broadcast_to([P, HALF_TILES, C]) for m in wide}
                    by_tile = lambda ap: ap.rearrange("p (n c) -> p n c", c=C)
                    dve.wait_ge(filled[s], b * slot_uses[s] + use + 1)
                    if stage in ("w", "a"):
                        n = what + (2 if stage == "a" else 0)
                        dve.wait_ge(z_used, b * 4 + n)
                        dve.wait_ge(w_packed, b * 2 + min(n, 2))
                        dve.tensor_tensor(by_tile(z[:]), by_tile(ps[:]), wide_of[stage], ALU.add)\
                           .then_inc(emptied[s], 1)
                    elif stage == "g":
                        dve.wait_ge(gate_stored, b * 32 + what * 16)
                        dve.tensor_tensor(by_tile(gate_sb[:]), by_tile(ps[:]), wide_of["g"], ALU.add)\
                           .then_inc(emptied[s], 1)
                    elif stage == "k":
                        dve.wait_ge(z_used, b * 4 + 2 + what + 1)
                        own.up(dve.scalar_tensor_tensor(
                            out=by_tile(scaled[:]), in0=by_tile(a_sig[what][:]), scalar=-1.0, in1=wide_of["k_a"],
                            op0=ALU.add, op1=ALU.mult))
                        dve.wait_ge(squared, b * 2 + what)
                        dve.tensor_tensor(by_tile(kk[:]), by_tile(ps[:]), wide_of["k_k"], ALU.mult)\
                           .then_inc(kk_ready, 1)
                        own.done()
                        dve.scalar_tensor_tensor(out=field(what, FK), in0=by_head(scaled[:]), scalar=1.0,
                                                 in1=by_head(ps[:]), op0=ALU.add, op1=ALU.mult)\
                           .then_inc(emptied[s], 1)
                        dve.wait_ge(squared, b * 2 + what + 1)
                        dve.tensor_reduce(norm[:], by_head(squares[:]), AX.X, ALU.add).then_inc(norm2_ready, 1)
                        dve.wait_ge(norm_ready, b * 2 + what + 1)
                        own.link(dve.tensor_scalar(norm[:], norm[:], 1e-12, -1.0, ALU.max, ALU.mult))
                        own.link(dve.reciprocal(norm[:], norm[:]))
                        own.link(dve.tensor_tensor(field(what, FA), by_head(kk[:]),
                                                   norm[:].unsqueeze(2).broadcast_to([P, HALF_TILES * HEADS, D]),
                                                   ALU.mult))
                        own.up(dve.scalar_tensor_tensor(out=field(what, FB), in0=field(what, FA), scalar=-1.0,
                                                        in1=by_head(a_sig[what][:]), op0=ALU.mult, op1=ALU.mult))
                        own.done()
                for h in range(2):
                    dve.wait_ge(rr_ready, b * 4 + h * 2 + 2)
                    own.link(dve.tensor_reduce(dots[:], by_head(rr[:]), AX.X, ALU.add))
                    read_out(dve, b, ("v", h))
                    dve.wait_ge(bonus_stored, b * 32 + h * 16)
                    dve.tensor_tensor(by_head(bonus[:]), field(h, FV),
                                      dots[:].unsqueeze(2).broadcast_to([P, HALF_TILES * HEADS, D]), ALU.mult)\
                       .then_inc(bonus_ready, 1)
                assert own.n == TURN, own.n


def finish(nc, x_in, o_in, gate_in, bonus_in, gn_weight, gn_bias, w_o, x_out):
    with ExitStack() as ctx:
        def sb(name, shape, dt=F32):
            return ctx.enter_context(nc.sbuf_tensor("fi_" + name, shape, dt))

        sem = ctx.enter_context(semaphores(nc, "fi_"))

        slot = [ctx.enter_context(nc.psum_tensor(f"fi_slot{s}", [P, 2 * BANK], F32)) for s in range(4)]
        w = sb("w", [P, KC, C])
        ident = sb("ident", [P, P])
        wide_w = sb("wide_w", [P, C])
        wide_b = sb("wide_b", [P, C])
        x = [sb(f"x{k}", [P, TILES, C]) for k in range(2)]
        o = [sb(f"o{k}", [P, TILES, C]) for k in range(2)]
        gate = [sb(f"gate{k}", [P, TILES, C]) for k in range(2)]
        bonus = [sb(f"bonus{k}", [P, TILES, C]) for k in range(2)]
        squares = sb("squares", [P, TILES * C])
        mean = sb("mean", [P, TILES * HEADS])
        var = sb("var", [P, TILES * HEADS])
        turned = sb("turned", [P, KC, T])

        loaded = sem("loaded")
        consts = sem("consts")
        in_ready = [sem(f"in_ready{k}") for k in range(2)]
        chain = sem("chain")
        centred = sem("centred")
        squared = sem("squared")
        var_ready = sem("var_ready")
        std_ready = sem("std_ready")
        normed = sem("normed")
        with_bias = sem("with_bias")
        gated = sem("gated")
        turn_made = sem("turn_made")
        turn_ready = sem("turn_ready")
        y_made = sem("y_made")
        y_ready = sem("y_ready")
        stored = [sem(f"stored{k}") for k in range(2)]
        block = ctx.enter_context(nc.Block())

        @block.sync
        def _(sp):
            sp.dma_start(w[:], w_o.rearrange("(k p) n -> p k n", p=P)).then_inc(loaded, 16)
            sp.dma_start(wide_w[:], spread(gn_weight)).then_inc(loaded, 16)
            sp.dma_start(wide_b[:], spread(gn_bias)).then_inc(loaded, 16)
            with sp.Fori(0, BATCH // 2) as i:
                for k in range(2):
                    rows = bass.ds(i * 2 * TILES + k * TILES, TILES)
                    sp.wait_ge(stored[k], i * 16)
                    for dst, src in ((x, x_in), (o, o_in), (gate, gate_in), (bonus, bonus_in)):
                        sp.dma_start(dst[k][:], src[rows].rearrange("n p c -> p n c")).then_inc(in_ready[k], 16)

        @block.gpsimd
        def _(pool):
            own = Tally(pool, consts)
            own.link(pool.memset(ident[:], 0.0))
            own.up(pool.affine_select(out=ident[:], in_=ident[:], compare_op=ALU.not_equal, fill=1.0, base=0,
                                      pattern=[[-1, P]], channel_multiplier=1))
            pool.wait_ge(loaded, 48)
            bias_wide = wide_b[:].unsqueeze(1).broadcast_to([P, TILES, C])
            with pool.Fori(0, BATCH // 2) as i:
                for k in range(2):
                    b = i * 2 + k
                    pool.wait_ge(in_ready[k], (i + 1) * 64)
                    pool.tensor_tensor(bonus[k][:], bonus[k][:], bias_wide, ALU.add).then_inc(with_bias, 1)

        @block.tensor
        def _(pe):
            pe.wait_ge(consts, 2)
            pe.wait_ge(loaded, 48)
            with pe.Fori(0, BATCH // 2) as i:
                for k in range(2):
                    b = i * 2 + k
                    pe.wait_ge(gated, b + 1)
                    pe.wait_ge(turn_ready, b * KC)
                    for c in range(KC):
                        for t in range(TILES):
                            last = pe.transpose(slot[c][:, t * P:(t + 1) * P], o[k][:, t, c * P:(c + 1) * P], ident[:])
                        last.then_inc(turn_made, 1)
                    pe.wait_ge(turn_ready, b * KC + KC)
                    pe.wait_ge(y_ready, b * 2)
                    for h in range(2):
                        for n in range(HALF_TILES):
                            t = h * HALF_TILES + n
                            for c in range(KC):
                                last = pe.matmul(slot[2 + h][:, n * C:(n + 1) * C], turned[:, c, t * P:(t + 1) * P],
                                                 w[:, c, :], start=(c == 0), stop=(c == KC - 1))
                        last.then_inc(y_made, 1)

        @block.scalar
        def _(act):
            with act.Fori(0, BATCH // 2) as i:
                for k in range(2):
                    b = i * 2 + k
                    act.wait_ge(centred, b + 1)
                    act.activation(squares[:], o[k][:].rearrange("p n c -> p (n c)"), ACT.Square).then_inc(squared, 1)
                    act.wait_ge(var_ready, b + 1)
                    act.activation(var[:], var[:], ACT.Sqrt).then_inc(std_ready, 1)
                    act.wait_ge(y_made, b * 2)
                    for c in range(KC):
                        act.wait_ge(turn_made, b * KC + c + 1)
                        act.activation(turned[:, c, :], slot[c][:], ACT.Copy).then_inc(turn_ready, 1)
                    for h in range(2):
                        act.wait_ge(y_ready, b * 2 + h + 1)
                    act.dma_start(x_out[bass.ds(b * TILES, TILES)].rearrange("n p c -> p n c"), x[k][:])\
                       .then_inc(stored[k], 16)
            for k in range(2):
                act.wait_ge(stored[k], (BATCH // 2) * 16)

        @block.vector
        def _(dve):
            dve.wait_ge(loaded, 48)
            weight_wide = wide_w[:].unsqueeze(1).broadcast_to([P, TILES, C])
            TURN = 12
            with dve.Fori(0, BATCH // 2) as i:
                own = Tally(dve, chain, i * TURN)
                for k in range(2):
                    b = i * 2 + k
                    heads = o[k][:].rearrange("p n (h d) -> p (n h) d", d=D)
                    spread_out = lambda ap: ap.unsqueeze(2).broadcast_to([P, TILES * HEADS, D])
                    dve.wait_ge(in_ready[k], (i + 1) * 64)
                    own.link(dve.tensor_reduce(mean[:], heads, AX.X, ALU.add))
                    own.link(dve.tensor_scalar(mean[:], mean[:], 1.0 / D, None, ALU.mult))
                    dve.tensor_tensor(heads, heads, spread_out(mean[:]), ALU.subtract).then_inc(centred, 1)
                    dve.wait_ge(squared, b + 1)
                    own.link(dve.tensor_reduce(var[:], squares[:].rearrange("p (n d) -> p n d", d=D), AX.X, ALU.add))
                    dve.tensor_scalar(var[:], var[:], 1.0 / D, LN_EPS, ALU.mult, ALU.add).then_inc(var_ready, 1)
                    dve.wait_ge(std_ready, b + 1)
                    own.link(dve.reciprocal(var[:], var[:]))
                    own.link(dve.tensor_tensor(heads, heads, spread_out(var[:]), ALU.mult))
                    own.link(dve.tensor_tensor(o[k][:], o[k][:], weight_wide, ALU.mult))
                    dve.wait_ge(with_bias, b + 1)
                    dve.tensor_tensor(o[k][:], o[k][:], bonus[k][:], ALU.add).then_inc(normed, 1)
                    dve.wait_ge(normed, b + 1)
                    dve.tensor_tensor(o[k][:], o[k][:], gate[k][:], ALU.mult).then_inc(gated, 1)
                    for h in range(2):
                        dve.wait_ge(y_made, b * 2 + h + 1)
                        t = slice(h * HALF_TILES, (h + 1) * HALF_TILES)
                        dve.tensor_tensor(x[k][:, t, :], slot[2 + h][:].rearrange("p (n c) -> p n c", c=C),
                                          x[k][:, t, :], ALU.add).then_inc(y_ready, 1)
                assert own.n == TURN, own.n


def program(nc, a, out):
    def dram(name, shape):
        return nc.dram_tensor(name, shape, F32, kind="Internal").ap()

    def tiles(ap):
        return ap.rearrange("b (n p) c -> (b n) p c", p=P)

    x_attended, x_mixed, x_recurred = (dram(n, (NT, P, C)) for n in ("x_attended", "x_mixed", "x_recurred"))
    slots, results = dram("slots", (KEPT, C)), dram("results", (KEPT, C))
    packed = dram("packed", (NT, P, HEADS * PACK))
    gate, bonus, o = (dram(n, (NT, P, C)) for n in ("gate", "bonus", "o"))
    experts = (a["ffn_gate_weight"], a["ffn_ln_gamma"], a["ffn_ln_beta"], a["ffn_wi"], a["ffn_wo"], slots, results)

    attention(nc, tiles(a["attn_a_x"]), a["attn_a_w_attn"], a["attn_a_b_attn"], a["attn_a_w_proj"],
              a["attn_a_b_proj"], x_attended)
    mixture(nc, 0, x_attended, *experts, x_mixed, clear_slots=True)
    rw = {k.removeprefix("attn_b_"): v for k, v in a.items() if k.startswith("attn_b_")}
    prepare(nc, x_mixed, {m: rw["x_" + m] for m in MIXES}, rw["k_k"], rw["k_a"], rw["r_k"].rearrange("h d -> (h d)"),
            {"r": rw["W_r"], "k": rw["W_k"], "v": rw["W_v"]}, rw["w_lora_a"], rw["w_lora_b"], rw["w_lora_bias"],
            rw["a_lora_a"], rw["a_lora_b"], rw["a_lora_bias"], rw["g_lora_a"], rw["g_lora_b"], rw["g_lora_bias"],
            packed, gate, bonus)
    recurrence(nc, packed.rearrange("(b n) p (h f) -> b (n p) h f", b=BATCH, h=HEADS),
               o.rearrange("(b n) p (h d) -> b (n p) h d", b=BATCH, h=HEADS))
    finish(nc, x_mixed, o, gate, bonus, rw["gn_weight"], rw["gn_bias"], rw["W_o"], x_recurred)
    mixture(nc, 1, x_recurred, *experts, tiles(out), clear_slots=False)


_INS = ["attn_a_x", "attn_a_w_attn", "attn_a_b_attn", "attn_a_w_proj", "attn_a_b_proj",
        "attn_b_x_r", "attn_b_x_w", "attn_b_x_k", "attn_b_x_v", "attn_b_x_a", "attn_b_k_k", "attn_b_k_a",
        "attn_b_r_k", "attn_b_W_r", "attn_b_W_k", "attn_b_W_v", "attn_b_W_o", "attn_b_w_lora_a", "attn_b_w_lora_b",
        "attn_b_w_lora_bias", "attn_b_a_lora_a", "attn_b_a_lora_b", "attn_b_a_lora_bias", "attn_b_g_lora_a",
        "attn_b_g_lora_b", "attn_b_g_lora_bias", "attn_b_gn_weight", "attn_b_gn_bias",
        "ffn_gate_weight", "ffn_ln_gamma", "ffn_ln_beta", "ffn_wi", "ffn_wo"]


def kernel(**inputs):
    import concourse.bacc as _bacc
    from concourse.bass_utils import run_bass_kernel_spmd as _run

    nc = _bacc.Bacc("TRN2", target_bir_lowering=False, num_devices=1)
    arrays, args = {}, {}
    for name in _INS:
        array = np.ascontiguousarray(inputs["L0_" + name])
        arrays[f"in_{name}"] = array
        args[name] = nc.dram_tensor(f"in_{name}", array.shape, mybir.dt.from_np(array.dtype),
                                    kind="ExternalInput").ap()
    out = nc.dram_tensor("out_x", inputs["L0_attn_a_x"].shape, F32, kind="ExternalOutput").ap()
    program(nc, args, out)
    return _run(nc, [arrays], core_ids=[0]).results[0]["out_x"]
```

```python
from contextlib import ExitStack, contextmanager

import numpy as np

import concourse.bass as bass
from concourse import mybir

F32 = mybir.dt.float32
BF16 = mybir.dt.bfloat16
I32 = mybir.dt.int32
U32 = mybir.dt.uint32
ALU = mybir.AluOpType
ACT = mybir.ActivationFunctionType
AX = mybir.AxisListType

P = 128
BATCH, T, C = 8, 1024, 256
TILES = T // P
NT = BATCH * TILES
KC = C // P
HEADS, D = 16, 16
GROUP = 4
PAD = 32
BANK = 512
SLOTS = 3
LN_EPS = 1e-5
MASKED = -1e30


class Tally:

    def __init__(self, eng, sem, base=0):
        self.eng, self.sem, self.base, self.n = eng, sem, base, 0

    def up(self, ins):
        self.n += 1
        return ins.then_inc(self.sem, 1)

    def done(self):
        self.eng.wait_ge(self.sem, 1 + self.base + self.n)

    def link(self, ins):
        self.up(ins)
        self.done()


def spread(row, parts=P):
    return bass.AP(tensor=row.tensor, offset=row.offset, ap=[[0, parts], *row.ap])


@contextmanager
def semaphores(nc, prefix):
    made = []

    def sem(name, start=1):
        made.append(nc.alloc_semaphore(name=prefix + name))
        if start:
            nc.gpsimd.sem_inc(made[-1], start)
        return made[-1]

    yield sem
    nc.clear_and_free_semaphores(made)
    nc.all_engine_barrier()


def causal_rows(q_tile):
    return (q_tile + 1) * P


GROUPS = HEADS // GROUP
HALF_TILES = TILES // 2
HALF_HEADS = HEADS // 2
QK_ORDER = (0, 2, 1, 3)


def maxima(g):
    return [("maxima", (h, qt)) for qt in range(TILES) for h in range(GROUP * g, GROUP * g + GROUP)]


def weights(g):
    return [("weights", (h, kt)) for kt in range(TILES) for h in range(GROUP * g, GROUP * g + GROUP)]


def attention_start():
    plan = [("normalise", 0), ("turn_x", 0), ("turn_x", 1)]
    for n in range(4):
        plan += [("project_qk", n), ("split", n), ("third_part", n)]
    return plan + maxima(0) + [("turn_max", 0), ("project_v", 0), ("project_v", 1)]


def attention_turn(ahead):
    def groups(g):
        jobs = []
        beside = maxima(g + 1) if g + 1 < GROUPS else [("+" + s, w) for s, w in maxima(0)] if ahead else []
        extra = {}
        if g > 0:
            extra[3] = [("values", (g - 1, TILES - 1)), ("copy_out", g - 1)]
            extra[7] = [("turn_out", g - 1)]
        if ahead and g == 0:
            extra[4] = [("+normalise", 0)]
            extra[20] = [("+turn_x", 0), ("+turn_x", 1)]
        if ahead and g in (1, 2):
            n = 2 * g - 2
            extra[8] = [("+project_qk", n)]
            extra[10] = [("+split", n)]
            extra[14] = [("+third_part", n)]
            extra[18] = [("+project_qk", n + 1)]
            extra[20] = [("+split", n + 1)]
            extra[24] = [("+third_part", n + 1)]
        for n, job in enumerate(weights(g)):
            jobs.append(job)
            if beside:
                jobs.append(beside[n])
            jobs += extra.get(n, [])
            if n % GROUP == GROUP - 1 and n > GROUP:
                jobs.append(("values", (g, n // GROUP - 1)))
        if g + 1 < GROUPS:
            jobs.append(("turn_max", g + 1))
        elif ahead:
            jobs.append(("+turn_max", 0))
        return jobs

    plan = [job for g in range(GROUPS) for job in groups(g)]
    plan += [("values", (GROUPS - 1, TILES - 1)), ("copy_out", GROUPS - 1)]
    if ahead:
        plan += [("+project_v", 0)]
    plan += [("turn_out", GROUPS - 1)]
    if ahead:
        plan += [("+project_v", 1)]
    return plan + [("turn_o", c) for c in range(KC)] + [("project_o", half) for half in range(2)]


SLOT_USER = {"turn_x": "act", "project_qk": "act", "project_v": "dve", "maxima": "dve", "turn_max": "act",
             "weights": "act", "turn_out": "dve", "turn_o": "act", "project_o": "dve"}


class Plan:

    def __init__(self, jobs, users, slots):
        self.uses, self.place, self.jobs = [0] * slots, {}, []
        n = 0
        for stage, what in jobs:
            if stage.lstrip("+") in users:
                s = n % slots
                n += 1
                self.place[stage, what] = (s, self.uses[s])
                self.jobs.append((stage, what, s, self.uses[s]))
                self.uses[s] += 1
            else:
                self.jobs.append((stage, what, None, None))


class Slots:

    def __init__(self, plan, before, filled, emptied):
        self.plan, self.before, self.filled, self.emptied = plan, before, filled, emptied

    def wait_empty(self, eng, s, use):
        eng.wait_ge(self.emptied[s], 1 + self.before[s] + use)

    def wait_filled(self, eng, s, use):
        eng.wait_ge(self.filled[s], 1 + self.before[s] + use + 1)

    def wait_read(self, eng, *uses, alone=False):
        latest = {}
        for job in uses:
            s, use = self.plan.place[job]
            latest[s] = max(latest.get(s, 0), use + 1)
        for s, use in latest.items():
            eng.wait_ge(self.emptied[s], 1 + self.before[s] + use)
            if alone:
                eng.nop(nofuse=True)


def attention(nc, x_in, w_attn, b_attn, w_proj, b_proj, parts_dram, x_out):
    start = Plan(attention_start(), SLOT_USER, SLOTS)
    turn = Plan(attention_turn(True), SLOT_USER, SLOTS)
    last_turn = Plan(attention_turn(False), SLOT_USER, SLOTS)
    with ExitStack() as ctx:
        def sb(name, shape, dt=F32):
            return ctx.enter_context(nc.sbuf_tensor("at_" + name, shape, dt))

        sem = ctx.enter_context(semaphores(nc, "at_"))

        slot = [ctx.enter_context(nc.psum_tensor(f"at_slot{s}", [P, 2 * BANK], F32)) for s in range(SLOTS)]
        values = ctx.enter_context(nc.psum_tensor("at_values", [P, T], F32))

        w_qkv = sb("w_qkv", [P, KC, 3 * C])
        w_o = sb("w_o", [P, KC, C])
        bias_qk = sb("bias_qk", [P, 2 * KC])
        bias_v = sb("bias_v", [P, C])
        bias_o = sb("bias_o", [P, C])
        ident = sb("ident", [P, P])
        ident_bf = sb("ident_bf", [P, P], BF16)
        mask_q = sb("mask_q", [P, P], BF16)
        mask_k = sb("mask_k", [P, P], BF16)
        x = sb("x", [P, TILES, C])
        x_kept = sb("x_kept", [P, TILES, C])
        o_rows = sb("o_rows", [P, TILES, C])
        stats = sb("stats", [P, TILES, 6])
        mean_var = sb("mean_var", [P, TILES, 2])
        std = sb("std", [P, TILES])
        rstd = sb("rstd", [P, TILES])
        turned = sb("turned", [P, KC, T])
        turned_o = sb("turned_o", [P, KC, T])
        qk = sb("qk", [P, 2, T])
        rest = sb("rest", [P, 2, T])
        parts = sb("parts", [P, 2, 3, T], BF16)
        q_stack = sb("q_stack", [P, HEADS, T], BF16)
        k_stack = sb("k_stack", [P, HEADS, T], BF16)
        v_rows = sb("v_rows", [P, TILES, HEADS, PAD])
        neg_max = sb("neg_max", [P, TILES, HEADS])
        max_rest = sb("max_rest", [P, TILES, GROUP])
        max_part = sb("max_part", [P, TILES, 3, GROUP], BF16)
        max_rows = sb("max_rows", [3 * GROUP, T], BF16)
        NPROB = 2 * GROUP
        prob = sb("prob", [P, NPROB, T])
        out_t = sb("out_t", [P, T])
        inv_sum = sb("inv_sum", [P, TILES, GROUP])

        consts = sem("consts")
        w_in = sem("w_in")
        bias_ready = sem("bias_ready")
        x_loaded = sem("x_loaded")
        x_kept_in = sem("x_kept_in")
        start_chain = sem("start_chain")
        heads_chain = sem("heads_chain")
        max_chain = sem("max_chain")
        var_ready = sem("var_ready")
        std_ready = sem("std_ready")
        xn_ready = sem("xn_ready")
        with_bias = sem("with_bias")
        filled = [sem(f"filled{s}") for s in range(SLOTS)]
        emptied = [sem(f"emptied{s}") for s in range(SLOTS)]
        qk_ready = sem("qk_ready")
        rest_ready = sem("rest_ready")
        part2_ready = sem("part2_ready")
        part3_ready = sem("part3_ready")
        parts_out = [sem(f"parts_out{k}") for k in range(2)]
        stacked = [sem(f"stacked{k}") for k in range(2)]
        max_ready = sem("max_ready")
        max_stacked = sem("max_stacked")
        prob_used = sem("prob_used")
        out_t_ready = sem("out_t_ready")
        stored = sem("stored")

        ctx.enter_context(nc.allow_non_contiguous_dma(reason="bias columns"))
        nc.all_engine_barrier()
        block = ctx.enter_context(nc.Block())
        STACK_DMAS = 2 * 6

        def counts(plan, before):
            return Slots(plan, before, filled, emptied)

        def run(eng, part):
            part(counts(start, [0] * SLOTS), None, 0)
            with eng.Fori(0, BATCH - 1) as b:
                part(counts(turn, [start.uses[s] + b * turn.uses[s] for s in range(SLOTS)]), b, b + 1)
            part(counts(last_turn, [start.uses[s] + (BATCH - 1) * turn.uses[s] for s in range(SLOTS)]),
                 BATCH - 1, None)

        @block.gpsimd
        def _(pool):
            own = Tally(pool, consts)
            own.up(pool.memset(ident[:], 0.0))
            own.up(pool.memset(mask_q[:], 0.0))
            own.up(pool.memset(mask_k[:], 0.0))
            own.up(pool.memset(v_rows[:], 0.0))
            own.up(pool.memset(k_stack[:], 1.0))
            own.done()
            own.up(pool.affine_select(out=ident[:], in_=ident[:], compare_op=ALU.not_equal, fill=1.0, base=0,
                                      pattern=[[-1, P]], channel_multiplier=1))
            own.up(pool.affine_select(out=mask_q[:], in_=mask_q[:], compare_op=ALU.is_ge, fill=MASKED, base=0,
                                      pattern=[[-1, P]], channel_multiplier=1))
            own.up(pool.affine_select(out=mask_k[:], in_=mask_k[:], compare_op=ALU.is_ge, fill=MASKED, base=0,
                                      pattern=[[1, P]], channel_multiplier=-1))
            own.up(pool.memset(v_rows[:, :, :, D], 1.0))
            own.done()
            own.up(pool.tensor_copy(ident_bf[:], ident[:]))
            assert own.n == 10
            pool.wait_ge(w_in, 1 + 16 * 5)

            def part(slots, b, f):
                for stage, what, s, use in slots.plan.jobs:
                    if stage.lstrip("+") == "split":
                        pool.wait_ge(rest_ready, 1 + f * 4 + what + 1)
                        pool.nop(nofuse=True)
                        pool.tensor_copy(parts[:, what % 2, 1, :], rest[:, what % 2, :]).then_inc(part2_ready, 1)
                    elif stage == "copy_out" and what == 0:
                        pool.wait_ge(x_kept_in, 1 + (b + 1) * 16)
                        pool.tensor_tensor(x_kept[:], x_kept[:],
                                           bias_o[:].unsqueeze(1).broadcast_to([P, TILES, C]), ALU.add)\
                            .then_inc(with_bias, 1)

            run(pool, part)

        @block.sync
        def _(sp):
            sp.dma_start(w_qkv[:], w_attn.rearrange("(k p) n -> p k n", p=P)).then_inc(w_in, 16)
            sp.dma_start(w_o[:], w_proj.rearrange("(k p) n -> p k n", p=P)).then_inc(w_in, 16)
            sp.dma_start(bias_qk[:], b_attn[0:2 * C].rearrange("(k p) -> p k", p=P)).then_inc(w_in, 16)
            sp.dma_start(bias_v[:], spread(b_attn[2 * C:3 * C])).then_inc(w_in, 16)
            sp.dma_start(bias_o[:], spread(b_proj)).then_inc(w_in, 16)
            sp.wait_ge(consts, 1 + 5)

            def rows(ap, b, first=0, n=TILES):
                return ap[bass.ds(b * TILES + first, n)].rearrange("n p c -> p n c")

            def load_stack(f, half):
                for k in range(2):
                    sp.wait_ge(parts_out[k], 1 + 16 * (f * 2 + half + 1))
                    sp.nop(nofuse=True)
                for stack, oc, order in ((q_stack, half, (0, 0, 0, 1, 1, 2)), (k_stack, KC + half, (0, 1, 2, 0, 1, 0))):
                    for blk, k in enumerate(order):
                        sp.dma_start(stack[blk * D:(blk + 1) * D, half * HALF_HEADS:(half + 1) * HALF_HEADS, :],
                                     parts_dram[oc, k].rearrange("(h d) t -> d h t", d=D)).then_inc(stacked[half], 16)

            def store_parts(f, n):
                sp.wait_ge(part3_ready, 1 + f * 4 + n + 1)
                sp.nop(nofuse=True)
                sp.wait_ge(stacked[n // 2], 1 + f * 16 * STACK_DMAS)
                sp.nop(nofuse=True)
                sp.dma_start(parts_dram[QK_ORDER[n]].rearrange("k p t -> p k t"), parts[:, n % 2, :, :])\
                  .then_inc(parts_out[n % 2], 16)

            def part(slots, b, f):
                if b is not None:
                    sp.wait_ge(stored, 1 + b * 32)
                    sp.nop(nofuse=True)
                    sp.dma_start(x_kept[:], rows(x_in, b)).then_inc(x_kept_in, 16)
                if f is not None:
                    if b is not None:
                        sp.wait_ge(part2_ready, 1 + f * 4)
                        sp.nop(nofuse=True)
                    sp.dma_start(x[:], rows(x_in, f)).then_inc(x_loaded, 16)
                    for n in range(2):
                        store_parts(f, n)
                    if b is not None:
                        slots.wait_read(sp, *[("weights", (h, TILES - 1)) for h in range(GROUP, 2 * GROUP)], alone=True)
                    load_stack(f, 0)
                    for n in range(2, 4):
                        store_parts(f, n)
                    if b is not None:
                        slots.wait_read(sp, *[("weights", (h, TILES - 1)) for h in range(HEADS - GROUP, HEADS)],
                                        alone=True)
                    load_stack(f, 1)
                if b is not None:
                    for half in range(2):
                        slots.wait_read(sp, ("project_o", half), alone=True)
                        sp.dma_start(rows(x_out, b, half * HALF_TILES, HALF_TILES),
                                     x_kept[:, half * HALF_TILES:(half + 1) * HALF_TILES, :]).then_inc(stored, 16)

            run(sp, part)
            sp.wait_ge(stored, 1 + 16 * 2 * BATCH)

        @block.tensor
        def _(pe):
            pe.wait_ge(consts, 1 + 10)
            pe.wait_ge(w_in, 1 + 16 * 5)

            def part(slots, b, f):
                for full_stage, what, s, use in slots.plan.jobs:
                    stage = full_stage.lstrip("+")
                    q = f if full_stage != stage or b is None else b
                    if s is not None:
                        ps = slot[s]
                        slots.wait_empty(pe, s, use)
                    if stage == "turn_x":
                        if what == 0:
                            pe.wait_ge(xn_ready, 1 + (q + 1) * TILES)
                        for t in range(TILES):
                            last = pe.transpose(ps[:, t * P:(t + 1) * P], x[:, t, what * P:(what + 1) * P], ident[:])
                    elif stage == "project_qk":
                        if what == 0:
                            mark = full_stage[:-len(stage)]
                            slots.wait_read(pe, (mark + "turn_x", 0), (mark + "turn_x", 1))
                        oc = QK_ORDER[what]
                        for half in range(2):
                            for k in range(KC):
                                last = pe.matmul(ps[:, half * BANK:(half + 1) * BANK],
                                                 w_qkv[:, k, oc * P:(oc + 1) * P],
                                                 turned[:, k, half * BANK:(half + 1) * BANK],
                                                 start=(k == 0), stop=(k == KC - 1))
                    elif stage == "project_v":
                        for n in range(HALF_TILES):
                            t = HALF_TILES * what + n
                            for k in range(KC):
                                last = pe.matmul(ps[:, n * C:(n + 1) * C], turned[:, k, t * P:(t + 1) * P],
                                                 w_qkv[:, k, 2 * C:3 * C], start=(k == 0), stop=(k == KC - 1))
                    elif stage == "maxima":
                        h, qt = what
                        if h % HALF_HEADS == 0 and qt == 0:
                            pe.wait_ge(stacked[h // HALF_HEADS], 1 + (q + 1) * 16 * STACK_DMAS)
                        keys = (qt + 1) * P
                        for k0 in range(0, keys, BANK):
                            k1 = min(k0 + BANK, keys)
                            pe.matmul(ps[:, k0:k1], q_stack[0:6 * D, h, qt * P:(qt + 1) * P],
                                      k_stack[0:6 * D, h, k0:k1], start=True, stop=True)
                        last = pe.matmul(ps[:, keys - P:keys], ident_bf[:], mask_q[:], start=False, stop=True,
                                         skip_group_check=True)
                    elif stage == "turn_max":
                        pe.wait_ge(max_ready, 1 + q * GROUPS + what + 1)
                        rows = ps[:].bitcast(BF16)
                        for t in range(TILES):
                            last = pe.transpose(rows[0:3 * GROUP, t * P:(t + 1) * P],
                                                max_part[:, t, :, :].rearrange("p k g -> p (k g)"), ident_bf[:])
                    elif stage == "weights":
                        h, kt = what
                        if (h % GROUP, kt) == (0, 0):
                            pe.wait_ge(max_stacked, 1 + (q * GROUPS + h // GROUP + 1) * 48)
                        q_from = kt * P
                        for q0 in range(0, T, BANK):
                            if q0 + BANK <= q_from:
                                continue
                            lo = max(q0, q_from)
                            last = pe.matmul(ps[:, lo:q0 + BANK], k_stack[0:6 * D + 3, h, kt * P:(kt + 1) * P],
                                             q_stack[0:6 * D + 3, h, lo:q0 + BANK], start=True, stop=True)
                            if lo == q_from:
                                last = pe.matmul(ps[:, lo:lo + P], ident_bf[:], mask_k[:], start=False, stop=True,
                                                 skip_group_check=True)
                    elif stage == "values":
                        g, kt = what
                        slots.wait_read(pe, *[("weights", (GROUP * g + j, kt)) for j in range(GROUP)])
                        if kt == 0:
                            pe.wait_ge(out_t_ready, 1 + q * GROUPS + g)
                        for q0 in range(0, T, BANK):
                            q1 = q0 + BANK
                            if q1 <= kt * P:
                                continue
                            lo = max(q0, kt * P)
                            for j in range(GROUP):
                                n = (g * TILES + kt) * GROUP + j
                                last = pe.matmul(values[PAD * j:PAD * j + PAD, lo:q1],
                                                 v_rows[:, kt, GROUP * g + j, :], prob[:, n % NPROB, lo:q1],
                                                 start=(kt == 0), stop=(q1 == (kt + 1) * P),
                                                 tile_position=(0, PAD * j))
                        last.then_inc(prob_used, 1)
                    elif stage == "turn_out":
                        pe.wait_ge(out_t_ready, 1 + q * GROUPS + what + 1)
                        for t in range(TILES):
                            last = pe.transpose(ps[:, t * P:(t + 1) * P], out_t[:, t * P:(t + 1) * P], ident[:])
                    elif stage == "turn_o":
                        if what == 0:
                            slots.wait_read(pe, *[("turn_out", g) for g in range(GROUPS)])
                        for t in range(TILES):
                            last = pe.transpose(ps[:, t * P:(t + 1) * P], o_rows[:, t, what * P:(what + 1) * P],
                                                ident[:])
                    elif stage == "project_o":
                        if what == 0:
                            slots.wait_read(pe, ("turn_o", 0), ("turn_o", 1))
                        for n in range(HALF_TILES):
                            t = HALF_TILES * what + n
                            for k in range(KC):
                                last = pe.matmul(ps[:, n * C:(n + 1) * C], turned_o[:, k, t * P:(t + 1) * P],
                                                 w_o[:, k, :], start=(k == 0), stop=(k == KC - 1))
                    if s is not None:
                        last.then_inc(filled[s], 1)

            run(pe, part)

        @block.scalar
        def _(act):
            act.wait_ge(w_in, 1 + 16 * 5)
            act.wait_ge(consts, 1 + 10)
            act.activation(bias_qk[:, 0:KC], bias_qk[:, 0:KC], ACT.Copy, scale=D ** -0.5).then_inc(bias_ready, 1)
            act.wait_ge(bias_ready, 1 + 1)

            def part(slots, b, f):
                for full_stage, what, s, use in slots.plan.jobs:
                    stage = full_stage.lstrip("+")
                    q = f if full_stage != stage or b is None else b
                    if stage == "normalise":
                        act.wait_ge(var_ready, 1 + q + 1)
                        act.activation(std[:], mean_var[:, :, 1], ACT.Sqrt).then_inc(std_ready, 1)
                    elif stage == "copy_out":
                        act.wait_ge(prob_used, 1 + (q * GROUPS + what + 1) * TILES)
                        if what:
                            slots.wait_read(act, ("turn_out", what - 1))
                        act.activation(out_t[:], values[:], ACT.Copy).then_inc(out_t_ready, 1)
                    if SLOT_USER.get(stage) != "act":
                        continue
                    ps = slot[s]
                    slots.wait_filled(act, s, use)
                    if stage in ("turn_x", "turn_o"):
                        dst = turned if stage == "turn_x" else turned_o
                        act.activation(dst[:, what, :], ps[:], ACT.Copy).then_inc(emptied[s], 1)
                    elif stage == "project_qk":
                        k, oc = what % 2, QK_ORDER[what]
                        act.wait_ge(parts_out[k], 1 + 16 * (q * 2 + what // 2))
                        act.activation(qk[:, k, :], ps[:], ACT.Identity, bias=bias_qk[:, oc:oc + 1],
                                       scale=D ** -0.5 if oc < KC else 1.0).then_inc(emptied[s], 1)
                        slots.wait_read(act, (full_stage, what))
                        act.activation(parts[:, k, 0, :], qk[:, k, :], ACT.Copy).then_inc(qk_ready, 1)
                    elif stage == "turn_max":
                        act.wait_ge(max_stacked, 1 + (q * GROUPS + what) * 48)
                        act.activation(max_rows[:], ps[:].bitcast(BF16)[0:3 * GROUP, 0:T], ACT.Copy)\
                           .then_inc(emptied[s], 1)
                        slots.wait_read(act, (full_stage, what))
                        for k in range(3):
                            act.dma_start(q_stack[6 * D + k:6 * D + k + 1, GROUP * what:GROUP * what + GROUP, :],
                                          max_rows[GROUP * k:GROUP * k + GROUP, :]).then_inc(max_stacked, 16)
                    elif stage == "weights":
                        h, kt = what
                        n = ((h // GROUP) * TILES + kt) * GROUP + h % GROUP
                        if n % GROUP == 0:
                            act.wait_ge(prob_used, 1 + q * GROUPS * TILES + max(n // GROUP - 1, 0))
                        act.activation(prob[:, n % NPROB, kt * P:T], ps[:, kt * P:T], ACT.Exp).then_inc(emptied[s], 1)

            run(act, part)

        @block.vector
        def _(dve):
            dve.wait_ge(consts, 1 + 10)
            dve.wait_ge(w_in, 1 + 16 * 5)
            START = 2 * TILES + 1

            def part(slots, b, f):
                in_start = Tally(dve, start_chain, 0 if f is None else f * START)
                in_heads = Tally(dve, heads_chain, 0 if b is None else b * GROUPS)
                for full_stage, what, s, use in slots.plan.jobs:
                    stage = full_stage.lstrip("+")
                    mark = full_stage[:-len(stage)]
                    q = f if full_stage != stage or b is None else b
                    if stage == "normalise":
                        dve.wait_ge(x_loaded, 1 + (q + 1) * 16)
                        for t in range(TILES):
                            in_start.up(dve.bn_stats(stats[:, t, :], x[:, t, :]))
                        in_start.done()
                        dve.nop(nofuse=True)
                        for t in range(TILES):
                            in_start.up(dve.bn_aggr(mean_var[:, t, :], stats[:, t, :]))
                        in_start.done()
                        dve.tensor_scalar(mean_var[:, :, 1], mean_var[:, :, 1], LN_EPS, None, ALU.add)\
                           .then_inc(var_ready, 1)
                        dve.wait_ge(std_ready, 1 + q + 1)
                        in_start.link(dve.reciprocal(rstd[:], std[:]))
                        for t in range(TILES):
                            dve.tensor_scalar(x[:, t, :], x[:, t, :], mean_var[:, t, 0:1], rstd[:, t:t + 1],
                                              ALU.subtract, ALU.mult).then_inc(xn_ready, 1)
                    elif stage == "split":
                        k = what % 2
                        dve.wait_ge(qk_ready, 1 + q * 4 + what + 1)
                        dve.tensor_tensor(rest[:, k, :], qk[:, k, :], parts[:, k, 0, :], ALU.subtract)\
                           .then_inc(rest_ready, 1)
                    elif stage == "third_part":
                        k = what % 2
                        dve.wait_ge(part2_ready, 1 + q * 4 + what + 1)
                        dve.tensor_tensor(parts[:, k, 2, :], rest[:, k, :], parts[:, k, 1, :], ALU.subtract)\
                           .then_inc(part3_ready, 1)
                    elif stage == "turn_max":
                        heads = slice(GROUP * what, GROUP * what + GROUP)
                        own = Tally(dve, max_chain, (q * GROUPS + what) * 3)
                        slots.wait_read(dve, *[(mark + "maxima", (h, TILES - 1)) for h in range(heads.start, heads.stop)])
                        dve.wait_ge(max_stacked, 1 + (q * GROUPS + what) * 48)
                        own.link(dve.tensor_copy(max_part[:, :, 0, :], neg_max[:, :, heads]))
                        own.link(dve.tensor_tensor(max_rest[:], neg_max[:, :, heads], max_part[:, :, 0, :],
                                                   ALU.subtract))
                        own.link(dve.tensor_copy(max_part[:, :, 1, :], max_rest[:]))
                        dve.tensor_tensor(max_part[:, :, 2, :], max_rest[:], max_part[:, :, 1, :],
                                          ALU.subtract).then_inc(max_ready, 1)
                    if SLOT_USER.get(stage) != "dve":
                        continue
                    ps = slot[s]
                    slots.wait_filled(dve, s, use)
                    if stage == "project_v":
                        if b is not None:
                            dve.wait_ge(prob_used, 1 + (b + 1) * GROUPS * TILES)
                        for n in range(HALF_TILES):
                            v_chunk = dve.tensor_tensor(
                                v_rows[:, HALF_TILES * what + n, :, 0:D],
                                ps[:, n * C:(n + 1) * C].rearrange("p (h d) -> p h d", d=D),
                                bias_v[:].rearrange("p (h d) -> p h d", d=D), ALU.add)
                        v_chunk.then_inc(emptied[s], 1)
                    elif stage == "maxima":
                        h, qt = what
                        dve.tensor_reduce(neg_max[:, qt, h:h + 1], ps[:, 0:(qt + 1) * P], AX.X, ALU.max, negate=True)\
                           .then_inc(emptied[s], 1)
                    elif stage == "turn_out":
                        rows = ps[:].rearrange("p (t h d) -> p t h d", t=TILES, d=PAD)
                        in_heads.link(dve.reciprocal(inv_sum[:], rows[:, :, :, D]))
                        dve.tensor_tensor(
                            o_rows[:].rearrange("p t (h d) -> p t h d", d=D)[:, :, GROUP * what:GROUP * what + GROUP, :],
                            rows[:, :, :, 0:D], inv_sum[:].unsqueeze(3).broadcast_to([P, TILES, GROUP, D]),
                            ALU.mult).then_inc(emptied[s], 1)
                    elif stage == "project_o":
                        dve.wait_ge(with_bias, 1 + b + 1)
                        tiles_of = x_kept[:, HALF_TILES * what:HALF_TILES * (what + 1), :]
                        dve.tensor_tensor(tiles_of, ps[:].rearrange("p (n c) -> p n c", c=C), tiles_of, ALU.add)\
                           .then_inc(emptied[s], 1)

            run(dve, part)


EXPERTS, HIDDEN, CAPACITY = 8, 1024, 512
KEPT = EXPERTS * CAPACITY
HC = HIDDEN // P
ST = CAPACITY // P


def mixture(nc, n, x_in, gate_w, gamma, beta, w_in, w_out, slots_dram, results_dram, x_out, clear_slots):
    with ExitStack() as outer:
        def sb(name, shape, dt=F32, ctx=outer):
            return ctx.enter_context(nc.sbuf_tensor(f"f{n}_{name}", shape, dt))

        def psum(ctx, name, shape, dt=F32):
            return ctx.enter_context(nc.psum_tensor(f"f{n}_{name}", shape, dt))

        sem = outer.enter_context(semaphores(nc, f"f{n}_"))

        outer.enter_context(nc.allow_non_contiguous_dma(reason="gate weights by channel"))
        base = sb("base", [P, NT, C])
        weight = sb("weight", [P, NT])
        fetch_at = sb("fetch_at", [P, NT], I32)
        send_to = sb("send_to", [P, NT], I32)
        ident = sb("ident", [P, P])
        up_w = [sb(f"up_w{k}", [P, KC, HIDDEN]) for k in range(2)]
        down_w = [sb(f"down_w{k}", [P, HC, C]) for k in range(2)]
        consts = sem("consts")
        weights_in = [sem(f"weights_in{k}") for k in range(2)]

        def load_weights(eng, e, k):
            eng.dma_start(up_w[k][:], w_in[bass.ds(e, 1)].rearrange("a (k p) n -> (a p) k n", p=P))\
               .then_inc(weights_in[k], 16)
            eng.dma_start(down_w[k][:], w_out[bass.ds(e, 1)].rearrange("a (k p) n -> (a p) k n", p=P))\
               .then_inc(weights_in[k], 16)

        with ExitStack() as ctx:
            tokens = sb("tokens", [P, NT, C], ctx=ctx)
            u = sb("u", [P, TILES, C], ctx=ctx)
            tok = [sb(f"tok{j}", [P, TILES, C], ctx=ctx) for j in range(2)]
            turned = sb("turned", [P, KC, T], ctx=ctx)
            gate = sb("gate", [P, KC, EXPERTS], ctx=ctx)
            gamma_b = sb("gamma_b", [P, C], ctx=ctx)
            beta_b = sb("beta_b", [P, C], ctx=ctx)
            stats = sb("stats", [P, TILES, 6], ctx=ctx)
            mean_var = sb("mean_var", [P, 2, TILES, 2], ctx=ctx)
            std = sb("std", [P, 2, TILES], ctx=ctx)
            rstd = sb("rstd", [P, 2, TILES], ctx=ctx)
            logits = sb("logits", [P, NT, EXPERTS], ctx=ctx)
            before = sb("before", [P, P], ctx=ctx)
            ones = sb("ones", [P, P], ctx=ctx)
            order = sb("order", [P, EXPERTS], ctx=ctx)
            onehot = sb("onehot", [P, NT, EXPERTS], ctx=ctx)
            work = sb("work", [P, NT, EXPERTS], ctx=ctx)
            tops = sb("tops", [P, NT], ctx=ctx)
            first = sb("first", [P, NT], ctx=ctx)
            total = sb("total", [P, NT], ctx=ctx)
            rank = sb("rank", [P, NT], ctx=ctx)
            keep = sb("keep", [P, NT], ctx=ctx)
            place = sb("place", [P, NT], ctx=ctx)
            totals = sb("totals", [P, NT, EXPERTS], ctx=ctx)
            zeros = totals[:].rearrange("p t e -> p (t e)")
            zero_rows = P * NT * EXPERTS // C
            earlier = u[:, 0:NT * EXPERTS // C, :].rearrange("p n (t e) -> p (n t) e", e=EXPERTS)
            ps_turn = [psum(ctx, f"turn{k}", [P, T]) for k in range(KC)]
            ps_gate = psum(ctx, "ps_gate", [P, TILES * EXPERTS])
            ps_before = psum(ctx, "ps_before", [P, NT * EXPERTS])
            ps_total = psum(ctx, "ps_total", [P, NT * EXPERTS])

            x_loaded = sem("x_loaded")
            loaded = sem("loaded")
            cleared = sem("cleared")
            chain = sem("chain")
            var_ready = sem("var_ready")
            std_ready = sem("std_ready")
            scaled = sem("scaled")
            tok_ready = sem("tok_ready")
            base_ready = sem("base_ready")
            turn_ready = sem("turn_ready")
            turned_ready = sem("turned_ready")
            kept = sem("kept")
            gate_ready = sem("gate_ready")
            logits_ready = sem("logits_ready")
            shifted = sem("shifted")
            exp_ready = sem("exp_ready")
            onehot_ready = sem("onehot_ready")
            counts_ready = sem("counts_ready")
            routed = sem("routed")
            sent = sem("sent", start=0)

            nc.all_engine_barrier()
            block = ctx.enter_context(nc.Block())

            @block.sync
            def _(sp):
                for k in range(KC):
                    sp.dma_start(gate[:, k, :], gate_w[:, k * P:(k + 1) * P].rearrange("e p -> p e")).then_inc(loaded, 16)
                sp.dma_start(gamma_b[:], spread(gamma)).then_inc(loaded, 16)
                sp.dma_start(beta_b[:], spread(beta)).then_inc(loaded, 16)
                with sp.Fori(0, BATCH) as b:
                    sp.wait_ge(x_loaded, 1 + b * 16)
                    sp.nop(nofuse=True)
                    sp.dma_start(base[:, bass.ds(b * TILES, TILES), :],
                                 x_in[bass.ds(b * TILES, TILES)].rearrange("n p c -> p n c")).then_inc(x_loaded, 16)
                if clear_slots:
                    sp.wait_ge(consts, 1 + 1)
                    sp.nop(nofuse=True)
                    for k in range(KEPT // zero_rows):
                        sp.dma_start(slots_dram[k * zero_rows:(k + 1) * zero_rows, :]
                                     .rearrange("(p r) c -> p (r c)", p=P), zeros).then_inc(cleared, 16)
                for k in range(2):
                    load_weights(sp, k, k)

            TURN = 2 * (3 * TILES + 1)

            def sequences(eng, first, part):
                with eng.Fori(0, (BATCH - first) // 2) as i:
                    for j in range(2):
                        part(first + i * 2 + j, (first + j) % 2)
                if (BATCH - first) % 2:
                    part(BATCH - 1, (BATCH - 1) % 2)

            @block.gpsimd
            def _(pool):
                own = Tally(pool, consts)
                own.up(pool.memset(zeros, 0.0))
                own.up(pool.memset(ident[:], 0.0))
                own.up(pool.memset(before[:], 1.0))
                own.up(pool.memset(ones[:], 1.0))
                own.up(pool.iota(fetch_at[:, 0:EXPERTS], pattern=[[-1, EXPERTS]], base=EXPERTS, channel_multiplier=0))
                own.done()
                own.up(pool.affine_select(out=ident[:], in_=ident[:], compare_op=ALU.not_equal, fill=1.0, base=0,
                                          pattern=[[-1, P]], channel_multiplier=1))
                own.up(pool.affine_select(out=before[:], in_=before[:], compare_op=ALU.is_gt, fill=0.0, base=0,
                                          pattern=[[1, P]], channel_multiplier=-1))
                own.up(pool.tensor_copy(order[:], fetch_at[:, 0:EXPERTS]))
                own.done()
                assert own.n == 8
                pool.wait_ge(loaded, 1 + 64)
                beta_wide = beta_b[:].unsqueeze(1).broadcast_to([P, TILES, C])

                def shift(b, j):
                    span = base[:, bass.ds(b * TILES, TILES), :]
                    pool.wait_ge(chain, 1 + b * TURN + TURN // 2)
                    pool.tensor_tensor(span, span, u[:], ALU.add).then_inc(base_ready, 1)
                    pool.wait_ge(scaled, 1 + b + 1)
                    pool.tensor_tensor(tok[j][:], tok[j][:], beta_wide, ALU.add).then_inc(tok_ready, 1)

                sequences(pool, 0, shift)
                pool.wait_ge(routed, 1 + 1)
                pool.wait_ge(kept, 1 + BATCH)
                for t in range(NT):
                    pool.indirect_dma_start(
                        out=slots_dram, out_offset=bass.IndirectOffsetOnAxis(ap=send_to[:, t:t + 1].bitcast(U32), axis=0),
                        in_=tokens[:, t, :], in_offset=None, bounds_check=KEPT - 1, oob_is_err=False)\
                        .then_inc(sent, 16)
                pool.wait_ge(sent, 16 * NT)

            @block.tensor
            def _(pe):
                pe.wait_ge(consts, 1 + 8)
                pe.wait_ge(loaded, 1 + 64)

                def gate_logits(b, j):
                    pe.wait_ge(tok_ready, 1 + b + 1)
                    pe.wait_ge(turned_ready, 1 + b * KC)
                    for k in range(KC):
                        for t in range(TILES):
                            last = pe.transpose(ps_turn[k][:, t * P:(t + 1) * P], tok[j][:, t, k * P:(k + 1) * P],
                                                ident[:])
                        last.then_inc(turn_ready, 1)
                    pe.wait_ge(turned_ready, 1 + b * KC + KC)
                    pe.wait_ge(logits_ready, 1 + b)
                    for t in range(TILES):
                        for k in range(KC):
                            last = pe.matmul(ps_gate[:, t * EXPERTS:(t + 1) * EXPERTS],
                                             turned[:, k, t * P:(t + 1) * P], gate[:, k, :],
                                             start=(k == 0), stop=(k == KC - 1))
                    last.then_inc(gate_ready, 1)

                sequences(pe, 0, gate_logits)
                pe.wait_ge(onehot_ready, 1 + 1)
                chosen = onehot[:].rearrange("p t e -> p (t e)")
                pe.matmul(ps_before[:], before[:], chosen, start=True, stop=True)
                pe.matmul(ps_total[:], ones[:], chosen, start=True, stop=True).then_inc(counts_ready, 1)

            @block.scalar
            def _(act):
                def root(b, k):
                    act.wait_ge(var_ready, 1 + b * 2 + k + 1)
                    act.activation(std[:, k, :], mean_var[:, k, :, 1], ACT.Sqrt).then_inc(std_ready, 1)

                def keep_tokens(b, j):
                    act.wait_ge(gate_ready, 1 + b)
                    for k in range(KC):
                        act.wait_ge(turn_ready, 1 + b * KC + k + 1)
                        act.activation(turned[:, k, :], ps_turn[k][:], ACT.Copy).then_inc(turned_ready, 1)
                    act.activation(tokens[:, bass.ds(b * TILES, TILES), :], tok[j][:], ACT.Copy).then_inc(kept, 1)

                root(0, 0)
                root(0, 1)

                def part(b, j):
                    root(b, 0)
                    root(b, 1)
                    keep_tokens(b - 1, 1 - j)

                sequences(act, 1, part)
                keep_tokens(BATCH - 1, (BATCH - 1) % 2)
                act.wait_ge(shifted, 1 + 1)
                act.activation(work[:], work[:], ACT.Exp).then_inc(exp_ready, 1)

            @block.vector
            def _(dve):
                dve.wait_ge(consts, 1 + 8)
                dve.wait_ge(loaded, 1 + 64)
                gamma_wide = gamma_b[:].unsqueeze(1).broadcast_to([P, TILES, C])

                def normalise(own, b, j, k):
                    def src(t):
                        return u[:, t, :] if k else base[:, bass.ds(b * TILES + t, 1), :].rearrange("p a c -> p (a c)")

                    if k == 0:
                        dve.wait_ge(x_loaded, 1 + (b + 1) * 16)
                    for t in range(TILES):
                        own.up(dve.bn_stats(stats[:, t, :], src(t)))
                    own.done()
                    dve.nop(nofuse=True)
                    for t in range(TILES):
                        own.up(dve.bn_aggr(mean_var[:, k, t, :], stats[:, t, :]))
                    own.done()
                    dve.tensor_scalar(mean_var[:, k, :, 1], mean_var[:, k, :, 1], LN_EPS, None, ALU.add)\
                       .then_inc(var_ready, 1)
                    dve.wait_ge(std_ready, 1 + b * 2 + k + 1)
                    own.link(dve.reciprocal(rstd[:, k, :], std[:, k, :]))
                    if k == 0:
                        dve.wait_ge(base_ready, 1 + b)
                    elif not (isinstance(b, int) and b < 2):
                        dve.wait_ge(kept, 1 + b - 1)
                        dve.wait_ge(turn_ready, 1 + (b - 1) * KC)
                    for t in range(TILES):
                        own.up(dve.tensor_scalar((tok[j] if k else u)[:, t, :], src(t), mean_var[:, k, t, 0:1],
                                                 rstd[:, k, t:t + 1], ALU.subtract, ALU.mult))
                    own.done()
                    if k:
                        dve.tensor_tensor(tok[j][:], tok[j][:], gamma_wide, ALU.mult).then_inc(scaled, 1)

                def take_logits(b):
                    dve.wait_ge(gate_ready, 1 + b + 1)
                    dve.tensor_copy(logits[:, bass.ds(b * TILES, TILES), :],
                                    ps_gate[:].rearrange("p (t e) -> p t e", e=EXPERTS)).then_inc(logits_ready, 1)

                own = Tally(dve, chain)
                normalise(own, 0, 0, 0)
                normalise(own, 0, 0, 1)

                def part(b, j):
                    own = Tally(dve, chain, b * TURN)
                    normalise(own, b, j, 0)
                    normalise(own, b, j, 1)
                    take_logits(b - 1)
                    assert own.n == TURN, own.n

                sequences(dve, 1, part)
                take_logits(BATCH - 1)
                own = Tally(dve, chain, BATCH * TURN)
                wide = [P, NT, EXPERTS]
                dve.wait_ge(logits_ready, 1 + BATCH)
                own.link(dve.tensor_reduce(tops[:], logits[:], AX.X, ALU.max))
                tops_wide = tops[:].unsqueeze(2).broadcast_to(wide)
                dve.tensor_tensor(work[:], logits[:], tops_wide, ALU.subtract).then_inc(shifted, 1)
                own.link(dve.tensor_tensor(onehot[:], logits[:], tops_wide, ALU.is_equal))
                own.link(dve.tensor_tensor(onehot[:], onehot[:], order[:].unsqueeze(1).broadcast_to(wide), ALU.mult))
                own.link(dve.tensor_reduce(first[:], onehot[:], AX.X, ALU.max))
                dve.tensor_tensor(onehot[:], onehot[:], first[:].unsqueeze(2).broadcast_to(wide), ALU.is_equal)\
                   .then_inc(onehot_ready, 1)
                dve.wait_ge(exp_ready, 1 + 1)
                own.link(dve.tensor_reduce(total[:], work[:], AX.X, ALU.add))
                own.link(dve.reciprocal(weight[:], total[:]))
                dve.wait_ge(counts_ready, 1 + 1)
                if clear_slots:
                    dve.wait_ge(cleared, 1 + KEPT // zero_rows * 16)
                own.link(dve.tensor_copy(totals[:], ps_total[:].rearrange("p (t e) -> p t e", e=EXPERTS)))
                dve.wait_ge(base_ready, 1 + BATCH)
                for e in range(EXPERTS):
                    own.up(dve.tensor_tensor_scan(earlier[:, :, e], ones[:, 0:NT], totals[:, :, e], 0.0,
                                                  ALU.mult, ALU.add))
                own.done()
                own.link(dve.tensor_tensor(earlier, earlier, totals[:], ALU.subtract))
                own.link(dve.tensor_tensor(earlier, earlier, ps_before[:].rearrange("p (t e) -> p t e", e=EXPERTS),
                                           ALU.add))
                dve.wait_ge(onehot_ready, 1 + 1)
                own.link(dve.tensor_tensor(earlier, earlier, onehot[:], ALU.mult))
                own.link(dve.tensor_reduce(rank[:], earlier, AX.X, ALU.add))
                own.link(dve.tensor_scalar(keep[:], rank[:], float(CAPACITY), None, ALU.is_lt))
                own.link(dve.tensor_scalar(place[:], first[:], -float(CAPACITY), float(EXPERTS * CAPACITY), ALU.mult, ALU.add))
                own.link(dve.tensor_tensor(place[:], place[:], rank[:], ALU.add))
                own.link(dve.tensor_tensor(place[:], place[:], keep[:], ALU.mult))
                own.link(dve.tensor_tensor(weight[:], weight[:], keep[:], ALU.mult))
                own.link(dve.tensor_copy(fetch_at[:], place[:]))
                own.link(dve.tensor_scalar(keep[:], keep[:], -float(KEPT), float(KEPT), ALU.mult, ALU.add))
                own.link(dve.tensor_tensor(place[:], place[:], keep[:], ALU.add))
                dve.tensor_copy(send_to[:], place[:]).then_inc(routed, 1)

        with ExitStack() as ctx:
            rows = [sb(f"rows{k}", [P, ST, C], ctx=ctx) for k in range(2)]
            cols = [sb(f"cols{k}", [P, KC, CAPACITY], ctx=ctx) for k in range(2)]
            hidden = [sb(f"hidden{k}", [P, HC, CAPACITY], ctx=ctx) for k in range(2)]
            result = [sb(f"result{k}", [P, ST, C], ctx=ctx) for k in range(2)]
            ps_cols = psum(ctx, "ps_cols", [P, KC * CAPACITY])
            ps_hid = [psum(ctx, f"ps_hid{k}", [P, 2 * CAPACITY]) for k in range(2)]
            ps_res = psum(ctx, "ps_res", [P, ST * C])

            rows_in = [sem(f"rows_in{k}") for k in range(2)]
            cols_turned = sem("cols_turned")
            cols_ready = sem("cols_ready")
            hid_made = sem("hid_made")
            hid_ready = sem("hid_ready")
            res_made = [sem(f"res_made{k}") for k in range(2)]
            res_ready = sem("res_ready")
            res_stored = [sem(f"res_stored{k}") for k in range(2)]

            nc.all_engine_barrier()
            block = ctx.enter_context(nc.Block())

            TURNS = EXPERTS // 2

            def slot_rows(dram, e):
                return dram.rearrange("(e s p) c -> e p s c", s=ST, p=P)[bass.ds(e, 1)].rearrange("a p s c -> (a p) s c")

            @block.sync
            def _(sp):
                def load_rows(e, k):
                    sp.dma_start(rows[k][:], slot_rows(slots_dram, e)).then_inc(rows_in[k], 16)

                def store(turn, k):
                    sp.wait_ge(res_ready, 1 + turn * 2 + k + 1)
                    sp.nop(nofuse=True)
                    sp.dma_start(slot_rows(results_dram, turn * 2 + k), result[k][:]).then_inc(res_stored[k], 16)

                for k in range(2):
                    load_rows(k, k)
                with sp.Fori(1, TURNS) as turn:
                    for k in range(2):
                        sp.wait_ge(res_made[k], 1 + turn)
                        sp.nop(nofuse=True)
                        load_rows(turn * 2 + k, k)
                        load_weights(sp, turn * 2 + k, k)
                        store(turn - 1, k)
                for k in range(2):
                    store(TURNS - 1, k)
                for k in range(2):
                    sp.wait_ge(res_stored[k], 1 + 16 * TURNS)

            @block.scalar
            def _(act):
                with act.Fori(0, TURNS) as turn:
                    for k in range(2):
                        e = turn * 2 + k
                        for pair in range(HC // 2):
                            act.wait_ge(hid_made, 1 + e * (HC // 2) + pair + 1)
                            act.activation(hidden[k][:, 2 * pair:2 * pair + 2, :],
                                           ps_hid[pair % 2][:].rearrange("p (a s) -> p a s", a=2), ACT.Gelu)\
                               .then_inc(hid_ready, 1)

            @block.vector
            def _(dve):
                def take_cols(e, k):
                    dve.wait_ge(cols_turned, 1 + e + 1)
                    dve.tensor_copy(cols[k][:].rearrange("p k s -> p (k s)"), ps_cols[:]).then_inc(cols_ready, 1)

                def part(turn, last):
                    for k in range(2):
                        if not (last and k):
                            take_cols(turn * 2 + k + 1, 1 - k)
                        dve.wait_ge(res_made[k], 1 + turn + 1)
                        dve.wait_ge(res_stored[k], 1 + turn * 16)
                        dve.tensor_copy(result[k][:].rearrange("p s c -> p (s c)"), ps_res[:]).then_inc(res_ready, 1)

                take_cols(0, 0)
                with dve.Fori(0, TURNS - 1) as turn:
                    part(turn, False)
                part(TURNS - 1, True)

            @block.tensor
            def _(pe):
                def turn_rows(e, turn, k):
                    pe.wait_ge(rows_in[k], 1 + (turn + 1) * 16)
                    pe.wait_ge(cols_ready, 1 + e)
                    for c in range(KC):
                        for s in range(ST):
                            last = pe.transpose(ps_cols[:, c * CAPACITY + s * P:c * CAPACITY + (s + 1) * P],
                                                rows[k][:, s, c * P:(c + 1) * P], ident[:])
                    last.then_inc(cols_turned, 1)

                def part(turn, last_turn):
                    for k in range(2):
                        e = turn * 2 + k
                        pe.wait_ge(cols_ready, 1 + e + 1)
                        pe.wait_ge(weights_in[k], 1 + (turn + 1) * 32)
                        for pair in range(HC // 2):
                            if pair >= 2:
                                pe.wait_ge(hid_ready, 1 + e * (HC // 2) + pair - 1)
                            else:
                                pe.wait_ge(hid_ready, 1 + e * (HC // 2))
                            for m in range(2):
                                for c in range(KC):
                                    last = pe.matmul(ps_hid[pair % 2][:, m * CAPACITY:(m + 1) * CAPACITY],
                                                     up_w[k][:, c, (2 * pair + m) * P:(2 * pair + m + 1) * P],
                                                     cols[k][:, c, :], start=(c == 0), stop=(c == KC - 1))
                            last.then_inc(hid_made, 1)
                        if not (last_turn and k):
                            turn_rows(e + 1, turn + k, 1 - k)
                        pe.wait_ge(hid_ready, 1 + (e + 1) * (HC // 2))
                        pe.wait_ge(res_ready, 1 + e)
                        for s in range(ST):
                            for m in range(HC):
                                last = pe.matmul(ps_res[:, s * C:(s + 1) * C], hidden[k][:, m, s * P:(s + 1) * P],
                                                 down_w[k][:, m, :], start=(m == 0), stop=(m == HC - 1))
                        last.then_inc(res_made[k], 1)

                turn_rows(0, 0, 0)
                with pe.Fori(0, TURNS - 1) as turn:
                    part(turn, False)
                part(TURNS - 1, True)

        with ExitStack() as ctx:
            RING = 8
            got = sb("got", [P, RING, C], ctx=ctx)
            fetched = [sem(f"fetched{k}", start=0) for k in range(RING)]
            added = sem("added")
            stored = sem("stored")
            nc.all_engine_barrier()
            block = ctx.enter_context(nc.Block())

            @block.gpsimd
            def _(pool):
                for t in range(NT):
                    if t >= RING:
                        pool.wait_ge(added, 1 + t - RING + 1)
                    pool.indirect_dma_start(
                        out=got[:, t % RING, :], out_offset=None, in_=results_dram,
                        in_offset=bass.IndirectOffsetOnAxis(ap=fetch_at[:, t:t + 1].bitcast(U32), axis=0),
                        bounds_check=KEPT - 1, oob_is_err=False).then_inc(fetched[t % RING], 16)

            @block.vector
            def _(dve):
                for t in range(NT):
                    dve.wait_ge(fetched[t % RING], 16 * (t // RING + 1))
                    dve.scalar_tensor_tensor(out=base[:, t, :], in0=got[:, t % RING, :], scalar=weight[:, t:t + 1],
                                             in1=base[:, t, :], op0=ALU.mult, op1=ALU.add).then_inc(added, 1)

            @block.sync
            def _(sp):
                with sp.Fori(0, BATCH) as b:
                    sp.wait_ge(added, 1 + (b + 1) * TILES)
                    sp.nop(nofuse=True)
                    sp.dma_start(x_out[bass.ds(b * TILES, TILES)].rearrange("n p c -> p n c"),
                                 base[:, bass.ds(b * TILES, TILES), :]).then_inc(stored, 16)
                sp.wait_ge(stored, 1 + 16 * BATCH)


FIELDS = 6
FA, FW, FR, FB, FK, FV = range(FIELDS)
PACK = FIELDS * D
SPAN = 16
PAIRS = SPAN // 2
STATE = D * D
RING = 4
TURN_SPANS = 4


def recurrence(nc, packed, o_out):
    with ExitStack() as ctx:
        def sb(name, shape, dt=F32):
            return ctx.enter_context(nc.sbuf_tensor("sc_" + name, shape, dt))

        def psum(name, shape):
            return ctx.enter_context(nc.psum_tensor("sc_" + name, shape, F32))

        sem = ctx.enter_context(semaphores(nc, "sc_"))

        pack = [sb(f"pack{n}", [P, SPAN, PACK]) for n in range(4)]
        outer = [sb(f"outer{n}", [P, SPAN, STATE]) for n in range(2)]
        seen = sb("seen", [P, 2 * PAIRS, STATE])
        terms = [sb(f"terms{n}", [P, SPAN, STATE]) for n in range(2)]
        dot_terms = sb("dot_terms", [P, PAIRS, 2, 2, D])
        dots = [sb(f"dots{n}", [P, PAIRS, 2, 2]) for n in range(4)]
        b_part = sb("b_part", [P, PAIRS, 2, D])
        from_v = [sb(f"from_v{n}", [P, PAIRS, D]) for n in range(4)]
        from_u = [sb(f"from_u{n}", [P, PAIRS, D]) for n in range(2)]
        o_buf = [sb(f"o_buf{n}", [P, SPAN * D]) for n in range(2)]
        ident = sb("ident", [P, P])
        u = [sb(f"u{n}", [P, PAIRS, 2, D]) for n in range(2)]
        rank = sb("rank", [P, 2, STATE])
        decayed = sb("decayed", [P, STATE])
        state = psum("state", [P, RING, STATE])
        prod = psum("prod", [P, 2 * STATE])
        partial = psum("partial", [P, STATE])
        added = [psum(f"added{n}", [P, STATE]) for n in range(2)]
        ps_o = [psum(f"ps_o{n}", [P, SPAN * D]) for n in range(2)]

        NSPANS = T // SPAN
        COPIES = PAIRS // 2
        OPS = 7
        AHEAD = 10
        BEHIND = 6

        def counter(name, lead):
            return sem(name, start=1 + lead), 1 + lead

        chain, CHAIN = counter("chain", 4 * OPS)
        times, TIMES = counter("times", 4 * BEHIND)
        copied, COPIED = counter("copied", COPIES)
        added_made, ADDED = counter("added_made", 2 * PAIRS)
        o_made, O_MADE = counter("o_made", 4)
        o_copied, O_COPIED = counter("o_copied", 4)
        consts = sem("consts")
        packed_in = [sem(f"packed_in{n}") for n in range(4)]
        pre = sem("pre")
        dots_made = sem("dots_made")
        o_stored = [sem(f"o_stored{n}") for n in range(2)]

        nc.all_engine_barrier()
        block = ctx.enter_context(nc.Block())

        def spans(eng, part):
            for m in range(TURN_SPANS):
                part(m, 0, m)
            last = NSPANS // TURN_SPANS - 1
            with eng.Fori(1, last) as i:
                for m in range(TURN_SPANS):
                    part(i * TURN_SPANS + m, i, m)
            for m in range(TURN_SPANS):
                part(last * TURN_SPANS + m, last, m)

        def there(g, i, m, shift):
            if isinstance(g, int) and not 0 <= g + shift < NSPANS:
                return None
            return g + shift, i + (m + shift) // TURN_SPANS, (m + shift) % TURN_SPANS

        def by_pair(m):
            return pack[m % 4][:].rearrange("p (n s) f -> p n s f", s=2)

        def vectors(m, step, field):
            return by_pair(m)[:, :, step, field * D:(field + 1) * D]

        def two_vectors(m, step, field):
            return by_pair(m)[:, :, step, field * D:(field + 2) * D].rearrange("p n (f d) -> p n f d", d=D)

        @block.sync
        def _(sp):
            def load(g, i, m):
                sp.wait_ge(times, TIMES + (g - 3) * BEHIND)
                sp.nop(nofuse=True)
                for b in range(BATCH):
                    sp.dma_start(pack[m % 4][b * HEADS:(b + 1) * HEADS, :, :],
                                 packed[b, bass.ds(g * SPAN, SPAN)].rearrange("t h f -> h t f"))\
                      .then_inc(packed_in[m % 4], 16)

            def store(g, i, m):
                sp.wait_ge(o_copied, O_COPIED + g + 1)
                sp.nop(nofuse=True)
                for b in range(BATCH):
                    sp.dma_start(o_out[b, bass.ds(g * SPAN, SPAN)].rearrange("t h d -> h t d"),
                                 o_buf[m % 2][b * HEADS:(b + 1) * HEADS, :].rearrange("p (t d) -> p t d", d=D))\
                      .then_inc(o_stored[m % 2], 16)

            for g in range(3):
                load(g, 0, g)

            def part(*at):
                ahead, behind = there(*at, 3), there(*at, -3)
                if ahead:
                    load(*ahead)
                if behind:
                    store(*behind)

            spans(sp, part)
            for g in range(NSPANS - 3, NSPANS):
                store(g, g // TURN_SPANS, g % TURN_SPANS)
            for n in range(2):
                sp.wait_ge(o_stored[n], 1 + NSPANS // 2 * 16 * BATCH)

        @block.gpsimd
        def _(pool):
            own = Tally(pool, consts)
            own.link(pool.memset(ident[:], 0.0))
            own.up(pool.memset(seen[:, 2 * PAIRS - 1, :], 0.0))
            own.up(pool.affine_select(out=ident[:], in_=ident[:], compare_op=ALU.not_equal, fill=1.0, base=0,
                                      pattern=[[-1, P]], channel_multiplier=1))
            own.done()
            pairwise = [P, PAIRS, 2, D]

            def dot_products(g, i, m):
                pool.wait_ge(packed_in[m % 4], 1 + (i + 1) * 16 * BATCH)
                pool.wait_ge(dots_made, 1 + g)
                for n, (step, field) in enumerate(((1, FA), (0, FR))):
                    pool.tensor_tensor(dot_terms[:, :, n, :, :], two_vectors(m, 0, FB),
                                       vectors(m, step, field).unsqueeze(2).broadcast_to(pairwise), ALU.mult)\
                        .then_inc(pre, 1)

            def prepare_span(g, i, m):
                own = Tally(pool, pre, g * AHEAD + 2)
                pool.wait_ge(dots_made, 1 + g + 1)
                own.up(pool.tensor_tensor(two_vectors(m, 0, FB), two_vectors(m, 0, FB),
                                          vectors(m, 1, FW).unsqueeze(2).broadcast_to(pairwise), ALU.mult))
                own.up(pool.tensor_tensor(b_part[:], dots[m % 4][:, :, 0, :].unsqueeze(3).broadcast_to(pairwise),
                                          vectors(m, 1, FB).unsqueeze(2).broadcast_to(pairwise), ALU.mult))
                own.done()
                own.up(pool.tensor_tensor(two_vectors(m, 0, FB), two_vectors(m, 0, FB), b_part[:], ALU.add))
                own.up(pool.tensor_tensor(two_vectors(m, 1, FA), two_vectors(m, 1, FA),
                                          vectors(m, 0, FW).unsqueeze(2).broadcast_to(pairwise), ALU.mult))
                own.up(pool.tensor_tensor(vectors(m, 0, FR), vectors(m, 0, FR), vectors(m, 0, FW), ALU.mult))
                pool.wait_ge(o_made, O_MADE + g - 3)
                own.up(pool.tensor_tensor(from_v[m % 4][:], vectors(m, 0, FV),
                                          dots[m % 4][:, :, 1, 1:2].broadcast_to([P, PAIRS, D]), ALU.mult))
                own.done()
                pool.wait_ge(added_made, ADDED + (g - 1) * PAIRS)
                for half in range(2):
                    t = slice(half * PAIRS, (half + 1) * PAIRS)
                    shape = [P, PAIRS, D, D]
                    own.up(pool.tensor_tensor(
                        outer[m % 2][:, t, :].rearrange("p t (i j) -> p t i j", j=D),
                        pack[m % 4][:, t, FV * D:(FV + 1) * D].unsqueeze(3).broadcast_to(shape),
                        pack[m % 4][:, t, FK * D:(FK + 1) * D].unsqueeze(2).broadcast_to(shape), ALU.mult))
                assert own.n + 2 == AHEAD

            def read_states(g, i, m):
                pool.wait_ge(o_made, O_MADE + g - 1)
                made = 0

                def product(slot, pair, n, step):
                    shape = [P, n, D, D]
                    return pool.tensor_tensor(
                        terms[m % 2][:].rearrange("p (n s) (i j) -> p n s i j", s=2, j=D)[:, pair:pair + n, step],
                        seen[:, slot:slot + n, :].rearrange("p n (i j) -> p n i j", j=D),
                        vectors(m, step, FR)[:, pair:pair + n, :].unsqueeze(2).broadcast_to(shape), ALU.mult)

                first = m % 2 * PAIRS
                for half in range(2):
                    pair, n = half * PAIRS // 2, PAIRS // 2
                    pool.wait_ge(copied, COPIED + g * COPIES + (half + 1) * COPIES // 2)
                    product(first + pair, pair, n, 1).then_inc(times, 1)
                    if first + pair == 0:
                        product(2 * PAIRS - 1, 0, 1, 0).then_inc(times, 1)
                        product(0, 1, n - 1, 0).then_inc(times, 1)
                        made += 3
                    else:
                        last = pair == PAIRS // 2
                        more = BEHIND - 1 - made - 1 if last else 1
                        product(first + pair - 1, pair, n, 0).then_inc(times, more)
                        made += 1 + more
                pool.tensor_tensor(from_u[m % 2][:], u[m % 2][:, :, 0, :],
                                   dots[m % 4][:, :, 1, 0:1].broadcast_to([P, PAIRS, D]), ALU.mult)\
                    .then_inc(times, 1)
                assert made + 1 == BEHIND

            dot_products(0, 0, 0)
            prepare_span(0, 0, 0)

            def part(*at):
                ahead, behind = there(*at, 1), there(*at, -1)
                if ahead:
                    dot_products(*ahead)
                if behind:
                    read_states(*behind)
                if ahead:
                    prepare_span(*ahead)

            spans(pool, part)
            read_states(NSPANS - 1, NSPANS // TURN_SPANS - 1, TURN_SPANS - 1)

        @block.vector
        def _(dve):
            dve.memset(state[:, RING - 1, :], 0.0).then_inc(chain, 1)
            square, two = [P, D, D], [P, 2, D, D]

            def sum_dots(g, i, m):
                dve.wait_ge(pre, 1 + g * AHEAD + 2)
                dve.tensor_reduce(dots[m % 4][:].rearrange("p n x y -> p (n x y)"),
                                  dot_terms[:].rearrange("p n x y d -> p (n x y) d"), AX.X, ALU.add)\
                   .then_inc(dots_made, 1)

            sum_dots(0, 0, 0)

            def part(g, i, m):
                ahead = there(g, i, m, 1)
                for pair in range(PAIRS):
                    q = g * PAIRS + pair
                    slot = (m * PAIRS + pair) % RING
                    base = CHAIN + 1 + q * OPS
                    old = state[:, (slot - 1) % RING, :].rearrange("p (i j) -> p i j", j=D)
                    steps = pack[m % 4][:, 2 * pair:2 * pair + 2, :]
                    if pair == 0:
                        dve.wait_ge(pre, 1 + g * AHEAD + AHEAD - 2)
                        dve.wait_ge(times, TIMES + (g - 1) * BEHIND)
                    dve.wait_ge(chain, base)
                    dve.tensor_tensor(prod[:].rearrange("p (s i j) -> p s i j", s=2, j=D),
                                      old.unsqueeze(1).broadcast_to(two),
                                      steps[:, :, FA * D:(FA + 1) * D].unsqueeze(2).broadcast_to(two), ALU.mult)\
                       .then_inc(chain, 1)
                    dve.tensor_tensor(decayed[:].rearrange("p (i j) -> p i j", j=D), old,
                                      steps[:, 1, FW * D:(FW + 1) * D].unsqueeze(1).broadcast_to(square), ALU.mult).then_inc(chain, 1)
                    dve.wait_ge(chain, base + 1)
                    dve.tensor_reduce(u[m % 2][:, pair, :, :].rearrange("p s i -> p (s i)"),
                                      prod[:].rearrange("p (n j) -> p n j", j=D), AX.X, ALU.add).then_inc(chain, 1)
                    dve.wait_ge(chain, base + 3)
                    for s in range(2):
                        dve.tensor_tensor(rank[:, s, :].rearrange("p (i j) -> p i j", j=D),
                                          u[m % 2][:, pair, s, :].unsqueeze(2).broadcast_to(square),
                                          steps[:, s, FB * D:(FB + 1) * D].unsqueeze(1).broadcast_to(square),
                                          ALU.mult).then_inc(chain, 1)
                    if pair % 2 == 0:
                        dve.wait_ge(copied, COPIED + g * COPIES + pair // 2 - 1)
                    dve.wait_ge(added_made, ADDED + q + 1)
                    dve.wait_ge(chain, base + 4)
                    dve.tensor_tensor(partial[:], added[pair % 2][:], rank[:, 0, :], ALU.add).then_inc(chain, 1)
                    dve.wait_ge(chain, base + 6)
                    dve.tensor_tensor(state[:, slot, :], partial[:], rank[:, 1, :], ALU.add).then_inc(chain, 1)
                    if pair == PAIRS // 2 and ahead:
                        sum_dots(*ahead)

            spans(dve, part)
            dve.wait_ge(chain, CHAIN + 1 + NSPANS * PAIRS * OPS)
            dve.memset(rank[:], 0.0).then_inc(chain, 2)

        @block.scalar
        def _(act):
            def bring(g, i, m, n):
                pair = 2 * n
                if n in (0, COPIES - 1):
                    act.wait_ge(times, TIMES + (g - 1 if n == 0 else g) * BEHIND)
                act.wait_ge(chain, CHAIN + 1 + (g * PAIRS + pair + 2) * OPS + 2)
                slot, to = (m * PAIRS + pair) % RING, m % 2 * PAIRS + pair
                act.activation(seen[:, to:to + 2, :], state[:, slot:slot + 2, :], ACT.Copy).then_inc(copied, 1)

            def copy_o(g, i, m):
                act.wait_ge(o_made, O_MADE + g + 1)
                act.wait_ge(o_stored[m % 2], 1 + (i * 2 + m // 2) * 16 * BATCH)
                act.activation(o_buf[m % 2][:], ps_o[m % 2][:], ACT.Copy).then_inc(o_copied, 1)

            act.wait_ge(consts, 1 + 3)

            def part(*at):
                behind = there(*at, -3)
                for n in range(COPIES):
                    bring(*at, n)
                    if n == 1 and behind:
                        copy_o(*behind)

            spans(act, part)
            for g in range(NSPANS - 3, NSPANS):
                copy_o(g, g // TURN_SPANS, g % TURN_SPANS)

        @block.tensor
        def _(pe):
            pe.wait_ge(consts, 1 + 3)

            def add_outers(g, i, m, n):
                if n in (0, PAIRS // 2):
                    pe.wait_ge(pre, 1 + g * AHEAD + AHEAD - 1 + n // (PAIRS // 2))
                pe.wait_ge(chain, CHAIN + 1 + (g * PAIRS + n - 2) * OPS + 6)
                for s in range(2):
                    pe.matmul(added[n % 2][:], ident[:], outer[m % 2][:, 2 * n + s, :], start=(s == 0), stop=False)

            def add_decayed(g, n):
                pe.wait_ge(chain, CHAIN + 1 + (g * PAIRS + n) * OPS + 2)
                pe.matmul(added[n % 2][:], ident[:], decayed[:], start=False, stop=True).then_inc(added_made, 1)

            def add_terms(g, i, m, n):
                if n == 0:
                    pe.wait_ge(times, TIMES + (g + 1) * BEHIND)
                    pe.wait_ge(o_copied, O_COPIED + g - 1)
                by_column = terms[m % 2][:].rearrange("p t (i j) -> p (t i) j", j=D)
                share = D // PAIRS
                for j in range(n * share, (n + 1) * share):
                    last = pe.matmul(ps_o[m % 2][:], ident[:], by_column[:, :, j], start=(j == 0), stop=(j == D - 1))
                    if j == share:
                        first_steps = ps_o[m % 2][:].rearrange("p (n s d) -> p n s d", s=2, d=D)[:, :, 0, :]
                        pe.matmul(first_steps, ident[:], from_u[m % 2][:], start=False, stop=False)
                        pe.matmul(first_steps, ident[:], from_v[m % 4][:], start=False, stop=False)
                if n == PAIRS - 1:
                    last.then_inc(o_made, 1)

            add_outers(0, 0, 0, 0)

            def part(*at):
                ahead, behind = there(*at, 1), there(*at, -2)
                for n in range(PAIRS):
                    if n + 1 < PAIRS:
                        add_outers(*at, n + 1)
                    elif ahead:
                        add_outers(*ahead, 0)
                    add_decayed(at[0], n)
                    if behind:
                        add_terms(*behind, n)

            spans(pe, part)
            for g in range(NSPANS - 2, NSPANS):
                for n in range(PAIRS):
                    add_terms(g, g // TURN_SPANS, g % TURN_SPANS, n)


RW, RG = 64, 128
MIXES = ("r", "w", "a", "k", "v")


def with_slots(plan, slots=SLOTS):
    uses, out, place = [0] * slots, [], {}
    for n, (stage, what) in enumerate(plan):
        s = n % slots
        out.append((stage, what, s, uses[s]))
        place[stage, what] = (s, uses[s])
        uses[s] += 1
    return out, uses, place


def preparation_plan():
    plan = [("turn_x", c) for c in range(KC)]
    plan += [("r", 0), ("r", 1), ("turn_r", 0), ("turn_r", 1), ("w_inner", 0), ("g_inner", 0), ("w", 0), ("w", 1),
             ("a_inner", 0), ("g", 0), ("g", 1), ("a", 0), ("a", 1), ("k", 0), ("k", 1), ("v", 0), ("v", 1)]
    return plan


PREPARATION_USER = {"turn_x": "act", "r": "act", "turn_r": "act", "w_inner": "act", "g_inner": "act", "w": "dve",
                    "a_inner": "act", "g": "dve", "a": "dve", "k": "dve", "v": "act"}


def prepare(nc, x_in, mixes, k_k, k_a, r_k, weights, w_a, w_b, w_bias, a_a, a_b, a_bias, g_a, g_b, g_bias,
            packed, gate_out, bonus_out):
    plan, slot_uses, place = with_slots(preparation_plan())
    with ExitStack() as ctx:
        def sb(name, shape, dt=F32):
            return ctx.enter_context(nc.sbuf_tensor("pr_" + name, shape, dt))

        sem = ctx.enter_context(semaphores(nc, "pr_"))

        ctx.enter_context(nc.allow_non_contiguous_dma(reason="mixing columns"))
        slot = [ctx.enter_context(nc.psum_tensor(f"pr_slot{s}", [P, 2 * BANK], F32)) for s in range(SLOTS)]
        big = {m: sb("big_" + m, [P, KC, C]) for m in "rkv"}
        mu = {m: sb("mu_" + m, [P, KC]) for m in MIXES}
        inner_a = {"w": sb("w_inner_a", [P, KC, RW]), "a": sb("a_inner_a", [P, KC, RW]), "g": sb("g_inner_a", [P, KC, RG])}
        inner_b = {"w": sb("w_inner_b", [RW, C]), "a": sb("a_inner_b", [RW, C]), "g": sb("g_inner_b", [RG, C])}
        wide = {m: sb("wide_" + m, [P, C]) for m in ("k_k", "k_a", "r_k", "w", "a", "g")}
        ident = sb("ident", [P, P])
        x = sb("x", [P, TILES, C])
        xn = sb("xn", [P, TILES, C])
        stats = sb("stats", [P, TILES, 6])
        mean_var = sb("mean_var", [P, TILES, 2])
        std = sb("std", [P, TILES])
        rstd = sb("rstd", [P, TILES])
        turned = sb("turned", [P, KC, T + 1])
        delta = sb("delta", [P, KC, T])
        mixed = [sb(f"mixed{k}", [P, KC, T]) for k in range(2)]
        pack = [sb(f"pack{h}", [P, HALF_TILES * HEADS, PACK]) for h in range(2)]
        r_turned = sb("r_turned", [P, KC, T])
        inner = {"w": sb("w_inner", [RW, T]), "a": sb("a_inner", [RW, T]), "g": sb("g_inner", [RG, T])}
        HW = HALF_TILES * C
        r_rows = [sb(f"r_rows{h}", [P, HW]) for h in range(2)]
        gate_sb = sb("gate_sb", [P, HW])
        z = sb("z", [P, HW])
        a_sig = [sb(f"a_sig{h}", [P, HW]) for h in range(2)]
        scaled = sb("scaled", [P, HW])
        kk = sb("kk", [P, HW])
        squares = sb("squares", [P, HW])
        norm = sb("norm", [P, HALF_TILES * HEADS])
        rr = sb("rr", [P, HW])
        dots = sb("dots", [P, HALF_TILES * HEADS])
        bonus = sb("bonus", [P, HW])

        loaded = sem("loaded")
        consts = sem("consts")
        x_loaded = sem("x_loaded")
        var_ready = sem("var_ready")
        std_ready = sem("std_ready")
        xn_ready = sem("xn_ready")
        chain = sem("chain")
        mix_ready = sem("mix_ready")
        filled = [sem(f"filled{s}") for s in range(SLOTS)]
        emptied = [sem(f"emptied{s}") for s in range(SLOTS)]
        r_copied = sem("r_copied")
        z_used = sem("z_used")
        w_packed = sem("w_packed")
        kk_ready = sem("kk_ready")
        squared = sem("squared")
        norm2_ready = sem("norm2_ready")
        norm_ready = sem("norm_ready")
        rr_ready = sem("rr_ready")
        bonus_ready = sem("bonus_ready")
        pack_stored = sem("pack_stored")
        gate_stored = sem("gate_stored")
        bonus_stored = sem("bonus_stored")
        N_LOADS = 3 + len(MIXES) + 6 + 6

        def read_out(eng, b, *uses):
            latest = {}
            for stage, what in uses:
                s, use = place[stage, what]
                latest[s] = max(latest.get(s, 0), use + 1)
            for s, use in latest.items():
                eng.wait_ge(emptied[s], 1 + b * slot_uses[s] + use)
                if eng is nc.sync:
                    eng.nop(nofuse=True)

        def field(h, f):
            return pack[h][:, :, f * D:(f + 1) * D]

        def by_head(ap):
            return ap.rearrange("p (n d) -> p n d", d=D)

        nc.all_engine_barrier()
        block = ctx.enter_context(nc.Block())

        @block.sync
        def _(sp):
            loads = [(big[m][:], weights[m].rearrange("(k p) n -> p k n", p=P)) for m in "rkv"]
            loads += [(mu[m][:], mixes[m].rearrange("(k p) -> p k", p=P)) for m in MIXES]
            loads += [(inner_a[m][:], src.rearrange("(k p) n -> p k n", p=P)) for m, src in
                      (("w", w_a), ("a", a_a), ("g", g_a))]
            loads += [(inner_b[m][:], src) for m, src in (("w", w_b), ("a", a_b), ("g", g_b))]
            loads += [(wide[m][:], spread(src)) for m, src in
                      (("k_k", k_k), ("k_a", k_a), ("r_k", r_k), ("w", w_bias), ("a", a_bias), ("g", g_bias))]
            assert len(loads) == N_LOADS
            for dst, src in loads:
                sp.dma_start(dst, src).then_inc(loaded, 16)
            with sp.Fori(0, BATCH) as b:
                sp.wait_ge(xn_ready, 1 + b * TILES)
                sp.nop(nofuse=True)
                sp.dma_start(x[:], x_in[bass.ds(b * TILES, TILES)].rearrange("n p c -> p n c")).then_inc(x_loaded, 16)
                for h in range(2):
                    rows = bass.ds(b * TILES + h * HALF_TILES, HALF_TILES)
                    read_out(sp, b, ("g", h))
                    sp.dma_start(gate_out[rows].rearrange("n p c -> p n c"),
                                 gate_sb[:].rearrange("p (n c) -> p n c", c=C)).then_inc(gate_stored, 16)
                for h in range(2):
                    rows = bass.ds(b * TILES + h * HALF_TILES, HALF_TILES)
                    sp.wait_ge(bonus_ready, 1 + b * 2 + h + 1)
                    sp.nop(nofuse=True)
                    sp.dma_start(bonus_out[rows].rearrange("n p c -> p n c"),
                                 bonus[:].rearrange("p (n c) -> p n c", c=C)).then_inc(bonus_stored, 16)
                    sp.wait_ge(w_packed, 1 + b * 2 + h + 1)
                    sp.nop(nofuse=True)
                    sp.dma_start(packed[rows].rearrange("n p f -> p n f"),
                                 pack[h][:].rearrange("p (n h) f -> p n (h f)", h=HEADS)).then_inc(pack_stored, 16)
            sp.wait_ge(gate_stored, 1 + BATCH * 32)
            sp.wait_ge(bonus_stored, 1 + BATCH * 32)
            sp.wait_ge(pack_stored, 1 + BATCH * 32)

        @block.gpsimd
        def _(pool):
            own = Tally(pool, consts)
            own.up(pool.memset(turned[:], 0.0))
            own.link(pool.memset(ident[:], 0.0))
            own.up(pool.affine_select(out=ident[:], in_=ident[:], compare_op=ALU.not_equal, fill=1.0, base=0,
                                      pattern=[[-1, P]], channel_multiplier=1))
            pool.wait_ge(loaded, 1 + 16 * N_LOADS)
            r_k_wide = wide["r_k"][:].unsqueeze(1).broadcast_to([P, HALF_TILES, C])\
                .rearrange("p n (h d) -> p n h d", d=D)
            with pool.Fori(0, BATCH) as b:
                for h in range(2):
                    read_out(pool, b, ("r", h))
                    pool.wait_ge(bonus_ready, 1 + b * 2 + h)
                    pool.tensor_tensor(rr[:].rearrange("p (n h d) -> p n h d", d=D, h=HEADS),
                                       field(h, FR).rearrange("p (n h) d -> p n h d", h=HEADS), r_k_wide, ALU.mult)\
                        .then_inc(rr_ready, 1)
                    read_out(pool, b, ("k", h))
                    pool.wait_ge(rr_ready, 1 + b * 4 + h * 2 + 1)
                    pool.tensor_tensor(by_head(rr[:]), by_head(rr[:]), field(h, FK), ALU.mult).then_inc(rr_ready, 1)

        @block.tensor
        def _(pe):
            pe.wait_ge(consts, 1 + 3)
            pe.wait_ge(loaded, 1 + 16 * N_LOADS)
            mixed_of = {m: (mixed[n % 2], n) for n, m in enumerate(MIXES)}
            with pe.Fori(0, BATCH) as b:
                for stage, what, s, use in plan:
                    ps = slot[s]
                    pe.wait_ge(emptied[s], 1 + b * slot_uses[s] + use)
                    if stage == "turn_x":
                        if what == 0:
                            pe.wait_ge(xn_ready, 1 + (b + 1) * TILES)
                        for t in range(TILES):
                            last = pe.transpose(ps[:, t * P:(t + 1) * P], xn[:, t, what * P:(what + 1) * P], ident[:])
                    elif stage in ("r", "k", "v"):
                        src, n = mixed_of[stage]
                        if what == 0:
                            pe.wait_ge(mix_ready, 1 + b * len(MIXES) + n + 1)
                        for n in range(HALF_TILES):
                            t = HALF_TILES * what + n
                            for k in range(KC):
                                last = pe.matmul(ps[:, n * C:(n + 1) * C], src[:, k, t * P:(t + 1) * P],
                                                 big[stage][:, k, :], start=(k == 0), stop=(k == KC - 1))
                    elif stage == "turn_r":
                        if what == 0:
                            read_out(pe, b, ("r", 0), ("r", 1))
                        for t in range(TILES):
                            n = (t % HALF_TILES) * C + what * P
                            last = pe.transpose(ps[:, t * P:(t + 1) * P], r_rows[t // HALF_TILES][:, n:n + P],
                                                ident[:])
                    elif stage in ("w_inner", "a_inner", "g_inner"):
                        m = stage[0]
                        if m == "g":
                            read_out(pe, b, ("turn_r", 0), ("turn_r", 1))
                            src = r_turned
                        else:
                            src, n = mixed_of[m]
                            pe.wait_ge(mix_ready, 1 + b * len(MIXES) + n + 1)
                        width = inner_a[m].shape[2]
                        for half in range(2):
                            for k in range(KC):
                                last = pe.matmul(ps[0:width, half * BANK:(half + 1) * BANK], inner_a[m][:, k, :],
                                                 src[:, k, half * BANK:(half + 1) * BANK],
                                                 start=(k == 0), stop=(k == KC - 1))
                    else:
                        if what == 0:
                            read_out(pe, b, (stage + "_inner", 0))
                        for n in range(HALF_TILES):
                            t = HALF_TILES * what + n
                            last = pe.matmul(ps[:, n * C:(n + 1) * C], inner[stage][:, t * P:(t + 1) * P],
                                             inner_b[stage][:], start=True, stop=True)
                    last.then_inc(filled[s], 1)

        @block.scalar
        def _(act):
            act.wait_ge(consts, 1 + 3)
            with act.Fori(0, BATCH) as b:
                act.wait_ge(var_ready, 1 + b + 1)
                act.activation(std[:], mean_var[:, :, 1], ACT.Sqrt).then_inc(std_ready, 1)
                for stage, what, s, use in plan:
                    ps = slot[s]
                    if PREPARATION_USER[stage] == "act":
                        act.wait_ge(filled[s], 1 + b * slot_uses[s] + use + 1)
                    if stage == "turn_x":
                        if what == 0:
                            act.wait_ge(mix_ready, 1 + b * len(MIXES))
                        act.activation(turned[:, what, 1:T + 1], ps[:], ACT.Copy).then_inc(emptied[s], 1)
                    elif stage in ("r", "v"):
                        f = FR if stage == "r" else FV
                        if stage == "r":
                            act.wait_ge(pack_stored, 1 + b * 32)
                            act.activation(r_rows[what][:], ps[:], ACT.Copy).then_inc(r_copied, 1)
                            act.wait_ge(r_copied, 1 + b * 2 + what + 1)
                        act.activation(field(what, f), by_head(ps[:]), ACT.Copy).then_inc(emptied[s], 1)
                    elif stage == "turn_r":
                        act.activation(r_turned[:, what, :], ps[:], ACT.Copy).then_inc(emptied[s], 1)
                    elif stage in ("w_inner", "a_inner", "g_inner"):
                        m = stage[0]
                        width = inner_a[m].shape[2]
                        act.activation(inner[m][:], ps[0:width, :],
                                       {"w": ACT.Tanh, "a": ACT.Copy, "g": ACT.Sigmoid}[m]).then_inc(emptied[s], 1)
                    elif stage == "w":
                        read_out(act, b, (stage, what))
                        act.activation(z[:], z[:], ACT.Sigmoid).then_inc(z_used, 1)
                        act.wait_ge(z_used, 1 + b * 4 + what + 1)
                        act.activation(field(what, FW), by_head(z[:]), ACT.Copy, scale=float(np.exp(-0.5)))\
                           .then_inc(w_packed, 1)
                    elif stage == "a":
                        read_out(act, b, (stage, what))
                        act.wait_ge(bonus_ready, 1 + b * 2)
                        act.activation(a_sig[what][:], z[:], ACT.Sigmoid).then_inc(z_used, 1)
                    elif stage == "k":
                        act.wait_ge(kk_ready, 1 + b * 2 + what + 1)
                        act.activation(squares[:], kk[:], ACT.Square).then_inc(squared, 1)
                        act.wait_ge(norm2_ready, 1 + b * 2 + what + 1)
                        act.activation(norm[:], norm[:], ACT.Sqrt).then_inc(norm_ready, 1)

        @block.vector
        def _(dve):
            dve.wait_ge(consts, 1 + 3)
            dve.wait_ge(loaded, 1 + 16 * N_LOADS)
            TURN = 2 * TILES + 1 + KC + 2 * 6
            with dve.Fori(0, BATCH) as b:
                own = Tally(dve, chain, b * TURN)
                dve.wait_ge(x_loaded, 1 + (b + 1) * 16)
                for t in range(TILES):
                    own.up(dve.bn_stats(stats[:, t, :], x[:, t, :]))
                own.done()
                dve.nop(nofuse=True)
                for t in range(TILES):
                    own.up(dve.bn_aggr(mean_var[:, t, :], stats[:, t, :]))
                own.done()
                dve.tensor_scalar(mean_var[:, :, 1], mean_var[:, :, 1], LN_EPS, None, ALU.add).then_inc(var_ready, 1)
                dve.wait_ge(std_ready, 1 + b + 1)
                own.link(dve.reciprocal(rstd[:], std[:]))
                for t in range(TILES):
                    dve.tensor_scalar(xn[:, t, :], x[:, t, :], mean_var[:, t, 0:1], rstd[:, t:t + 1],
                                      ALU.subtract, ALU.mult).then_inc(xn_ready, 1)
                read_out(dve, b, ("turn_x", 0), ("turn_x", 1))
                for k in range(KC):
                    own.up(dve.tensor_tensor(delta[:, k, :], turned[:, k, 0:T], turned[:, k, 1:T + 1], ALU.subtract))
                own.done()

                def mix(m):
                    n = MIXES.index(m)
                    if n >= 2:
                        before = MIXES[n - 2]
                        read_out(dve, b, *{"r": [("r", 1)], "w": [("w_inner", 0)], "a": [("a_inner", 0)]}[before])
                    for k in range(KC):
                        ins = dve.scalar_tensor_tensor(out=mixed[n % 2][:, k, :], in0=delta[:, k, :],
                                                       scalar=mu[m][:, k:k + 1], in1=turned[:, k, 1:T + 1],
                                                       op0=ALU.mult, op1=ALU.add)
                    ins.then_inc(mix_ready, 1)

                mix("r")
                mix("w")
                for stage, what, s, use in plan:
                    ps = slot[s]
                    if stage == "w" and what == 0:
                        mix("a")
                    if stage == "g" and what == 0:
                        mix("k")
                    if stage == "k" and what == 0:
                        mix("v")
                    if PREPARATION_USER[stage] != "dve":
                        continue
                    wide_of = {m: wide[m][:].unsqueeze(1).broadcast_to([P, HALF_TILES, C]) for m in wide}
                    by_tile = lambda ap: ap.rearrange("p (n c) -> p n c", c=C)
                    dve.wait_ge(filled[s], 1 + b * slot_uses[s] + use + 1)
                    if stage in ("w", "a"):
                        n = what + (2 if stage == "a" else 0)
                        dve.wait_ge(z_used, 1 + b * 4 + n)
                        dve.wait_ge(w_packed, 1 + b * 2 + min(n, 2))
                        dve.tensor_tensor(by_tile(z[:]), by_tile(ps[:]), wide_of[stage], ALU.add)\
                           .then_inc(emptied[s], 1)
                    elif stage == "g":
                        dve.wait_ge(gate_stored, 1 + b * 32 + what * 16)
                        dve.tensor_tensor(by_tile(gate_sb[:]), by_tile(ps[:]), wide_of["g"], ALU.add)\
                           .then_inc(emptied[s], 1)
                    elif stage == "k":
                        dve.wait_ge(z_used, 1 + b * 4 + 2 + what + 1)
                        own.up(dve.scalar_tensor_tensor(
                            out=by_tile(scaled[:]), in0=by_tile(a_sig[what][:]), scalar=-1.0, in1=wide_of["k_a"],
                            op0=ALU.add, op1=ALU.mult))
                        dve.wait_ge(squared, 1 + b * 2 + what)
                        dve.tensor_tensor(by_tile(kk[:]), by_tile(ps[:]), wide_of["k_k"], ALU.mult)\
                           .then_inc(kk_ready, 1)
                        own.done()
                        dve.scalar_tensor_tensor(out=field(what, FK), in0=by_head(scaled[:]), scalar=1.0,
                                                 in1=by_head(ps[:]), op0=ALU.add, op1=ALU.mult)\
                           .then_inc(emptied[s], 1)
                        dve.wait_ge(squared, 1 + b * 2 + what + 1)
                        dve.tensor_reduce(norm[:], by_head(squares[:]), AX.X, ALU.add).then_inc(norm2_ready, 1)
                        dve.wait_ge(norm_ready, 1 + b * 2 + what + 1)
                        own.link(dve.tensor_scalar(norm[:], norm[:], 1e-12, -1.0, ALU.max, ALU.mult))
                        own.link(dve.reciprocal(norm[:], norm[:]))
                        own.link(dve.tensor_tensor(field(what, FA), by_head(kk[:]),
                                                   norm[:].unsqueeze(2).broadcast_to([P, HALF_TILES * HEADS, D]),
                                                   ALU.mult))
                        own.up(dve.scalar_tensor_tensor(out=field(what, FB), in0=field(what, FA), scalar=-1.0,
                                                        in1=by_head(a_sig[what][:]), op0=ALU.mult, op1=ALU.mult))
                        own.done()
                for h in range(2):
                    dve.wait_ge(rr_ready, 1 + b * 4 + h * 2 + 2)
                    own.link(dve.tensor_reduce(dots[:], by_head(rr[:]), AX.X, ALU.add))
                    read_out(dve, b, ("v", h))
                    dve.wait_ge(bonus_stored, 1 + b * 32 + h * 16)
                    dve.tensor_tensor(by_head(bonus[:]), field(h, FV),
                                      dots[:].unsqueeze(2).broadcast_to([P, HALF_TILES * HEADS, D]), ALU.mult)\
                       .then_inc(bonus_ready, 1)
                assert own.n == TURN, own.n


def finish(nc, x_in, o_in, gate_in, bonus_in, gn_weight, gn_bias, w_o, x_out):
    with ExitStack() as ctx:
        def sb(name, shape, dt=F32):
            return ctx.enter_context(nc.sbuf_tensor("fi_" + name, shape, dt))

        sem = ctx.enter_context(semaphores(nc, "fi_"))

        slot = [ctx.enter_context(nc.psum_tensor(f"fi_slot{s}", [P, 2 * BANK], F32)) for s in range(4)]
        w = sb("w", [P, KC, C])
        ident = sb("ident", [P, P])
        wide_w = sb("wide_w", [P, C])
        wide_b = sb("wide_b", [P, C])
        x = [sb(f"x{k}", [P, TILES, C]) for k in range(2)]
        o = [sb(f"o{k}", [P, TILES, C]) for k in range(2)]
        gate = [sb(f"gate{k}", [P, TILES, C]) for k in range(2)]
        bonus = [sb(f"bonus{k}", [P, TILES, C]) for k in range(2)]
        squares = sb("squares", [P, TILES * C])
        mean = sb("mean", [P, TILES * HEADS])
        var = sb("var", [P, TILES * HEADS])
        turned = sb("turned", [P, KC, T])

        loaded = sem("loaded")
        consts = sem("consts")
        in_ready = [sem(f"in_ready{k}") for k in range(2)]
        chain = sem("chain")
        centred = sem("centred")
        squared = sem("squared")
        var_ready = sem("var_ready")
        std_ready = sem("std_ready")
        normed = sem("normed")
        with_bias = sem("with_bias")
        gated = sem("gated")
        turn_made = sem("turn_made")
        turn_ready = sem("turn_ready")
        y_made = sem("y_made")
        y_ready = sem("y_ready")
        stored = [sem(f"stored{k}") for k in range(2)]
        nc.all_engine_barrier()
        block = ctx.enter_context(nc.Block())

        @block.sync
        def _(sp):
            sp.dma_start(w[:], w_o.rearrange("(k p) n -> p k n", p=P)).then_inc(loaded, 16)
            sp.dma_start(wide_w[:], spread(gn_weight)).then_inc(loaded, 16)
            sp.dma_start(wide_b[:], spread(gn_bias)).then_inc(loaded, 16)
            with sp.Fori(0, BATCH // 2) as i:
                for k in range(2):
                    rows = bass.ds(i * 2 * TILES + k * TILES, TILES)
                    sp.wait_ge(stored[k], 1 + i * 16)
                    sp.nop(nofuse=True)
                    for dst, src in ((x, x_in), (o, o_in), (gate, gate_in), (bonus, bonus_in)):
                        sp.dma_start(dst[k][:], src[rows].rearrange("n p c -> p n c")).then_inc(in_ready[k], 16)

        @block.gpsimd
        def _(pool):
            own = Tally(pool, consts)
            own.link(pool.memset(ident[:], 0.0))
            own.up(pool.affine_select(out=ident[:], in_=ident[:], compare_op=ALU.not_equal, fill=1.0, base=0,
                                      pattern=[[-1, P]], channel_multiplier=1))
            pool.wait_ge(loaded, 1 + 48)
            bias_wide = wide_b[:].unsqueeze(1).broadcast_to([P, TILES, C])
            with pool.Fori(0, BATCH // 2) as i:
                for k in range(2):
                    b = i * 2 + k
                    pool.wait_ge(in_ready[k], 1 + (i + 1) * 64)
                    pool.tensor_tensor(bonus[k][:], bonus[k][:], bias_wide, ALU.add).then_inc(with_bias, 1)

        @block.tensor
        def _(pe):
            pe.wait_ge(consts, 1 + 2)
            pe.wait_ge(loaded, 1 + 48)
            with pe.Fori(0, BATCH // 2) as i:
                for k in range(2):
                    b = i * 2 + k
                    pe.wait_ge(gated, 1 + b + 1)
                    pe.wait_ge(turn_ready, 1 + b * KC)
                    for c in range(KC):
                        for t in range(TILES):
                            last = pe.transpose(slot[c][:, t * P:(t + 1) * P], o[k][:, t, c * P:(c + 1) * P], ident[:])
                        last.then_inc(turn_made, 1)
                    pe.wait_ge(turn_ready, 1 + b * KC + KC)
                    pe.wait_ge(y_ready, 1 + b * 2)
                    for h in range(2):
                        for n in range(HALF_TILES):
                            t = h * HALF_TILES + n
                            for c in range(KC):
                                last = pe.matmul(slot[2 + h][:, n * C:(n + 1) * C], turned[:, c, t * P:(t + 1) * P],
                                                 w[:, c, :], start=(c == 0), stop=(c == KC - 1))
                        last.then_inc(y_made, 1)

        @block.scalar
        def _(act):
            with act.Fori(0, BATCH // 2) as i:
                for k in range(2):
                    b = i * 2 + k
                    act.wait_ge(centred, 1 + b + 1)
                    act.activation(squares[:], o[k][:].rearrange("p n c -> p (n c)"), ACT.Square).then_inc(squared, 1)
                    act.wait_ge(var_ready, 1 + b + 1)
                    act.activation(var[:], var[:], ACT.Sqrt).then_inc(std_ready, 1)
                    act.wait_ge(y_made, 1 + b * 2)
                    for c in range(KC):
                        act.wait_ge(turn_made, 1 + b * KC + c + 1)
                        act.activation(turned[:, c, :], slot[c][:], ACT.Copy).then_inc(turn_ready, 1)
                    for h in range(2):
                        act.wait_ge(y_ready, 1 + b * 2 + h + 1)
                    act.dma_start(x_out[bass.ds(b * TILES, TILES)].rearrange("n p c -> p n c"), x[k][:])\
                       .then_inc(stored[k], 16)
            for k in range(2):
                act.wait_ge(stored[k], 1 + (BATCH // 2) * 16)

        @block.vector
        def _(dve):
            dve.wait_ge(loaded, 1 + 48)
            weight_wide = wide_w[:].unsqueeze(1).broadcast_to([P, TILES, C])
            TURN = 12
            with dve.Fori(0, BATCH // 2) as i:
                own = Tally(dve, chain, i * TURN)
                for k in range(2):
                    b = i * 2 + k
                    heads = o[k][:].rearrange("p n (h d) -> p (n h) d", d=D)
                    spread_out = lambda ap: ap.unsqueeze(2).broadcast_to([P, TILES * HEADS, D])
                    dve.wait_ge(in_ready[k], 1 + (i + 1) * 64)
                    own.link(dve.tensor_reduce(mean[:], heads, AX.X, ALU.add))
                    own.link(dve.tensor_scalar(mean[:], mean[:], 1.0 / D, None, ALU.mult))
                    dve.tensor_tensor(heads, heads, spread_out(mean[:]), ALU.subtract).then_inc(centred, 1)
                    dve.wait_ge(squared, 1 + b + 1)
                    own.link(dve.tensor_reduce(var[:], squares[:].rearrange("p (n d) -> p n d", d=D), AX.X, ALU.add))
                    dve.tensor_scalar(var[:], var[:], 1.0 / D, LN_EPS, ALU.mult, ALU.add).then_inc(var_ready, 1)
                    dve.wait_ge(std_ready, 1 + b + 1)
                    own.link(dve.reciprocal(var[:], var[:]))
                    own.link(dve.tensor_tensor(heads, heads, spread_out(var[:]), ALU.mult))
                    own.link(dve.tensor_tensor(o[k][:], o[k][:], weight_wide, ALU.mult))
                    dve.wait_ge(with_bias, 1 + b + 1)
                    dve.tensor_tensor(o[k][:], o[k][:], bonus[k][:], ALU.add).then_inc(normed, 1)
                    dve.wait_ge(normed, 1 + b + 1)
                    dve.tensor_tensor(o[k][:], o[k][:], gate[k][:], ALU.mult).then_inc(gated, 1)
                    for h in range(2):
                        dve.wait_ge(y_made, 1 + b * 2 + h + 1)
                        t = slice(h * HALF_TILES, (h + 1) * HALF_TILES)
                        dve.tensor_tensor(x[k][:, t, :], slot[2 + h][:].rearrange("p (n c) -> p n c", c=C),
                                          x[k][:, t, :], ALU.add).then_inc(y_ready, 1)
                assert own.n == TURN, own.n


def program(nc, a, out):
    def dram(name, shape):
        return nc.dram_tensor(name, shape, F32, kind="Internal").ap()

    def tiles(ap):
        return ap.rearrange("b (n p) c -> (b n) p c", p=P)

    x_attended, x_mixed, x_recurred = (dram(n, (NT, P, C)) for n in ("x_attended", "x_mixed", "x_recurred"))
    slots, results = dram("slots", (KEPT, C)), dram("results", (KEPT, C))
    packed = dram("packed", (NT, P, HEADS * PACK))
    gate, bonus, o = (dram(n, (NT, P, C)) for n in ("gate", "bonus", "o"))
    experts = (a["ffn_gate_weight"], a["ffn_ln_gamma"], a["ffn_ln_beta"], a["ffn_wi"], a["ffn_wo"], slots, results)

    attention(nc, tiles(a["attn_a_x"]), a["attn_a_w_attn"], a["attn_a_b_attn"], a["attn_a_w_proj"],
              a["attn_a_b_proj"], nc.dram_tensor("parts", (2 * KC, 3, P, T), BF16, kind="Internal").ap(), x_attended)
    mixture(nc, 0, x_attended, *experts, x_mixed, clear_slots=True)
    rw = {k.removeprefix("attn_b_"): v for k, v in a.items() if k.startswith("attn_b_")}
    prepare(nc, x_mixed, {m: rw["x_" + m] for m in MIXES}, rw["k_k"], rw["k_a"], rw["r_k"].rearrange("h d -> (h d)"),
            {"r": rw["W_r"], "k": rw["W_k"], "v": rw["W_v"]}, rw["w_lora_a"], rw["w_lora_b"], rw["w_lora_bias"],
            rw["a_lora_a"], rw["a_lora_b"], rw["a_lora_bias"], rw["g_lora_a"], rw["g_lora_b"], rw["g_lora_bias"],
            packed, gate, bonus)
    recurrence(nc, packed.rearrange("(b n) p (h f) -> b (n p) h f", b=BATCH, h=HEADS),
               o.rearrange("(b n) p (h d) -> b (n p) h d", b=BATCH, h=HEADS))
    finish(nc, x_mixed, o, gate, bonus, rw["gn_weight"], rw["gn_bias"], rw["W_o"], x_recurred)
    mixture(nc, 1, x_recurred, *experts, tiles(out), clear_slots=False)


_INS = ["attn_a_x", "attn_a_w_attn", "attn_a_b_attn", "attn_a_w_proj", "attn_a_b_proj",
        "attn_b_x_r", "attn_b_x_w", "attn_b_x_k", "attn_b_x_v", "attn_b_x_a", "attn_b_k_k", "attn_b_k_a",
        "attn_b_r_k", "attn_b_W_r", "attn_b_W_k", "attn_b_W_v", "attn_b_W_o", "attn_b_w_lora_a", "attn_b_w_lora_b",
        "attn_b_w_lora_bias", "attn_b_a_lora_a", "attn_b_a_lora_b", "attn_b_a_lora_bias", "attn_b_g_lora_a",
        "attn_b_g_lora_b", "attn_b_g_lora_bias", "attn_b_gn_weight", "attn_b_gn_bias",
        "ffn_gate_weight", "ffn_ln_gamma", "ffn_ln_beta", "ffn_wi", "ffn_wo"]


def kernel(**inputs):
    import concourse.bacc as _bacc
    from concourse.bass_utils import run_bass_kernel_spmd as _run

    nc = _bacc.Bacc("TRN2", target_bir_lowering=False, num_devices=1)
    arrays, args = {}, {}
    for name in _INS:
        array = np.ascontiguousarray(inputs["L0_" + name])
        arrays[f"in_{name}"] = array
        args[name] = nc.dram_tensor(f"in_{name}", array.shape, mybir.dt.from_np(array.dtype),
                                    kind="ExternalInput").ap()
    out = nc.dram_tensor("out_x", inputs["L0_attn_a_x"].shape, F32, kind="ExternalOutput").ap()
    program(nc, args, out)
    return _run(nc, [arrays], core_ids=[0]).results[0]["out_x"]
```

```python
from contextlib import ExitStack, contextmanager

import numpy as np

import concourse.bass as bass
from concourse import mybir

F32 = mybir.dt.float32
BF16 = mybir.dt.bfloat16
I32 = mybir.dt.int32
U32 = mybir.dt.uint32
ALU = mybir.AluOpType
ACT = mybir.ActivationFunctionType
AX = mybir.AxisListType

P = 128
BATCH, T, C = 8, 1024, 256
TILES = T // P
NT = BATCH * TILES
KC = C // P
HEADS, D = 16, 16
GROUP = 4
PAD = 32
BANK = 512
SLOTS = 3
LN_EPS = 1e-5
MASKED = -1e30


class Tally:

    def __init__(self, eng, sem, base=0):
        self.eng, self.sem, self.base, self.n = eng, sem, base, 0

    def up(self, ins):
        self.n += 1
        return ins.then_inc(self.sem, 1)

    def done(self):
        self.eng.wait_ge(self.sem, 1 + self.base + self.n)

    def link(self, ins):
        self.up(ins)
        self.done()


def spread(row, parts=P):
    return bass.AP(tensor=row.tensor, offset=row.offset, ap=[[0, parts], *row.ap])


@contextmanager
def semaphores(nc, prefix):
    made = []

    def sem(name, start=1):
        made.append(nc.alloc_semaphore(name=prefix + name))
        if start:
            nc.gpsimd.sem_inc(made[-1], start)
        return made[-1]

    yield sem
    nc.clear_and_free_semaphores(made)
    nc.all_engine_barrier()




GROUPS = HEADS // GROUP
HALF_TILES = TILES // 2
HALF_HEADS = HEADS // 2
QK_ORDER = (0, 2, 1, 3)


def maxima(g):
    return [("maxima", (h, qt)) for qt in reversed(range(TILES)) for h in range(GROUP * g, GROUP * g + GROUP)]


def weights(g):
    return [("weights", (h, kt)) for kt in range(TILES) for h in range(GROUP * g, GROUP * g + GROUP)]


LEFT = 9
LEAD = 12


def attention_start():
    plan = [("normalise", 0), ("turn_x", 0), ("turn_x", 1)]
    for n in range(4):
        plan += [("project_qk", n), ("split", n), ("third_part", n)]
    return (plan + maxima(0) + [("turn_max", 0), ("project_v", 0), ("project_v", 1)]
            + maxima(1)[:LEAD])


def attention_turn(ahead):
    beside = [job for g in range(1, GROUPS) for job in maxima(g)]
    if ahead:
        beside += [("+" + stage, what) for stage, what in maxima(0) + maxima(1)[:LEAD]]
    beside = beside[LEAD:]
    left = beside[len(beside) - LEFT:] if ahead else []
    beside = beside[:len(beside) - len(left)]
    of_group = GROUP * TILES
    extra = {}

    def put(g, n, *jobs):
        extra.setdefault(g * of_group + n, []).extend(jobs)

    for g in range(1, GROUPS):
        put(g, 3, ("values", (g - 1, TILES - 1)), ("copy_out", g - 1))
        put(g, 7, ("turn_out", g - 1))
        put(g - 1, of_group - 1 - LEAD, ("turn_max", g))
    if ahead:
        put(0, 4, ("+normalise", 0))
        put(0, 20, ("+turn_x", 0), ("+turn_x", 1))
        for n in range(4):
            at = 8 + 10 * (n % 2)
            put(1 + n // 2, at, ("+project_qk", n))
            put(1 + n // 2, at + 2, ("+split", n))
            put(1 + n // 2, at + 6, ("+third_part", n))
        put(GROUPS - 1, of_group - 1 - LEAD, ("+turn_max", 0))
    plan = []
    for at, job in enumerate(job for g in range(GROUPS) for job in weights(g)):
        g, n = divmod(at, of_group)
        plan.append(job)
        if at < len(beside):
            plan.append(beside[at])
        plan += extra.get(at, [])
        if n % GROUP == GROUP - 1 and n > GROUP:
            plan.append(("values", (g, n // GROUP - 1)))
    plan += [("values", (GROUPS - 1, TILES - 1)), ("copy_out", GROUPS - 1)]
    if ahead:
        plan += [("+project_v", 0)]
    plan += [("turn_out", GROUPS - 1)]
    if ahead:
        plan += [("+project_v", 1)]
    third = len(left) // 3
    return (plan + left[:third] + [("turn_o", c) for c in range(KC)] + left[third:2 * third]
            + [("project_o", half) for half in range(2)] + left[2 * third:])


SLOT_USER = {"turn_x": "act", "project_qk": "act", "project_v": "dve", "maxima": "dve", "turn_max": "act",
             "weights": "act", "turn_out": "dve", "turn_o": "act", "project_o": "dve"}


class Plan:

    def __init__(self, jobs, users, slots):
        self.uses, self.place, self.jobs = [0] * slots, {}, []
        n = 0
        for stage, what in jobs:
            if stage.lstrip("+") in users:
                s = n % slots
                n += 1
                self.place[stage, what] = (s, self.uses[s])
                self.jobs.append((stage, what, s, self.uses[s]))
                self.uses[s] += 1
            else:
                self.jobs.append((stage, what, None, None))


class Slots:

    def __init__(self, plan, before, filled, emptied):
        self.plan, self.before, self.filled, self.emptied = plan, before, filled, emptied

    def wait_empty(self, eng, s, use):
        eng.wait_ge(self.emptied[s], 1 + self.before[s] + use)

    def wait_filled(self, eng, s, use):
        eng.wait_ge(self.filled[s], 1 + self.before[s] + use + 1)

    def wait_read(self, eng, *uses, alone=False):
        latest = {}
        for job in uses:
            s, use = self.plan.place[job]
            latest[s] = max(latest.get(s, 0), use + 1)
        for s, use in latest.items():
            eng.wait_ge(self.emptied[s], 1 + self.before[s] + use)
            if alone:
                eng.nop(nofuse=True)


def attention(nc, x_in, w_attn, b_attn, w_proj, b_proj, parts_dram, x_out):
    start = Plan(attention_start(), SLOT_USER, SLOTS)
    turn = Plan(attention_turn(True), SLOT_USER, SLOTS)
    last_turn = Plan(attention_turn(False), SLOT_USER, SLOTS)
    with ExitStack() as ctx:
        def sb(name, shape, dt=F32):
            return ctx.enter_context(nc.sbuf_tensor("at_" + name, shape, dt))

        sem = ctx.enter_context(semaphores(nc, "at_"))

        slot = [ctx.enter_context(nc.psum_tensor(f"at_slot{s}", [P, 2 * BANK], F32)) for s in range(SLOTS)]
        values = ctx.enter_context(nc.psum_tensor("at_values", [P, T], F32))

        w_qkv = sb("w_qkv", [P, KC, 3 * C])
        w_o = sb("w_o", [P, KC, C])
        bias_qk = sb("bias_qk", [P, 2 * KC])
        bias_v = sb("bias_v", [P, C])
        bias_o = sb("bias_o", [P, C])
        ident = sb("ident", [P, P])
        ident_bf = sb("ident_bf", [P, P], BF16)
        mask_q = sb("mask_q", [P, P], BF16)
        mask_k = sb("mask_k", [P, P], BF16)
        x = sb("x", [P, TILES, C])
        x_kept = sb("x_kept", [P, TILES, C])
        o_rows = sb("o_rows", [P, TILES, C])
        stats = sb("stats", [P, TILES, 6])
        mean_var = sb("mean_var", [P, TILES, 2])
        std = sb("std", [P, TILES])
        rstd = sb("rstd", [P, TILES])
        turned = sb("turned", [P, KC, T])
        turned_o = sb("turned_o", [P, KC, T])
        qk = sb("qk", [P, 2, T])
        rest = sb("rest", [P, 2, T])
        parts = sb("parts", [P, 2, 3, T], BF16)
        q_stack = sb("q_stack", [P, HEADS, T], BF16)
        k_stack = sb("k_stack", [P, HEADS, T], BF16)
        v_rows = sb("v_rows", [P, TILES, HEADS, PAD])
        neg_max = sb("neg_max", [P, TILES, HEADS])
        max_rest = sb("max_rest", [P, TILES, GROUP])
        max_part = sb("max_part", [P, TILES, 3, GROUP], BF16)
        max_rows = sb("max_rows", [3 * GROUP, T], BF16)
        NPROB = 2 * GROUP
        prob = sb("prob", [P, NPROB, T])
        out_t = sb("out_t", [P, T])
        inv_sum = sb("inv_sum", [P, TILES, GROUP])

        consts = sem("consts")
        w_in = sem("w_in")
        bias_ready = sem("bias_ready")
        x_loaded = sem("x_loaded")
        x_kept_in = sem("x_kept_in")
        start_chain = sem("start_chain")
        heads_chain = sem("heads_chain")
        max_chain = sem("max_chain")
        var_ready = sem("var_ready")
        std_ready = sem("std_ready")
        xn_ready = sem("xn_ready")
        with_bias = sem("with_bias")
        filled = [sem(f"filled{s}") for s in range(SLOTS)]
        emptied = [sem(f"emptied{s}") for s in range(SLOTS)]
        qk_ready = sem("qk_ready")
        rest_ready = sem("rest_ready")
        part2_ready = sem("part2_ready")
        part3_ready = sem("part3_ready")
        parts_out = [sem(f"parts_out{k}") for k in range(2)]
        stacked = [sem(f"stacked{k}") for k in range(2)]
        max_ready = sem("max_ready")
        max_stacked = sem("max_stacked")
        prob_used = sem("prob_used")
        out_t_ready = sem("out_t_ready")
        stored = sem("stored")

        ctx.enter_context(nc.allow_non_contiguous_dma(reason="bias columns"))
        nc.all_engine_barrier()
        block = ctx.enter_context(nc.Block())
        STACK_DMAS = 2 * 6

        def counts(plan, before):
            return Slots(plan, before, filled, emptied)

        def run(eng, part):
            part(counts(start, [0] * SLOTS), None, 0)
            with eng.Fori(0, BATCH - 1) as b:
                part(counts(turn, [start.uses[s] + b * turn.uses[s] for s in range(SLOTS)]), b, b + 1)
            part(counts(last_turn, [start.uses[s] + (BATCH - 1) * turn.uses[s] for s in range(SLOTS)]),
                 BATCH - 1, None)

        @block.gpsimd
        def _(pool):
            own = Tally(pool, consts)
            own.up(pool.memset(ident[:], 0.0))
            own.up(pool.memset(mask_q[:], 0.0))
            own.up(pool.memset(mask_k[:], 0.0))
            own.up(pool.memset(v_rows[:], 0.0))
            own.up(pool.memset(k_stack[:], 1.0))
            own.done()
            own.up(pool.affine_select(out=ident[:], in_=ident[:], compare_op=ALU.not_equal, fill=1.0, base=0,
                                      pattern=[[-1, P]], channel_multiplier=1))
            own.up(pool.affine_select(out=mask_q[:], in_=mask_q[:], compare_op=ALU.is_ge, fill=MASKED, base=0,
                                      pattern=[[-1, P]], channel_multiplier=1))
            own.up(pool.affine_select(out=mask_k[:], in_=mask_k[:], compare_op=ALU.is_ge, fill=MASKED, base=0,
                                      pattern=[[1, P]], channel_multiplier=-1))
            own.up(pool.memset(v_rows[:, :, :, D], 1.0))
            own.done()
            own.up(pool.tensor_copy(ident_bf[:], ident[:]))
            assert own.n == 10
            pool.wait_ge(w_in, 1 + 16 * 5)

            def part(slots, b, f):
                for stage, what, s, use in slots.plan.jobs:
                    if stage.lstrip("+") == "split":
                        pool.wait_ge(rest_ready, 1 + f * 4 + what + 1)
                        pool.nop(nofuse=True)
                        pool.tensor_copy(parts[:, what % 2, 1, :], rest[:, what % 2, :]).then_inc(part2_ready, 1)
                    elif stage == "copy_out" and what == 0:
                        pool.wait_ge(x_kept_in, 1 + (b + 1) * 16)
                        pool.tensor_tensor(x_kept[:], x_kept[:],
                                           bias_o[:].unsqueeze(1).broadcast_to([P, TILES, C]), ALU.add)\
                            .then_inc(with_bias, 1)

            run(pool, part)

        @block.sync
        def _(sp):
            sp.dma_start(w_qkv[:], w_attn.rearrange("(k p) n -> p k n", p=P)).then_inc(w_in, 16)
            sp.dma_start(w_o[:], w_proj.rearrange("(k p) n -> p k n", p=P)).then_inc(w_in, 16)
            sp.dma_start(bias_qk[:], b_attn[0:2 * C].rearrange("(k p) -> p k", p=P)).then_inc(w_in, 16)
            sp.dma_start(bias_v[:], spread(b_attn[2 * C:3 * C])).then_inc(w_in, 16)
            sp.dma_start(bias_o[:], spread(b_proj)).then_inc(w_in, 16)
            sp.wait_ge(consts, 1 + 5)

            def rows(ap, b, first=0, n=TILES):
                return ap[bass.ds(b * TILES + first, n)].rearrange("n p c -> p n c")

            def load_stack(f, half):
                for k in range(2):
                    sp.wait_ge(parts_out[k], 1 + 16 * (f * 2 + half + 1))
                    sp.nop(nofuse=True)
                for stack, oc, order in ((q_stack, half, (0, 0, 0, 1, 1, 2)), (k_stack, KC + half, (0, 1, 2, 0, 1, 0))):
                    for blk, k in enumerate(order):
                        sp.dma_start(stack[blk * D:(blk + 1) * D, half * HALF_HEADS:(half + 1) * HALF_HEADS, :],
                                     parts_dram[oc, k].rearrange("(h d) t -> d h t", d=D)).then_inc(stacked[half], 16)

            def store_parts(f, n):
                sp.wait_ge(part3_ready, 1 + f * 4 + n + 1)
                sp.nop(nofuse=True)
                sp.wait_ge(stacked[n // 2], 1 + f * 16 * STACK_DMAS)
                sp.nop(nofuse=True)
                sp.dma_start(parts_dram[QK_ORDER[n]].rearrange("k p t -> p k t"), parts[:, n % 2, :, :])\
                  .then_inc(parts_out[n % 2], 16)

            def part(slots, b, f):
                if b is not None:
                    sp.wait_ge(stored, 1 + b * 32)
                    sp.nop(nofuse=True)
                    sp.dma_start(x_kept[:], rows(x_in, b)).then_inc(x_kept_in, 16)
                if f is not None:
                    if b is not None:
                        sp.wait_ge(part2_ready, 1 + f * 4)
                        sp.nop(nofuse=True)
                    sp.dma_start(x[:], rows(x_in, f)).then_inc(x_loaded, 16)
                    for n in range(2):
                        store_parts(f, n)
                    if b is not None:
                        slots.wait_read(sp, *[("weights", (h, TILES - 1)) for h in range(GROUP, 2 * GROUP)], alone=True)
                    load_stack(f, 0)
                    for n in range(2, 4):
                        store_parts(f, n)
                    if b is not None:
                        slots.wait_read(sp, *[("weights", (h, TILES - 1)) for h in range(HEADS - GROUP, HEADS)],
                                        alone=True)
                    load_stack(f, 1)
                if b is not None:
                    for half in range(2):
                        slots.wait_read(sp, ("project_o", half), alone=True)
                        sp.dma_start(rows(x_out, b, half * HALF_TILES, HALF_TILES),
                                     x_kept[:, half * HALF_TILES:(half + 1) * HALF_TILES, :]).then_inc(stored, 16)

            run(sp, part)
            sp.wait_ge(stored, 1 + 16 * 2 * BATCH)

        @block.tensor
        def _(pe):
            pe.wait_ge(consts, 1 + 10)
            pe.wait_ge(w_in, 1 + 16 * 5)

            def part(slots, b, f):
                for full_stage, what, s, use in slots.plan.jobs:
                    stage = full_stage.lstrip("+")
                    q = f if full_stage != stage or b is None else b
                    if s is not None:
                        ps = slot[s]
                        slots.wait_empty(pe, s, use)
                    if stage == "turn_x":
                        if what == 0:
                            pe.wait_ge(xn_ready, 1 + (q + 1) * TILES)
                        for t in range(TILES):
                            last = pe.transpose(ps[:, t * P:(t + 1) * P], x[:, t, what * P:(what + 1) * P], ident[:])
                    elif stage == "project_qk":
                        if what == 0:
                            mark = full_stage[:-len(stage)]
                            slots.wait_read(pe, (mark + "turn_x", 0), (mark + "turn_x", 1))
                        oc = QK_ORDER[what]
                        for half in range(2):
                            for k in range(KC):
                                last = pe.matmul(ps[:, half * BANK:(half + 1) * BANK],
                                                 w_qkv[:, k, oc * P:(oc + 1) * P],
                                                 turned[:, k, half * BANK:(half + 1) * BANK],
                                                 start=(k == 0), stop=(k == KC - 1))
                    elif stage == "project_v":
                        for n in range(HALF_TILES):
                            t = HALF_TILES * what + n
                            for k in range(KC):
                                last = pe.matmul(ps[:, n * C:(n + 1) * C], turned[:, k, t * P:(t + 1) * P],
                                                 w_qkv[:, k, 2 * C:3 * C], start=(k == 0), stop=(k == KC - 1))
                    elif stage == "maxima":
                        h, qt = what
                        if h % HALF_HEADS == 0 and qt == TILES - 1:
                            pe.wait_ge(stacked[h // HALF_HEADS], 1 + (q + 1) * 16 * STACK_DMAS)
                        keys = (qt + 1) * P
                        for k0 in range(0, keys, BANK):
                            k1 = min(k0 + BANK, keys)
                            pe.matmul(ps[:, k0:k1], q_stack[0:6 * D, h, qt * P:(qt + 1) * P],
                                      k_stack[0:6 * D, h, k0:k1], start=True, stop=True)
                        last = pe.matmul(ps[:, keys - P:keys], ident_bf[:], mask_q[:], start=False, stop=True,
                                         skip_group_check=True)
                    elif stage == "turn_max":
                        pe.wait_ge(max_ready, 1 + q * GROUPS + what + 1)
                        rows = ps[:].bitcast(BF16)
                        for t in range(TILES):
                            last = pe.transpose(rows[0:3 * GROUP, t * P:(t + 1) * P],
                                                max_part[:, t, :, :].rearrange("p k g -> p (k g)"), ident_bf[:])
                    elif stage == "weights":
                        h, kt = what
                        if (h % GROUP, kt) == (0, 0):
                            pe.wait_ge(max_stacked, 1 + (q * GROUPS + h // GROUP + 1) * 48)
                        q_from = kt * P
                        for q0 in range(0, T, BANK):
                            if q0 + BANK <= q_from:
                                continue
                            lo = max(q0, q_from)
                            last = pe.matmul(ps[:, lo:q0 + BANK], k_stack[0:6 * D + 3, h, kt * P:(kt + 1) * P],
                                             q_stack[0:6 * D + 3, h, lo:q0 + BANK], start=True, stop=True)
                            if lo == q_from:
                                last = pe.matmul(ps[:, lo:lo + P], ident_bf[:], mask_k[:], start=False, stop=True,
                                                 skip_group_check=True)
                    elif stage == "values":
                        g, kt = what
                        slots.wait_read(pe, *[("weights", (GROUP * g + j, kt)) for j in range(GROUP)])
                        if kt == 0:
                            pe.wait_ge(out_t_ready, 1 + q * GROUPS + g)
                        for q0 in range(0, T, BANK):
                            q1 = q0 + BANK
                            if q1 <= kt * P:
                                continue
                            lo = max(q0, kt * P)
                            for j in range(GROUP):
                                n = (g * TILES + kt) * GROUP + j
                                last = pe.matmul(values[PAD * j:PAD * j + PAD, lo:q1],
                                                 v_rows[:, kt, GROUP * g + j, :], prob[:, n % NPROB, lo:q1],
                                                 start=(kt == 0), stop=(q1 == (kt + 1) * P),
                                                 tile_position=(0, PAD * j))
                        last.then_inc(prob_used, 1)
                    elif stage == "turn_out":
                        pe.wait_ge(out_t_ready, 1 + q * GROUPS + what + 1)
                        for t in range(TILES):
                            last = pe.transpose(ps[:, t * P:(t + 1) * P], out_t[:, t * P:(t + 1) * P], ident[:])
                    elif stage == "turn_o":
                        if what == 0:
                            slots.wait_read(pe, *[("turn_out", g) for g in range(GROUPS)])
                        for t in range(TILES):
                            last = pe.transpose(ps[:, t * P:(t + 1) * P], o_rows[:, t, what * P:(what + 1) * P],
                                                ident[:])
                    elif stage == "project_o":
                        if what == 0:
                            slots.wait_read(pe, ("turn_o", 0), ("turn_o", 1))
                        for n in range(HALF_TILES):
                            t = HALF_TILES * what + n
                            for k in range(KC):
                                last = pe.matmul(ps[:, n * C:(n + 1) * C], turned_o[:, k, t * P:(t + 1) * P],
                                                 w_o[:, k, :], start=(k == 0), stop=(k == KC - 1))
                    if s is not None:
                        last.then_inc(filled[s], 1)

            run(pe, part)

        @block.scalar
        def _(act):
            act.wait_ge(w_in, 1 + 16 * 5)
            act.wait_ge(consts, 1 + 10)
            act.activation(bias_qk[:, 0:KC], bias_qk[:, 0:KC], ACT.Copy, scale=D ** -0.5).then_inc(bias_ready, 1)
            act.wait_ge(bias_ready, 1 + 1)

            def part(slots, b, f):
                for full_stage, what, s, use in slots.plan.jobs:
                    stage = full_stage.lstrip("+")
                    q = f if full_stage != stage or b is None else b
                    if stage == "normalise":
                        act.wait_ge(var_ready, 1 + q + 1)
                        act.activation(std[:], mean_var[:, :, 1], ACT.Sqrt).then_inc(std_ready, 1)
                    elif stage == "copy_out":
                        act.wait_ge(prob_used, 1 + (q * GROUPS + what + 1) * TILES)
                        if what:
                            slots.wait_read(act, ("turn_out", what - 1))
                        act.activation(out_t[:], values[:], ACT.Copy).then_inc(out_t_ready, 1)
                    if SLOT_USER.get(stage) != "act":
                        continue
                    ps = slot[s]
                    slots.wait_filled(act, s, use)
                    if stage in ("turn_x", "turn_o"):
                        dst = turned if stage == "turn_x" else turned_o
                        act.activation(dst[:, what, :], ps[:], ACT.Copy).then_inc(emptied[s], 1)
                    elif stage == "project_qk":
                        k, oc = what % 2, QK_ORDER[what]
                        act.wait_ge(parts_out[k], 1 + 16 * (q * 2 + what // 2))
                        act.activation(qk[:, k, :], ps[:], ACT.Identity, bias=bias_qk[:, oc:oc + 1],
                                       scale=D ** -0.5 if oc < KC else 1.0).then_inc(emptied[s], 1)
                        slots.wait_read(act, (full_stage, what))
                        act.activation(parts[:, k, 0, :], qk[:, k, :], ACT.Copy).then_inc(qk_ready, 1)
                    elif stage == "turn_max":
                        act.wait_ge(max_stacked, 1 + (q * GROUPS + what) * 48)
                        act.activation(max_rows[:], ps[:].bitcast(BF16)[0:3 * GROUP, 0:T], ACT.Copy)\
                           .then_inc(emptied[s], 1)
                        slots.wait_read(act, (full_stage, what))
                        for k in range(3):
                            act.dma_start(q_stack[6 * D + k:6 * D + k + 1, GROUP * what:GROUP * what + GROUP, :],
                                          max_rows[GROUP * k:GROUP * k + GROUP, :]).then_inc(max_stacked, 16)
                    elif stage == "weights":
                        h, kt = what
                        n = ((h // GROUP) * TILES + kt) * GROUP + h % GROUP
                        if n % GROUP == 0:
                            act.wait_ge(prob_used, 1 + q * GROUPS * TILES + max(n // GROUP - 1, 0))
                        act.activation(prob[:, n % NPROB, kt * P:T], ps[:, kt * P:T], ACT.Exp).then_inc(emptied[s], 1)

            run(act, part)

        @block.vector
        def _(dve):
            dve.wait_ge(consts, 1 + 10)
            dve.wait_ge(w_in, 1 + 16 * 5)
            START = 2 * TILES + 1

            def part(slots, b, f):
                in_start = Tally(dve, start_chain, 0 if f is None else f * START)
                in_heads = Tally(dve, heads_chain, 0 if b is None else b * GROUPS)
                for full_stage, what, s, use in slots.plan.jobs:
                    stage = full_stage.lstrip("+")
                    mark = full_stage[:-len(stage)]
                    q = f if full_stage != stage or b is None else b
                    if stage == "normalise":
                        dve.wait_ge(x_loaded, 1 + (q + 1) * 16)
                        for t in range(TILES):
                            in_start.up(dve.bn_stats(stats[:, t, :], x[:, t, :]))
                        in_start.done()
                        dve.nop(nofuse=True)
                        for t in range(TILES):
                            in_start.up(dve.bn_aggr(mean_var[:, t, :], stats[:, t, :]))
                        in_start.done()
                        dve.tensor_scalar(mean_var[:, :, 1], mean_var[:, :, 1], LN_EPS, None, ALU.add)\
                           .then_inc(var_ready, 1)
                        dve.wait_ge(std_ready, 1 + q + 1)
                        in_start.link(dve.reciprocal(rstd[:], std[:]))
                        for t in range(TILES):
                            dve.tensor_scalar(x[:, t, :], x[:, t, :], mean_var[:, t, 0:1], rstd[:, t:t + 1],
                                              ALU.subtract, ALU.mult).then_inc(xn_ready, 1)
                    elif stage == "split":
                        k = what % 2
                        dve.wait_ge(qk_ready, 1 + q * 4 + what + 1)
                        dve.tensor_tensor(rest[:, k, :], qk[:, k, :], parts[:, k, 0, :], ALU.subtract)\
                           .then_inc(rest_ready, 1)
                    elif stage == "third_part":
                        k = what % 2
                        dve.wait_ge(part2_ready, 1 + q * 4 + what + 1)
                        dve.tensor_tensor(parts[:, k, 2, :], rest[:, k, :], parts[:, k, 1, :], ALU.subtract)\
                           .then_inc(part3_ready, 1)
                    elif stage == "turn_max":
                        heads = slice(GROUP * what, GROUP * what + GROUP)
                        own = Tally(dve, max_chain, (q * GROUPS + what) * 3)
                        slots.wait_read(dve, *[(mark + "maxima", (h, 0)) for h in range(heads.start, heads.stop)])
                        dve.wait_ge(max_stacked, 1 + (q * GROUPS + what) * 48)
                        own.link(dve.tensor_copy(max_part[:, :, 0, :], neg_max[:, :, heads]))
                        own.link(dve.tensor_tensor(max_rest[:], neg_max[:, :, heads], max_part[:, :, 0, :],
                                                   ALU.subtract))
                        own.link(dve.tensor_copy(max_part[:, :, 1, :], max_rest[:]))
                        dve.tensor_tensor(max_part[:, :, 2, :], max_rest[:], max_part[:, :, 1, :],
                                          ALU.subtract).then_inc(max_ready, 1)
                    if SLOT_USER.get(stage) != "dve":
                        continue
                    ps = slot[s]
                    slots.wait_filled(dve, s, use)
                    if stage == "project_v":
                        if b is not None:
                            dve.wait_ge(prob_used, 1 + (b + 1) * GROUPS * TILES)
                        for n in range(HALF_TILES):
                            v_chunk = dve.tensor_tensor(
                                v_rows[:, HALF_TILES * what + n, :, 0:D],
                                ps[:, n * C:(n + 1) * C].rearrange("p (h d) -> p h d", d=D),
                                bias_v[:].rearrange("p (h d) -> p h d", d=D), ALU.add)
                        v_chunk.then_inc(emptied[s], 1)
                    elif stage == "maxima":
                        h, qt = what
                        dve.tensor_reduce(neg_max[:, qt, h:h + 1], ps[:, 0:(qt + 1) * P], AX.X, ALU.max, negate=True)\
                           .then_inc(emptied[s], 1)
                    elif stage == "turn_out":
                        rows = ps[:].rearrange("p (t h d) -> p t h d", t=TILES, d=PAD)
                        in_heads.link(dve.reciprocal(inv_sum[:], rows[:, :, :, D]))
                        dve.tensor_tensor(
                            o_rows[:].rearrange("p t (h d) -> p t h d", d=D)[:, :, GROUP * what:GROUP * what + GROUP, :],
                            rows[:, :, :, 0:D], inv_sum[:].unsqueeze(3).broadcast_to([P, TILES, GROUP, D]),
                            ALU.mult).then_inc(emptied[s], 1)
                    elif stage == "project_o":
                        dve.wait_ge(with_bias, 1 + b + 1)
                        tiles_of = x_kept[:, HALF_TILES * what:HALF_TILES * (what + 1), :]
                        dve.tensor_tensor(tiles_of, ps[:].rearrange("p (n c) -> p n c", c=C), tiles_of, ALU.add)\
                           .then_inc(emptied[s], 1)

            run(dve, part)


EXPERTS, HIDDEN, CAPACITY = 8, 1024, 512
KEPT = EXPERTS * CAPACITY
HC = HIDDEN // P
ST = CAPACITY // P


def mixture(nc, n, x_in, gate_w, gamma, beta, w_in, w_out, slots_dram, results_dram, x_out, clear_slots):
    with ExitStack() as outer:
        def sb(name, shape, dt=F32, ctx=outer):
            return ctx.enter_context(nc.sbuf_tensor(f"f{n}_{name}", shape, dt))

        def psum(ctx, name, shape, dt=F32):
            return ctx.enter_context(nc.psum_tensor(f"f{n}_{name}", shape, dt))

        sem = outer.enter_context(semaphores(nc, f"f{n}_"))

        outer.enter_context(nc.allow_non_contiguous_dma(reason="gate weights by channel"))
        base = sb("base", [P, NT, C])
        weight = sb("weight", [P, NT])
        fetch_at = sb("fetch_at", [P, NT], I32)
        send_to = sb("send_to", [P, NT], I32)
        ident = sb("ident", [P, P])
        up_w = [sb(f"up_w{k}", [P, KC, HIDDEN]) for k in range(2)]
        down_w = [sb(f"down_w{k}", [P, HC, C]) for k in range(2)]
        consts = sem("consts")
        weights_in = [sem(f"weights_in{k}") for k in range(2)]

        def load_weights(eng, e, k):
            eng.dma_start(up_w[k][:], w_in[bass.ds(e, 1)].rearrange("a (k p) n -> (a p) k n", p=P))\
               .then_inc(weights_in[k], 16)
            eng.dma_start(down_w[k][:], w_out[bass.ds(e, 1)].rearrange("a (k p) n -> (a p) k n", p=P))\
               .then_inc(weights_in[k], 16)

        with ExitStack() as ctx:
            tokens = sb("tokens", [P, NT, C], ctx=ctx)
            u = sb("u", [P, TILES, C], ctx=ctx)
            tok = [sb(f"tok{j}", [P, TILES, C], ctx=ctx) for j in range(2)]
            turned = sb("turned", [P, KC, T], ctx=ctx)
            gate = sb("gate", [P, KC, EXPERTS], ctx=ctx)
            gamma_b = sb("gamma_b", [P, C], ctx=ctx)
            beta_b = sb("beta_b", [P, C], ctx=ctx)
            stats = sb("stats", [P, TILES, 6], ctx=ctx)
            mean_var = sb("mean_var", [P, 2, TILES, 2], ctx=ctx)
            std = sb("std", [P, 2, TILES], ctx=ctx)
            rstd = sb("rstd", [P, 2, TILES], ctx=ctx)
            logits = sb("logits", [P, NT, EXPERTS], ctx=ctx)
            before = sb("before", [P, P], ctx=ctx)
            ones = sb("ones", [P, P], ctx=ctx)
            order = sb("order", [P, EXPERTS], ctx=ctx)
            onehot = sb("onehot", [P, NT, EXPERTS], ctx=ctx)
            work = sb("work", [P, NT, EXPERTS], ctx=ctx)
            tops = sb("tops", [P, NT], ctx=ctx)
            first = sb("first", [P, NT], ctx=ctx)
            total = sb("total", [P, NT], ctx=ctx)
            rank = sb("rank", [P, NT], ctx=ctx)
            keep = sb("keep", [P, NT], ctx=ctx)
            place = sb("place", [P, NT], ctx=ctx)
            totals = sb("totals", [P, NT, EXPERTS], ctx=ctx)
            zeros = totals[:].rearrange("p t e -> p (t e)")
            zero_rows = P * NT * EXPERTS // C
            earlier = u[:, 0:NT * EXPERTS // C, :].rearrange("p n (t e) -> p (n t) e", e=EXPERTS)
            ps_turn = [psum(ctx, f"turn{k}", [P, T]) for k in range(KC)]
            ps_gate = psum(ctx, "ps_gate", [P, TILES * EXPERTS])
            ps_before = psum(ctx, "ps_before", [P, NT * EXPERTS])
            ps_total = psum(ctx, "ps_total", [P, NT * EXPERTS])

            x_loaded = sem("x_loaded")
            loaded = sem("loaded")
            cleared = sem("cleared")
            chain = sem("chain")
            var_ready = sem("var_ready")
            std_ready = sem("std_ready")
            scaled = sem("scaled")
            tok_ready = sem("tok_ready")
            base_ready = sem("base_ready")
            turn_ready = sem("turn_ready")
            turned_ready = sem("turned_ready")
            kept = sem("kept")
            gate_ready = sem("gate_ready")
            logits_ready = sem("logits_ready")
            shifted = sem("shifted")
            exp_ready = sem("exp_ready")
            onehot_ready = sem("onehot_ready")
            counts_ready = sem("counts_ready")
            routed = sem("routed")
            sent = sem("sent", start=0)

            nc.all_engine_barrier()
            block = ctx.enter_context(nc.Block())

            @block.sync
            def _(sp):
                def load_x(b):
                    sp.dma_start(base[:, bass.ds(b * TILES, TILES), :],
                                 x_in[bass.ds(b * TILES, TILES)].rearrange("n p c -> p n c")).then_inc(x_loaded, 16)

                load_x(0)
                sp.dma_start(gamma_b[:], spread(gamma)).then_inc(loaded, 16)
                sp.dma_start(beta_b[:], spread(beta)).then_inc(loaded, 16)
                for k in range(KC):
                    sp.dma_start(gate[:, k, :], gate_w[:, k * P:(k + 1) * P].rearrange("e p -> p e")).then_inc(loaded, 16)
                with sp.Fori(1, BATCH) as b:
                    sp.wait_ge(x_loaded, 1 + b * 16)
                    sp.nop(nofuse=True)
                    load_x(b)
                if clear_slots:
                    sp.wait_ge(consts, 1 + 1)
                    sp.nop(nofuse=True)
                    for k in range(KEPT // zero_rows):
                        sp.dma_start(slots_dram[k * zero_rows:(k + 1) * zero_rows, :]
                                     .rearrange("(p r) c -> p (r c)", p=P), zeros).then_inc(cleared, 16)
                for k in range(2):
                    load_weights(sp, k, k)

            TURN = 2 * (3 * TILES + 1)

            def sequences(eng, first, part):
                with eng.Fori(0, (BATCH - first) // 2) as i:
                    for j in range(2):
                        part(first + i * 2 + j, (first + j) % 2)
                if (BATCH - first) % 2:
                    part(BATCH - 1, (BATCH - 1) % 2)

            @block.gpsimd
            def _(pool):
                own = Tally(pool, consts)
                own.up(pool.memset(zeros, 0.0))
                own.up(pool.memset(ident[:], 0.0))
                own.up(pool.memset(before[:], 1.0))
                own.up(pool.memset(ones[:], 1.0))
                own.up(pool.iota(fetch_at[:, 0:EXPERTS], pattern=[[-1, EXPERTS]], base=EXPERTS, channel_multiplier=0))
                own.done()
                own.up(pool.affine_select(out=ident[:], in_=ident[:], compare_op=ALU.not_equal, fill=1.0, base=0,
                                          pattern=[[-1, P]], channel_multiplier=1))
                own.up(pool.affine_select(out=before[:], in_=before[:], compare_op=ALU.is_gt, fill=0.0, base=0,
                                          pattern=[[1, P]], channel_multiplier=-1))
                own.up(pool.tensor_copy(order[:], fetch_at[:, 0:EXPERTS]))
                own.done()
                assert own.n == 8
                pool.wait_ge(loaded, 1 + 64)
                beta_wide = beta_b[:].unsqueeze(1).broadcast_to([P, TILES, C])

                def shift(b, j):
                    span = base[:, bass.ds(b * TILES, TILES), :]
                    pool.wait_ge(chain, 1 + b * TURN + TURN // 2)
                    pool.tensor_tensor(span, span, u[:], ALU.add).then_inc(base_ready, 1)
                    pool.wait_ge(scaled, 1 + b + 1)
                    pool.tensor_tensor(tok[j][:], tok[j][:], beta_wide, ALU.add).then_inc(tok_ready, 1)

                sequences(pool, 0, shift)
                pool.wait_ge(routed, 1 + 1)
                pool.wait_ge(kept, 1 + BATCH)
                for t in range(NT):
                    pool.indirect_dma_start(
                        out=slots_dram, out_offset=bass.IndirectOffsetOnAxis(ap=send_to[:, t:t + 1].bitcast(U32), axis=0),
                        in_=tokens[:, t, :], in_offset=None, bounds_check=KEPT - 1, oob_is_err=False)\
                        .then_inc(sent, 16)
                pool.wait_ge(sent, 16 * NT)

            @block.tensor
            def _(pe):
                pe.wait_ge(consts, 1 + 8)
                pe.wait_ge(loaded, 1 + 64)

                def gate_logits(b, j):
                    pe.wait_ge(tok_ready, 1 + b + 1)
                    pe.wait_ge(turned_ready, 1 + b * KC)
                    for k in range(KC):
                        for t in range(TILES):
                            last = pe.transpose(ps_turn[k][:, t * P:(t + 1) * P], tok[j][:, t, k * P:(k + 1) * P],
                                                ident[:])
                        last.then_inc(turn_ready, 1)
                    pe.wait_ge(turned_ready, 1 + b * KC + KC)
                    pe.wait_ge(logits_ready, 1 + b)
                    for t in range(TILES):
                        for k in range(KC):
                            last = pe.matmul(ps_gate[:, t * EXPERTS:(t + 1) * EXPERTS],
                                             turned[:, k, t * P:(t + 1) * P], gate[:, k, :],
                                             start=(k == 0), stop=(k == KC - 1))
                    last.then_inc(gate_ready, 1)

                sequences(pe, 0, gate_logits)
                pe.wait_ge(onehot_ready, 1 + 1)
                chosen = onehot[:].rearrange("p t e -> p (t e)")
                pe.matmul(ps_before[:], before[:], chosen, start=True, stop=True)
                pe.matmul(ps_total[:], ones[:], chosen, start=True, stop=True).then_inc(counts_ready, 1)

            @block.scalar
            def _(act):
                def root(b, k):
                    act.wait_ge(var_ready, 1 + b * 2 + k + 1)
                    act.activation(std[:, k, :], mean_var[:, k, :, 1], ACT.Sqrt).then_inc(std_ready, 1)

                def keep_tokens(b, j):
                    act.wait_ge(gate_ready, 1 + b)
                    for k in range(KC):
                        act.wait_ge(turn_ready, 1 + b * KC + k + 1)
                        act.activation(turned[:, k, :], ps_turn[k][:], ACT.Copy).then_inc(turned_ready, 1)
                    act.activation(tokens[:, bass.ds(b * TILES, TILES), :], tok[j][:], ACT.Copy).then_inc(kept, 1)

                root(0, 0)
                root(0, 1)

                def part(b, j):
                    root(b, 0)
                    root(b, 1)
                    keep_tokens(b - 1, 1 - j)

                sequences(act, 1, part)
                keep_tokens(BATCH - 1, (BATCH - 1) % 2)
                act.wait_ge(shifted, 1 + 1)
                act.activation(work[:], work[:], ACT.Exp).then_inc(exp_ready, 1)

            @block.vector
            def _(dve):
                gamma_wide = gamma_b[:].unsqueeze(1).broadcast_to([P, TILES, C])

                def normalise(own, b, j, k):
                    def src(t):
                        return u[:, t, :] if k else base[:, bass.ds(b * TILES + t, 1), :].rearrange("p a c -> p (a c)")

                    if k == 0:
                        dve.wait_ge(x_loaded, 1 + (b + 1) * 16)
                    for t in range(TILES):
                        own.up(dve.bn_stats(stats[:, t, :], src(t)))
                    own.done()
                    dve.nop(nofuse=True)
                    for t in range(TILES):
                        own.up(dve.bn_aggr(mean_var[:, k, t, :], stats[:, t, :]))
                    own.done()
                    dve.tensor_scalar(mean_var[:, k, :, 1], mean_var[:, k, :, 1], LN_EPS, None, ALU.add)\
                       .then_inc(var_ready, 1)
                    dve.wait_ge(std_ready, 1 + b * 2 + k + 1)
                    own.link(dve.reciprocal(rstd[:, k, :], std[:, k, :]))
                    if k == 0:
                        dve.wait_ge(base_ready, 1 + b)
                    elif not (isinstance(b, int) and b < 2):
                        dve.wait_ge(kept, 1 + b - 1)
                        dve.wait_ge(turn_ready, 1 + (b - 1) * KC)
                    for t in range(TILES):
                        own.up(dve.tensor_scalar((tok[j] if k else u)[:, t, :], src(t), mean_var[:, k, t, 0:1],
                                                 rstd[:, k, t:t + 1], ALU.subtract, ALU.mult))
                    own.done()
                    if k:
                        if isinstance(b, int) and b == 0:
                            dve.wait_ge(loaded, 1 + 64)
                        dve.tensor_tensor(tok[j][:], tok[j][:], gamma_wide, ALU.mult).then_inc(scaled, 1)

                def take_logits(b):
                    dve.wait_ge(gate_ready, 1 + b + 1)
                    dve.tensor_copy(logits[:, bass.ds(b * TILES, TILES), :],
                                    ps_gate[:].rearrange("p (t e) -> p t e", e=EXPERTS)).then_inc(logits_ready, 1)

                own = Tally(dve, chain)
                for b in range(2):
                    for k in range(2):
                        normalise(own, b, b, k)

                def part(b, j):
                    own = Tally(dve, chain, b * TURN)
                    normalise(own, b, j, 0)
                    take_logits(b - 2)
                    normalise(own, b, j, 1)
                    assert own.n == TURN, own.n

                sequences(dve, 2, part)
                for b in range(BATCH - 2, BATCH):
                    take_logits(b)
                dve.wait_ge(consts, 1 + 8)
                own = Tally(dve, chain, BATCH * TURN)
                wide = [P, NT, EXPERTS]
                dve.wait_ge(logits_ready, 1 + BATCH)
                own.link(dve.tensor_reduce(tops[:], logits[:], AX.X, ALU.max))
                tops_wide = tops[:].unsqueeze(2).broadcast_to(wide)
                dve.tensor_tensor(work[:], logits[:], tops_wide, ALU.subtract).then_inc(shifted, 1)
                own.link(dve.tensor_tensor(onehot[:], logits[:], tops_wide, ALU.is_equal))
                own.link(dve.tensor_tensor(onehot[:], onehot[:], order[:].unsqueeze(1).broadcast_to(wide), ALU.mult))
                own.link(dve.tensor_reduce(first[:], onehot[:], AX.X, ALU.max))
                dve.tensor_tensor(onehot[:], onehot[:], first[:].unsqueeze(2).broadcast_to(wide), ALU.is_equal)\
                   .then_inc(onehot_ready, 1)
                dve.wait_ge(exp_ready, 1 + 1)
                own.link(dve.tensor_reduce(total[:], work[:], AX.X, ALU.add))
                own.link(dve.reciprocal(weight[:], total[:]))
                dve.wait_ge(counts_ready, 1 + 1)
                if clear_slots:
                    dve.wait_ge(cleared, 1 + KEPT // zero_rows * 16)
                own.link(dve.tensor_copy(totals[:], ps_total[:].rearrange("p (t e) -> p t e", e=EXPERTS)))
                dve.wait_ge(base_ready, 1 + BATCH)
                for e in range(EXPERTS):
                    own.up(dve.tensor_tensor_scan(earlier[:, :, e], ones[:, 0:NT], totals[:, :, e], 0.0,
                                                  ALU.mult, ALU.add))
                own.done()
                own.link(dve.tensor_tensor(earlier, earlier, totals[:], ALU.subtract))
                own.link(dve.tensor_tensor(earlier, earlier, ps_before[:].rearrange("p (t e) -> p t e", e=EXPERTS),
                                           ALU.add))
                dve.wait_ge(onehot_ready, 1 + 1)
                own.link(dve.tensor_tensor(earlier, earlier, onehot[:], ALU.mult))
                own.link(dve.tensor_reduce(rank[:], earlier, AX.X, ALU.add))
                own.link(dve.tensor_scalar(keep[:], rank[:], float(CAPACITY), None, ALU.is_lt))
                own.link(dve.tensor_scalar(place[:], first[:], -float(CAPACITY), float(EXPERTS * CAPACITY), ALU.mult, ALU.add))
                own.link(dve.tensor_tensor(place[:], place[:], rank[:], ALU.add))
                own.link(dve.tensor_tensor(place[:], place[:], keep[:], ALU.mult))
                own.link(dve.tensor_tensor(weight[:], weight[:], keep[:], ALU.mult))
                own.link(dve.tensor_copy(fetch_at[:], place[:]))
                own.link(dve.tensor_scalar(keep[:], keep[:], -float(KEPT), float(KEPT), ALU.mult, ALU.add))
                own.link(dve.tensor_tensor(place[:], place[:], keep[:], ALU.add))
                dve.tensor_copy(send_to[:], place[:]).then_inc(routed, 1)

        with ExitStack() as ctx:
            rows = [sb(f"rows{k}", [P, ST, C], ctx=ctx) for k in range(2)]
            cols = [sb(f"cols{k}", [P, KC, CAPACITY], ctx=ctx) for k in range(2)]
            hidden = [sb(f"hidden{k}", [P, HC, CAPACITY], ctx=ctx) for k in range(2)]
            result = [sb(f"result{k}", [P, ST, C], ctx=ctx) for k in range(2)]
            ps_cols = psum(ctx, "ps_cols", [P, KC * CAPACITY])
            ps_hid = [psum(ctx, f"ps_hid{k}", [P, 2 * CAPACITY]) for k in range(2)]
            ps_res = psum(ctx, "ps_res", [P, ST * C])

            rows_in = [sem(f"rows_in{k}") for k in range(2)]
            cols_turned = sem("cols_turned")
            cols_ready = sem("cols_ready")
            hid_made = sem("hid_made")
            hid_ready = sem("hid_ready")
            res_made = [sem(f"res_made{k}") for k in range(2)]
            res_ready = sem("res_ready")
            res_stored = [sem(f"res_stored{k}") for k in range(2)]

            nc.all_engine_barrier()
            block = ctx.enter_context(nc.Block())

            TURNS = EXPERTS // 2

            def slot_rows(dram, e):
                return dram.rearrange("(e s p) c -> e p s c", s=ST, p=P)[bass.ds(e, 1)].rearrange("a p s c -> (a p) s c")

            @block.sync
            def _(sp):
                def load_rows(e, k):
                    sp.dma_start(rows[k][:], slot_rows(slots_dram, e)).then_inc(rows_in[k], 16)

                def store(turn, k):
                    sp.wait_ge(res_ready, 1 + turn * 2 + k + 1)
                    sp.nop(nofuse=True)
                    sp.dma_start(slot_rows(results_dram, turn * 2 + k), result[k][:]).then_inc(res_stored[k], 16)

                for k in range(2):
                    load_rows(k, k)
                with sp.Fori(1, TURNS) as turn:
                    for k in range(2):
                        sp.wait_ge(res_made[k], 1 + turn)
                        sp.nop(nofuse=True)
                        load_rows(turn * 2 + k, k)
                        load_weights(sp, turn * 2 + k, k)
                        store(turn - 1, k)
                for k in range(2):
                    store(TURNS - 1, k)
                for k in range(2):
                    sp.wait_ge(res_stored[k], 1 + 16 * TURNS)

            @block.scalar
            def _(act):
                with act.Fori(0, TURNS) as turn:
                    for k in range(2):
                        e = turn * 2 + k
                        for pair in range(HC // 2):
                            act.wait_ge(hid_made, 1 + e * (HC // 2) + pair + 1)
                            act.activation(hidden[k][:, 2 * pair:2 * pair + 2, :],
                                           ps_hid[pair % 2][:].rearrange("p (a s) -> p a s", a=2), ACT.Gelu)\
                               .then_inc(hid_ready, 1)

            @block.vector
            def _(dve):
                def take_cols(e, k):
                    dve.wait_ge(cols_turned, 1 + e + 1)
                    dve.tensor_copy(cols[k][:].rearrange("p k s -> p (k s)"), ps_cols[:]).then_inc(cols_ready, 1)

                def part(turn, last):
                    for k in range(2):
                        if not (last and k):
                            take_cols(turn * 2 + k + 1, 1 - k)
                        dve.wait_ge(res_made[k], 1 + turn + 1)
                        dve.wait_ge(res_stored[k], 1 + turn * 16)
                        dve.tensor_copy(result[k][:].rearrange("p s c -> p (s c)"), ps_res[:]).then_inc(res_ready, 1)

                take_cols(0, 0)
                with dve.Fori(0, TURNS - 1) as turn:
                    part(turn, False)
                part(TURNS - 1, True)

            @block.tensor
            def _(pe):
                def turn_rows(e, turn, k):
                    pe.wait_ge(rows_in[k], 1 + (turn + 1) * 16)
                    pe.wait_ge(cols_ready, 1 + e)
                    for c in range(KC):
                        for s in range(ST):
                            last = pe.transpose(ps_cols[:, c * CAPACITY + s * P:c * CAPACITY + (s + 1) * P],
                                                rows[k][:, s, c * P:(c + 1) * P], ident[:])
                    last.then_inc(cols_turned, 1)

                def part(turn, last_turn):
                    for k in range(2):
                        e = turn * 2 + k
                        pe.wait_ge(cols_ready, 1 + e + 1)
                        pe.wait_ge(weights_in[k], 1 + (turn + 1) * 32)
                        for pair in range(HC // 2):
                            if pair >= 2:
                                pe.wait_ge(hid_ready, 1 + e * (HC // 2) + pair - 1)
                            else:
                                pe.wait_ge(hid_ready, 1 + e * (HC // 2))
                            for m in range(2):
                                for c in range(KC):
                                    last = pe.matmul(ps_hid[pair % 2][:, m * CAPACITY:(m + 1) * CAPACITY],
                                                     up_w[k][:, c, (2 * pair + m) * P:(2 * pair + m + 1) * P],
                                                     cols[k][:, c, :], start=(c == 0), stop=(c == KC - 1))
                            last.then_inc(hid_made, 1)
                        if not (last_turn and k):
                            turn_rows(e + 1, turn + k, 1 - k)
                        pe.wait_ge(hid_ready, 1 + (e + 1) * (HC // 2))
                        pe.wait_ge(res_ready, 1 + e)
                        for s in range(ST):
                            for m in range(HC):
                                last = pe.matmul(ps_res[:, s * C:(s + 1) * C], hidden[k][:, m, s * P:(s + 1) * P],
                                                 down_w[k][:, m, :], start=(m == 0), stop=(m == HC - 1))
                        last.then_inc(res_made[k], 1)

                turn_rows(0, 0, 0)
                with pe.Fori(0, TURNS - 1) as turn:
                    part(turn, False)
                part(TURNS - 1, True)

        with ExitStack() as ctx:
            RING = 8
            got = sb("got", [P, RING, C], ctx=ctx)
            fetched = [sem(f"fetched{k}", start=0) for k in range(RING)]
            added = sem("added")
            stored = sem("stored")
            nc.all_engine_barrier()
            block = ctx.enter_context(nc.Block())

            @block.gpsimd
            def _(pool):
                for t in range(NT):
                    if t >= RING:
                        pool.wait_ge(added, 1 + t - RING + 1)
                    pool.indirect_dma_start(
                        out=got[:, t % RING, :], out_offset=None, in_=results_dram,
                        in_offset=bass.IndirectOffsetOnAxis(ap=fetch_at[:, t:t + 1].bitcast(U32), axis=0),
                        bounds_check=KEPT - 1, oob_is_err=False).then_inc(fetched[t % RING], 16)

            @block.vector
            def _(dve):
                for t in range(NT):
                    dve.wait_ge(fetched[t % RING], 16 * (t // RING + 1))
                    dve.scalar_tensor_tensor(out=base[:, t, :], in0=got[:, t % RING, :], scalar=weight[:, t:t + 1],
                                             in1=base[:, t, :], op0=ALU.mult, op1=ALU.add).then_inc(added, 1)

            @block.sync
            def _(sp):
                with sp.Fori(0, BATCH) as b:
                    sp.wait_ge(added, 1 + (b + 1) * TILES)
                    sp.nop(nofuse=True)
                    sp.dma_start(x_out[bass.ds(b * TILES, TILES)].rearrange("n p c -> p n c"),
                                 base[:, bass.ds(b * TILES, TILES), :]).then_inc(stored, 16)
                sp.wait_ge(stored, 1 + 16 * BATCH)


FIELDS = 6
FA, FW, FR, FB, FK, FV = range(FIELDS)
PACK = FIELDS * D
SPAN = 16
PAIRS = SPAN // 2
STATE = D * D
RING = 4
TURN_SPANS = 4


def recurrence(nc, packed, o_out):
    with ExitStack() as ctx:
        def sb(name, shape, dt=F32):
            return ctx.enter_context(nc.sbuf_tensor("sc_" + name, shape, dt))

        def psum(name, shape):
            return ctx.enter_context(nc.psum_tensor("sc_" + name, shape, F32))

        sem = ctx.enter_context(semaphores(nc, "sc_"))

        pack = [sb(f"pack{n}", [P, SPAN, PACK]) for n in range(4)]
        outer = [sb(f"outer{n}", [P, SPAN, STATE]) for n in range(2)]
        seen = sb("seen", [P, 2 * PAIRS, STATE])
        terms = [sb(f"terms{n}", [P, SPAN, STATE]) for n in range(2)]
        dot_terms = sb("dot_terms", [P, PAIRS, 2, 2, D])
        dots = [sb(f"dots{n}", [P, PAIRS, 2, 2]) for n in range(4)]
        b_part = sb("b_part", [P, PAIRS, 2, D])
        from_v = [sb(f"from_v{n}", [P, PAIRS, D]) for n in range(4)]
        from_u = [sb(f"from_u{n}", [P, PAIRS, D]) for n in range(2)]
        o_buf = [sb(f"o_buf{n}", [P, SPAN * D]) for n in range(2)]
        ident = sb("ident", [P, P])
        u = [sb(f"u{n}", [P, PAIRS, 2, D]) for n in range(2)]
        rank = sb("rank", [P, 2, STATE])
        decayed = sb("decayed", [P, STATE])
        state = psum("state", [P, RING, STATE])
        prod = psum("prod", [P, 2 * STATE])
        partial = psum("partial", [P, STATE])
        added = [psum(f"added{n}", [P, STATE]) for n in range(2)]
        ps_o = [psum(f"ps_o{n}", [P, SPAN * D]) for n in range(2)]

        NSPANS = T // SPAN
        COPIES = PAIRS // 2
        OPS = 7
        AHEAD = 10
        BEHIND = 6

        def counter(name, lead):
            return sem(name, start=1 + lead), 1 + lead

        chain, CHAIN = counter("chain", 4 * OPS)
        times, TIMES = counter("times", 4 * BEHIND)
        copied, COPIED = counter("copied", COPIES)
        added_made, ADDED = counter("added_made", 2 * PAIRS)
        o_made, O_MADE = counter("o_made", 4)
        o_copied, O_COPIED = counter("o_copied", 4)
        consts = sem("consts")
        packed_in = [sem(f"packed_in{n}") for n in range(4)]
        pre = sem("pre")
        dots_made = sem("dots_made")
        o_stored = [sem(f"o_stored{n}") for n in range(2)]

        nc.all_engine_barrier()
        block = ctx.enter_context(nc.Block())

        def spans(eng, part):
            for m in range(TURN_SPANS):
                part(m, 0, m)
            last = NSPANS // TURN_SPANS - 1
            with eng.Fori(1, last) as i:
                for m in range(TURN_SPANS):
                    part(i * TURN_SPANS + m, i, m)
            for m in range(TURN_SPANS):
                part(last * TURN_SPANS + m, last, m)

        def there(g, i, m, shift):
            if isinstance(g, int) and not 0 <= g + shift < NSPANS:
                return None
            return g + shift, i + (m + shift) // TURN_SPANS, (m + shift) % TURN_SPANS

        def by_pair(m):
            return pack[m % 4][:].rearrange("p (n s) f -> p n s f", s=2)

        def vectors(m, step, field):
            return by_pair(m)[:, :, step, field * D:(field + 1) * D]

        def two_vectors(m, step, field):
            return by_pair(m)[:, :, step, field * D:(field + 2) * D].rearrange("p n (f d) -> p n f d", d=D)

        @block.sync
        def _(sp):
            def load(g, i, m):
                sp.wait_ge(times, TIMES + (g - 3) * BEHIND)
                sp.nop(nofuse=True)
                for b in range(BATCH):
                    sp.dma_start(pack[m % 4][b * HEADS:(b + 1) * HEADS, :, :],
                                 packed[b, bass.ds(g * SPAN, SPAN)].rearrange("t h f -> h t f"))\
                      .then_inc(packed_in[m % 4], 16)

            def store(g, i, m):
                sp.wait_ge(o_copied, O_COPIED + g + 1)
                sp.nop(nofuse=True)
                for b in range(BATCH):
                    sp.dma_start(o_out[b, bass.ds(g * SPAN, SPAN)].rearrange("t h d -> h t d"),
                                 o_buf[m % 2][b * HEADS:(b + 1) * HEADS, :].rearrange("p (t d) -> p t d", d=D))\
                      .then_inc(o_stored[m % 2], 16)

            for g in range(3):
                load(g, 0, g)

            def part(*at):
                ahead, behind = there(*at, 3), there(*at, -3)
                if ahead:
                    load(*ahead)
                if behind:
                    store(*behind)

            spans(sp, part)
            for g in range(NSPANS - 3, NSPANS):
                store(g, g // TURN_SPANS, g % TURN_SPANS)
            for n in range(2):
                sp.wait_ge(o_stored[n], 1 + NSPANS // 2 * 16 * BATCH)

        @block.gpsimd
        def _(pool):
            own = Tally(pool, consts)
            own.link(pool.memset(ident[:], 0.0))
            own.up(pool.memset(seen[:, 2 * PAIRS - 1, :], 0.0))
            own.up(pool.affine_select(out=ident[:], in_=ident[:], compare_op=ALU.not_equal, fill=1.0, base=0,
                                      pattern=[[-1, P]], channel_multiplier=1))
            own.done()
            pairwise = [P, PAIRS, 2, D]

            def dot_products(g, i, m):
                pool.wait_ge(packed_in[m % 4], 1 + (i + 1) * 16 * BATCH)
                pool.wait_ge(dots_made, 1 + g)
                for n, (step, field) in enumerate(((1, FA), (0, FR))):
                    pool.tensor_tensor(dot_terms[:, :, n, :, :], two_vectors(m, 0, FB),
                                       vectors(m, step, field).unsqueeze(2).broadcast_to(pairwise), ALU.mult)\
                        .then_inc(pre, 1)

            def prepare_span(g, i, m):
                own = Tally(pool, pre, g * AHEAD + 2)
                pool.wait_ge(dots_made, 1 + g + 1)
                own.up(pool.tensor_tensor(two_vectors(m, 0, FB), two_vectors(m, 0, FB),
                                          vectors(m, 1, FW).unsqueeze(2).broadcast_to(pairwise), ALU.mult))
                own.up(pool.tensor_tensor(b_part[:], dots[m % 4][:, :, 0, :].unsqueeze(3).broadcast_to(pairwise),
                                          vectors(m, 1, FB).unsqueeze(2).broadcast_to(pairwise), ALU.mult))
                own.done()
                own.up(pool.tensor_tensor(two_vectors(m, 0, FB), two_vectors(m, 0, FB), b_part[:], ALU.add))
                own.up(pool.tensor_tensor(two_vectors(m, 1, FA), two_vectors(m, 1, FA),
                                          vectors(m, 0, FW).unsqueeze(2).broadcast_to(pairwise), ALU.mult))
                own.up(pool.tensor_tensor(vectors(m, 0, FR), vectors(m, 0, FR), vectors(m, 0, FW), ALU.mult))
                pool.wait_ge(o_made, O_MADE + g - 3)
                own.up(pool.tensor_tensor(from_v[m % 4][:], vectors(m, 0, FV),
                                          dots[m % 4][:, :, 1, 1:2].broadcast_to([P, PAIRS, D]), ALU.mult))
                own.done()
                pool.wait_ge(added_made, ADDED + (g - 1) * PAIRS)
                for half in range(2):
                    t = slice(half * PAIRS, (half + 1) * PAIRS)
                    shape = [P, PAIRS, D, D]
                    own.up(pool.tensor_tensor(
                        outer[m % 2][:, t, :].rearrange("p t (i j) -> p t i j", j=D),
                        pack[m % 4][:, t, FV * D:(FV + 1) * D].unsqueeze(3).broadcast_to(shape),
                        pack[m % 4][:, t, FK * D:(FK + 1) * D].unsqueeze(2).broadcast_to(shape), ALU.mult))
                assert own.n + 2 == AHEAD

            def read_states(g, i, m):
                pool.wait_ge(o_made, O_MADE + g - 1)
                made = 0

                def product(slot, pair, n, step):
                    shape = [P, n, D, D]
                    return pool.tensor_tensor(
                        terms[m % 2][:].rearrange("p (n s) (i j) -> p n s i j", s=2, j=D)[:, pair:pair + n, step],
                        seen[:, slot:slot + n, :].rearrange("p n (i j) -> p n i j", j=D),
                        vectors(m, step, FR)[:, pair:pair + n, :].unsqueeze(2).broadcast_to(shape), ALU.mult)

                first = m % 2 * PAIRS
                for half in range(2):
                    pair, n = half * PAIRS // 2, PAIRS // 2
                    pool.wait_ge(copied, COPIED + g * COPIES + (half + 1) * COPIES // 2)
                    product(first + pair, pair, n, 1).then_inc(times, 1)
                    if first + pair == 0:
                        product(2 * PAIRS - 1, 0, 1, 0).then_inc(times, 1)
                        product(0, 1, n - 1, 0).then_inc(times, 1)
                        made += 3
                    else:
                        last = pair == PAIRS // 2
                        more = BEHIND - 1 - made - 1 if last else 1
                        product(first + pair - 1, pair, n, 0).then_inc(times, more)
                        made += 1 + more
                pool.tensor_tensor(from_u[m % 2][:], u[m % 2][:, :, 0, :],
                                   dots[m % 4][:, :, 1, 0:1].broadcast_to([P, PAIRS, D]), ALU.mult)\
                    .then_inc(times, 1)
                assert made + 1 == BEHIND

            dot_products(0, 0, 0)
            prepare_span(0, 0, 0)

            def part(*at):
                ahead, behind = there(*at, 1), there(*at, -1)
                if ahead:
                    dot_products(*ahead)
                if behind:
                    read_states(*behind)
                if ahead:
                    prepare_span(*ahead)

            spans(pool, part)
            read_states(NSPANS - 1, NSPANS // TURN_SPANS - 1, TURN_SPANS - 1)

        @block.vector
        def _(dve):
            dve.memset(state[:, RING - 1, :], 0.0).then_inc(chain, 1)
            square, two = [P, D, D], [P, 2, D, D]

            def sum_dots(g, i, m):
                dve.wait_ge(pre, 1 + g * AHEAD + 2)
                dve.tensor_reduce(dots[m % 4][:].rearrange("p n x y -> p (n x y)"),
                                  dot_terms[:].rearrange("p n x y d -> p (n x y) d"), AX.X, ALU.add)\
                   .then_inc(dots_made, 1)

            sum_dots(0, 0, 0)

            def part(g, i, m):
                ahead = there(g, i, m, 1)
                for pair in range(PAIRS):
                    q = g * PAIRS + pair
                    slot = (m * PAIRS + pair) % RING
                    base = CHAIN + 1 + q * OPS
                    old = state[:, (slot - 1) % RING, :].rearrange("p (i j) -> p i j", j=D)
                    steps = pack[m % 4][:, 2 * pair:2 * pair + 2, :]
                    if pair == 0:
                        dve.wait_ge(pre, 1 + g * AHEAD + AHEAD - 2)
                        dve.wait_ge(times, TIMES + (g - 1) * BEHIND)
                    dve.wait_ge(chain, base)
                    dve.tensor_tensor(prod[:].rearrange("p (s i j) -> p s i j", s=2, j=D),
                                      old.unsqueeze(1).broadcast_to(two),
                                      steps[:, :, FA * D:(FA + 1) * D].unsqueeze(2).broadcast_to(two), ALU.mult)\
                       .then_inc(chain, 1)
                    dve.tensor_tensor(decayed[:].rearrange("p (i j) -> p i j", j=D), old,
                                      steps[:, 1, FW * D:(FW + 1) * D].unsqueeze(1).broadcast_to(square), ALU.mult).then_inc(chain, 1)
                    dve.wait_ge(chain, base + 1)
                    dve.tensor_reduce(u[m % 2][:, pair, :, :].rearrange("p s i -> p (s i)"),
                                      prod[:].rearrange("p (n j) -> p n j", j=D), AX.X, ALU.add).then_inc(chain, 1)
                    dve.wait_ge(chain, base + 3)
                    for s in range(2):
                        dve.tensor_tensor(rank[:, s, :].rearrange("p (i j) -> p i j", j=D),
                                          u[m % 2][:, pair, s, :].unsqueeze(2).broadcast_to(square),
                                          steps[:, s, FB * D:(FB + 1) * D].unsqueeze(1).broadcast_to(square),
                                          ALU.mult).then_inc(chain, 1)
                    if pair % 2 == 0:
                        dve.wait_ge(copied, COPIED + g * COPIES + pair // 2 - 1)
                    dve.wait_ge(added_made, ADDED + q + 1)
                    dve.wait_ge(chain, base + 4)
                    dve.tensor_tensor(partial[:], added[pair % 2][:], rank[:, 0, :], ALU.add).then_inc(chain, 1)
                    dve.wait_ge(chain, base + 6)
                    dve.tensor_tensor(state[:, slot, :], partial[:], rank[:, 1, :], ALU.add).then_inc(chain, 1)
                    if pair == PAIRS // 2 and ahead:
                        sum_dots(*ahead)

            spans(dve, part)
            dve.wait_ge(chain, CHAIN + 1 + NSPANS * PAIRS * OPS)
            dve.memset(rank[:], 0.0).then_inc(chain, 2)

        @block.scalar
        def _(act):
            def bring(g, i, m, n):
                pair = 2 * n
                if n in (0, COPIES - 1):
                    act.wait_ge(times, TIMES + (g - 1 if n == 0 else g) * BEHIND)
                act.wait_ge(chain, CHAIN + 1 + (g * PAIRS + pair + 2) * OPS + 2)
                slot, to = (m * PAIRS + pair) % RING, m % 2 * PAIRS + pair
                act.activation(seen[:, to:to + 2, :], state[:, slot:slot + 2, :], ACT.Copy).then_inc(copied, 1)

            def copy_o(g, i, m):
                act.wait_ge(o_made, O_MADE + g + 1)
                act.wait_ge(o_stored[m % 2], 1 + (i * 2 + m // 2) * 16 * BATCH)
                act.activation(o_buf[m % 2][:], ps_o[m % 2][:], ACT.Copy).then_inc(o_copied, 1)

            act.wait_ge(consts, 1 + 3)

            def part(*at):
                behind = there(*at, -3)
                for n in range(COPIES):
                    bring(*at, n)
                    if n == 1 and behind:
                        copy_o(*behind)

            spans(act, part)
            for g in range(NSPANS - 3, NSPANS):
                copy_o(g, g // TURN_SPANS, g % TURN_SPANS)

        @block.tensor
        def _(pe):
            pe.wait_ge(consts, 1 + 3)

            def add_outers(g, i, m, n):
                if n in (0, PAIRS // 2):
                    pe.wait_ge(pre, 1 + g * AHEAD + AHEAD - 1 + n // (PAIRS // 2))
                pe.wait_ge(chain, CHAIN + 1 + (g * PAIRS + n - 2) * OPS + 6)
                for s in range(2):
                    pe.matmul(added[n % 2][:], ident[:], outer[m % 2][:, 2 * n + s, :], start=(s == 0), stop=False)

            def add_decayed(g, n):
                pe.wait_ge(chain, CHAIN + 1 + (g * PAIRS + n) * OPS + 2)
                pe.matmul(added[n % 2][:], ident[:], decayed[:], start=False, stop=True).then_inc(added_made, 1)

            def add_terms(g, i, m, n):
                if n == 0:
                    pe.wait_ge(times, TIMES + (g + 1) * BEHIND)
                    pe.wait_ge(o_copied, O_COPIED + g - 1)
                by_column = terms[m % 2][:].rearrange("p t (i j) -> p (t i) j", j=D)
                share = D // PAIRS
                for j in range(n * share, (n + 1) * share):
                    last = pe.matmul(ps_o[m % 2][:], ident[:], by_column[:, :, j], start=(j == 0), stop=(j == D - 1))
                    if j == share:
                        first_steps = ps_o[m % 2][:].rearrange("p (n s d) -> p n s d", s=2, d=D)[:, :, 0, :]
                        pe.matmul(first_steps, ident[:], from_u[m % 2][:], start=False, stop=False)
                        pe.matmul(first_steps, ident[:], from_v[m % 4][:], start=False, stop=False)
                if n == PAIRS - 1:
                    last.then_inc(o_made, 1)

            add_outers(0, 0, 0, 0)

            def part(*at):
                ahead, behind = there(*at, 1), there(*at, -2)
                for n in range(PAIRS):
                    if n + 1 < PAIRS:
                        add_outers(*at, n + 1)
                    elif ahead:
                        add_outers(*ahead, 0)
                    add_decayed(at[0], n)
                    if behind:
                        add_terms(*behind, n)

            spans(pe, part)
            for g in range(NSPANS - 2, NSPANS):
                for n in range(PAIRS):
                    add_terms(g, g // TURN_SPANS, g % TURN_SPANS, n)


RW, RG = 64, 128
MIXES = ("r", "w", "a", "v", "k")
PREPARE_SLOTS = 4

PREPARE_USER = {"turn_x": "act", "r": "act", "turn_r": "act", "w_inner": "act", "g_inner": "act", "w": "dve",
                "a_inner": "act", "g": "dve", "a": "dve", "v": "act", "k": "dve"}


def prepare_start():
    return [("normalise", 0), ("turn_x", 0), ("turn_x", 1), ("mix", "r"), ("mix", "w")]


def prepare_turn(ahead):
    halves = lambda stage: [(stage, 0), (stage, 1)]
    plus = lambda jobs: [("+" + stage, what) for stage, what in jobs] if ahead else []
    return (halves("r") + halves("turn_r") + [("w_inner", 0), ("g_inner", 0), ("mix", "a")]
            + plus([("normalise", 0)]) + halves("w") + [("mix", "v"), ("a_inner", 0)] + halves("g") + halves("a") + [("mix", "k")]
            + plus(halves("turn_x")) + halves("v") + plus([("mix", "r")]) + halves("k")
            + halves("key") + plus([("mix", "w")]) + halves("bonus"))


def prepare(nc, x_in, mixes, k_k, k_a, r_k, weights, w_a, w_b, w_bias, a_a, a_b, a_bias, g_a, g_b, g_bias,
            packed, gate_out, bonus_out):
    start, turn, last_turn = (Plan(jobs, PREPARE_USER, PREPARE_SLOTS)
                              for jobs in (prepare_start(), prepare_turn(True), prepare_turn(False)))
    with ExitStack() as ctx:
        def sb(name, shape, dt=F32):
            return ctx.enter_context(nc.sbuf_tensor("pr_" + name, shape, dt))

        sem = ctx.enter_context(semaphores(nc, "pr_"))

        ctx.enter_context(nc.allow_non_contiguous_dma(reason="mixing columns"))
        slot = [ctx.enter_context(nc.psum_tensor(f"pr_slot{s}", [P, 2 * BANK], F32))
                for s in range(PREPARE_SLOTS)]
        big = {m: sb("big_" + m, [P, KC, C]) for m in "rkv"}
        mu = {m: sb("mu_" + m, [P, KC]) for m in MIXES}
        inner_a = {"w": sb("w_inner_a", [P, KC, RW]), "a": sb("a_inner_a", [P, KC, RW]), "g": sb("g_inner_a", [P, KC, RG])}
        inner_b = {"w": sb("w_inner_b", [RW, C]), "a": sb("a_inner_b", [RW, C]), "g": sb("g_inner_b", [RG, C])}
        wide = {m: sb("wide_" + m, [P, C]) for m in ("k_k", "k_a", "r_k", "w", "a", "g")}
        ident = sb("ident", [P, P])
        x = sb("x", [P, TILES, C])
        xn = sb("xn", [P, TILES, C])
        stats = sb("stats", [P, TILES, 6])
        mean_var = sb("mean_var", [P, TILES, 2])
        std = sb("std", [P, TILES])
        rstd = sb("rstd", [P, TILES])
        turned = sb("turned", [P, KC, T + 1])
        delta = sb("delta", [P, KC, T])
        mixed = {m: sb("mixed_" + m, [P, KC, T]) for m in "rwa"}
        mixed["v"], mixed["k"] = mixed["w"], mixed["a"]
        pack = [sb(f"pack{h}", [P, HALF_TILES * HEADS, PACK]) for h in range(2)]
        r_turned = sb("r_turned", [P, KC, T])
        inner = {"w": sb("w_inner", [RW, T]), "a": sb("a_inner", [RW, T]), "g": sb("g_inner", [RG, T])}
        HW = HALF_TILES * C
        r_rows = [sb(f"r_rows{h}", [P, HW]) for h in range(2)]
        gate_sb = [sb(f"gate_sb{h}", [P, HW]) for h in range(2)]
        z = {m: [sb(f"z_{m}{h}", [P, HW]) for h in range(2)] for m in "wa"}
        a_sig = z["a"]
        scaled = sb("scaled", [P, HW])
        kk = sb("kk", [P, HW])
        squares = sb("squares", [P, HW])
        norm = sb("norm", [P, HALF_TILES * HEADS])
        rr = [sb(f"rr{h}", [P, HW]) for h in range(2)]
        dots = [sb(f"dots{h}", [P, HALF_TILES * HEADS]) for h in range(2)]
        bonus = [sb(f"bonus{h}", [P, HW]) for h in range(2)]

        loaded = sem("loaded")
        consts = sem("consts")
        x_loaded = sem("x_loaded")
        var_ready = sem("var_ready")
        std_ready = sem("std_ready")
        xn_ready = sem("xn_ready")
        start_chain = sem("start_chain")
        chain = sem("chain")
        mix_ready = sem("mix_ready")
        filled = [sem(f"filled{s}") for s in range(PREPARE_SLOTS)]
        emptied = [sem(f"emptied{s}") for s in range(PREPARE_SLOTS)]
        z_used = sem("z_used")
        w_packed = sem("w_packed")
        r_packed = sem("r_packed")
        kk_ready = sem("kk_ready")
        squared = sem("squared")
        norm2_ready = sem("norm2_ready")
        norm_ready = sem("norm_ready")
        RR_FIRST = 1 + 4
        rr_ready = sem("rr_ready", start=RR_FIRST)
        bonus_ready = sem("bonus_ready")
        pack_stored = [sem(f"pack_stored{h}") for h in range(2)]
        gate_stored = [sem(f"gate_stored{h}") for h in range(2)]
        bonus_stored = [sem(f"bonus_stored{h}") for h in range(2)]
        N_LOADS = 3 + len(MIXES) + 6 + 6

        def turn_counts(plan, b):
            before = [start.uses[s] + b * turn.uses[s] for s in range(PREPARE_SLOTS)]
            return Slots(plan, before, filled, emptied)

        def run(eng, part):
            part(Slots(start, [0] * PREPARE_SLOTS, filled, emptied), None, 0)
            with eng.Fori(0, BATCH - 1) as b:
                part(turn_counts(turn, b), b, b + 1)
            part(turn_counts(last_turn, BATCH - 1), BATCH - 1, None)

        def field(h, f):
            return pack[h][:, :, f * D:(f + 1) * D]

        def by_head(ap):
            return ap.rearrange("p (n d) -> p n d", d=D)

        nc.all_engine_barrier()
        block = ctx.enter_context(nc.Block())

        @block.sync
        def _(sp):
            loads = [(big[m][:], weights[m].rearrange("(k p) n -> p k n", p=P)) for m in "rkv"]
            loads += [(mu[m][:], mixes[m].rearrange("(k p) -> p k", p=P)) for m in MIXES]
            loads += [(inner_a[m][:], src.rearrange("(k p) n -> p k n", p=P)) for m, src in
                      (("w", w_a), ("a", a_a), ("g", g_a))]
            loads += [(inner_b[m][:], src) for m, src in (("w", w_b), ("a", a_b), ("g", g_b))]
            loads += [(wide[m][:], spread(src)) for m, src in
                      (("k_k", k_k), ("k_a", k_a), ("r_k", r_k), ("w", w_bias), ("a", a_bias), ("g", g_bias))]
            assert len(loads) == N_LOADS
            for dst, src in loads:
                sp.dma_start(dst, src).then_inc(loaded, 16)

            def load_x(f):
                sp.wait_ge(xn_ready, 1 + f * TILES)
                sp.nop(nofuse=True)
                sp.dma_start(x[:], x_in[bass.ds(f * TILES, TILES)].rearrange("n p c -> p n c"))\
                  .then_inc(x_loaded, 16)

            def store(slots, b, next_x):
                for h in range(2):
                    rows = bass.ds(b * TILES + h * HALF_TILES, HALF_TILES)
                    slots.wait_read(sp, ("g", h), alone=True)
                    sp.dma_start(gate_out[rows].rearrange("n p c -> p n c"),
                                 gate_sb[h][:].rearrange("p (n c) -> p n c", c=C)).then_inc(gate_stored[h], 16)
                if next_x is not None:
                    load_x(next_x)
                for h in range(2):
                    rows = bass.ds(b * TILES + h * HALF_TILES, HALF_TILES)
                    sp.wait_ge(bonus_ready, 1 + b * 2 + h + 1)
                    sp.nop(nofuse=True)
                    sp.dma_start(bonus_out[rows].rearrange("n p c -> p n c"),
                                 bonus[h][:].rearrange("p (n c) -> p n c", c=C)).then_inc(bonus_stored[h], 16)
                    for packed_field in (w_packed, r_packed):
                        sp.wait_ge(packed_field, 1 + b * 2 + h + 1)
                        sp.nop(nofuse=True)
                    sp.dma_start(packed[rows].rearrange("n p f -> p n f"),
                                 pack[h][:].rearrange("p (n h) f -> p n (h f)", h=HEADS)).then_inc(pack_stored[h], 16)

            load_x(0)
            load_x(1)
            with sp.Fori(0, BATCH - 2) as b:
                store(turn_counts(turn, b), b, b + 2)
            store(turn_counts(turn, BATCH - 2), BATCH - 2, None)
            store(turn_counts(last_turn, BATCH - 1), BATCH - 1, None)
            for h in range(2):
                for kind in (gate_stored, bonus_stored, pack_stored):
                    sp.wait_ge(kind[h], 1 + BATCH * 16)

        @block.gpsimd
        def _(pool):
            own = Tally(pool, consts)
            own.up(pool.memset(turned[:], 0.0))
            own.link(pool.memset(ident[:], 0.0))
            own.up(pool.affine_select(out=ident[:], in_=ident[:], compare_op=ALU.not_equal, fill=1.0, base=0,
                                      pattern=[[-1, P]], channel_multiplier=1))
            pool.wait_ge(loaded, 1 + 16 * N_LOADS)
            r_k_wide = wide["r_k"][:].unsqueeze(1).broadcast_to([P, HALF_TILES, C])\
                .rearrange("p n (h d) -> p n h d", d=D)

            def part(slots, b, f):
                for stage, what, s, use in slots.plan.jobs:
                    if stage == "r":
                        slots.wait_read(pool, ("r", what))
                        pool.wait_ge(bonus_ready, 1 + b * 2)
                        pool.tensor_tensor(rr[what][:].rearrange("p (n h d) -> p n h d", d=D, h=HEADS),
                                           r_rows[what][:].rearrange("p (n h d) -> p n h d", d=D, h=HEADS),
                                           r_k_wide, ALU.mult).then_inc(rr_ready, 1)
                    elif stage == "key":
                        slots.wait_read(pool, ("k", what))
                        pool.wait_ge(rr_ready, RR_FIRST + b * 4 + what + 1)
                        pool.tensor_tensor(by_head(rr[what][:]), by_head(rr[what][:]), field(what, FK), ALU.mult)\
                            .then_inc(rr_ready, 1)

            run(pool, part)

        @block.tensor
        def _(pe):
            pe.wait_ge(consts, 1 + 3)
            pe.wait_ge(loaded, 1 + 16 * N_LOADS)

            def wait_mixed(b, m):
                pe.wait_ge(mix_ready, 1 + b * len(MIXES) + MIXES.index(m) + 1)
                return mixed[m]

            def part(slots, b, f):
                for full_stage, what, s, use in slots.plan.jobs:
                    if s is None:
                        continue
                    stage = full_stage.lstrip("+")
                    ps = slot[s]
                    slots.wait_empty(pe, s, use)
                    if stage == "turn_x":
                        if what == 0:
                            pe.wait_ge(xn_ready, 1 + (f + 1) * TILES)
                        for t in range(TILES):
                            last = pe.transpose(ps[:, t * P:(t + 1) * P], xn[:, t, what * P:(what + 1) * P], ident[:])
                    elif stage in ("r", "k", "v"):
                        src = wait_mixed(b, stage)
                        for n in range(HALF_TILES):
                            t = HALF_TILES * what + n
                            for k in range(KC):
                                last = pe.matmul(ps[:, n * C:(n + 1) * C], src[:, k, t * P:(t + 1) * P],
                                                 big[stage][:, k, :], start=(k == 0), stop=(k == KC - 1))
                    elif stage == "turn_r":
                        if what == 0:
                            slots.wait_read(pe, ("r", 0), ("r", 1))
                        for t in range(TILES):
                            n = (t % HALF_TILES) * C + what * P
                            last = pe.transpose(ps[:, t * P:(t + 1) * P], r_rows[t // HALF_TILES][:, n:n + P],
                                                ident[:])
                    elif stage in ("w_inner", "a_inner", "g_inner"):
                        m = stage[0]
                        if m == "g":
                            slots.wait_read(pe, ("turn_r", 0), ("turn_r", 1))
                            src = r_turned
                        else:
                            src = wait_mixed(b, m)
                        width = inner_a[m].shape[2]
                        for half in range(2):
                            for k in range(KC):
                                last = pe.matmul(ps[0:width, half * BANK:(half + 1) * BANK], inner_a[m][:, k, :],
                                                 src[:, k, half * BANK:(half + 1) * BANK],
                                                 start=(k == 0), stop=(k == KC - 1))
                    else:
                        if what == 0:
                            slots.wait_read(pe, (stage + "_inner", 0))
                        for n in range(HALF_TILES):
                            t = HALF_TILES * what + n
                            last = pe.matmul(ps[:, n * C:(n + 1) * C], inner[stage][:, t * P:(t + 1) * P],
                                             inner_b[stage][:], start=True, stop=True)
                    last.then_inc(filled[s], 1)

            run(pe, part)

        @block.scalar
        def _(act):
            act.wait_ge(consts, 1 + 3)

            def part(slots, b, f):
                for full_stage, what, s, use in slots.plan.jobs:
                    stage = full_stage.lstrip("+")
                    if PREPARE_USER.get(stage) == "act":
                        ps = slot[s]
                        slots.wait_filled(act, s, use)
                    if stage == "normalise":
                        act.wait_ge(var_ready, 1 + f + 1)
                        act.activation(std[:], mean_var[:, :, 1], ACT.Sqrt).then_inc(std_ready, 1)
                    elif stage == "turn_x":
                        if what == 0:
                            act.wait_ge(mix_ready, 1 + f * len(MIXES))
                        act.activation(turned[:, what, 1:T + 1], ps[:], ACT.Copy).then_inc(emptied[s], 1)
                    elif stage == "r":
                        act.wait_ge(rr_ready, RR_FIRST + (b - 1) * 4 + what + 1)
                        act.activation(r_rows[what][:], ps[:], ACT.Copy).then_inc(emptied[s], 1)
                    elif stage == "v":
                        act.wait_ge(pack_stored[what], 1 + b * 16)
                        act.wait_ge(z_used, 1 + b * 4 + what + 1)
                        act.activation(field(what, FW), by_head(z["w"][what][:]), ACT.Copy, scale=float(np.exp(-0.5)))\
                           .then_inc(w_packed, 1)
                        act.activation(field(what, FR), by_head(r_rows[what][:]), ACT.Copy).then_inc(r_packed, 1)
                        act.activation(field(what, FV), by_head(ps[:]), ACT.Copy).then_inc(emptied[s], 1)
                    elif stage == "turn_r":
                        act.activation(r_turned[:, what, :], ps[:], ACT.Copy).then_inc(emptied[s], 1)
                    elif stage in ("w_inner", "a_inner", "g_inner"):
                        m = stage[0]
                        width = inner_a[m].shape[2]
                        act.activation(inner[m][:], ps[0:width, :],
                                       {"w": ACT.Tanh, "a": ACT.Copy, "g": ACT.Sigmoid}[m]).then_inc(emptied[s], 1)
                    elif stage == "w":
                        slots.wait_read(act, (stage, what))
                        act.activation(z["w"][what][:], z["w"][what][:], ACT.Sigmoid).then_inc(z_used, 1)
                    elif stage == "a":
                        slots.wait_read(act, (stage, what))
                        act.activation(a_sig[what][:], a_sig[what][:], ACT.Sigmoid).then_inc(z_used, 1)
                    elif stage == "key":
                        act.wait_ge(kk_ready, 1 + b * 2 + what + 1)
                        act.activation(squares[:], kk[:], ACT.Square).then_inc(squared, 1)
                        act.wait_ge(norm2_ready, 1 + b * 2 + what + 1)
                        act.activation(norm[:], norm[:], ACT.Sqrt).then_inc(norm_ready, 1)

            run(act, part)

        @block.vector
        def _(dve):
            dve.wait_ge(consts, 1 + 3)
            dve.wait_ge(loaded, 1 + 16 * N_LOADS)
            START, TURN = 2 * TILES + 1 + KC, 2 * 6
            wide_of = {m: wide[m][:].unsqueeze(1).broadcast_to([P, HALF_TILES, C]) for m in wide}

            def by_tile(ap):
                return ap.rearrange("p (n c) -> p n c", c=C)

            def mix(slots, m):
                reader = {"r": ("r", 1), "w": ("v", 1), "a": ("r", 1), "v": ("w_inner", 0), "k": ("a_inner", 0)}[m]
                if reader in slots.plan.place:
                    slots.wait_filled(dve, *slots.plan.place[reader])
                for k in range(KC):
                    ins = dve.scalar_tensor_tensor(out=mixed[m][:, k, :], in0=delta[:, k, :],
                                                   scalar=mu[m][:, k:k + 1], in1=turned[:, k, 1:T + 1],
                                                   op0=ALU.mult, op1=ALU.add)
                ins.then_inc(mix_ready, 1)

            def part(slots, b, f):
                own = Tally(dve, chain, 0 if b is None else b * TURN)
                in_start = Tally(dve, start_chain, 0 if f is None else f * START)
                for full_stage, what, s, use in slots.plan.jobs:
                    stage = full_stage.lstrip("+")
                    mark = full_stage[:-len(stage)]
                    if stage == "normalise":
                        dve.wait_ge(x_loaded, 1 + (f + 1) * 16)
                        for t in range(TILES):
                            in_start.up(dve.bn_stats(stats[:, t, :], x[:, t, :]))
                        in_start.done()
                        dve.nop(nofuse=True)
                        for t in range(TILES):
                            in_start.up(dve.bn_aggr(mean_var[:, t, :], stats[:, t, :]))
                        in_start.done()
                        dve.tensor_scalar(mean_var[:, :, 1], mean_var[:, :, 1], LN_EPS, None, ALU.add)\
                           .then_inc(var_ready, 1)
                        dve.wait_ge(std_ready, 1 + f + 1)
                        in_start.link(dve.reciprocal(rstd[:], std[:]))
                        for t in range(TILES):
                            dve.tensor_scalar(xn[:, t, :], x[:, t, :], mean_var[:, t, 0:1], rstd[:, t:t + 1],
                                              ALU.subtract, ALU.mult).then_inc(xn_ready, 1)
                    elif stage == "mix":
                        if what == "r":
                            slots.wait_read(dve, (mark + "turn_x", 0), (mark + "turn_x", 1))
                            for k in range(KC):
                                in_start.up(dve.tensor_tensor(delta[:, k, :], turned[:, k, 0:T],
                                                              turned[:, k, 1:T + 1], ALU.subtract))
                            in_start.done()
                            assert in_start.n == START
                        mix(slots, what)
                    elif stage in ("w", "a"):
                        slots.wait_filled(dve, s, use)
                        if stage == "w":
                            dve.wait_ge(w_packed, 1 + b * 2)
                        else:
                            dve.wait_ge(z_used, 1 + b * 4)
                        dve.tensor_tensor(by_tile(z[stage][what][:]), by_tile(slot[s][:]), wide_of[stage], ALU.add)\
                           .then_inc(emptied[s], 1)
                    elif stage == "g":
                        slots.wait_filled(dve, s, use)
                        dve.wait_ge(gate_stored[what], 1 + b * 16)
                        dve.tensor_tensor(by_tile(gate_sb[what][:]), by_tile(slot[s][:]), wide_of["g"], ALU.add)\
                           .then_inc(emptied[s], 1)
                    elif stage == "key":
                        s, use = slots.plan.place["k", what]
                        ps = slot[s]
                        slots.wait_filled(dve, s, use)
                        dve.wait_ge(z_used, 1 + b * 4 + 2 + what + 1)
                        own.up(dve.scalar_tensor_tensor(
                            out=by_tile(scaled[:]), in0=by_tile(a_sig[what][:]), scalar=-1.0, in1=wide_of["k_a"],
                            op0=ALU.add, op1=ALU.mult))
                        dve.wait_ge(squared, 1 + b * 2 + what)
                        dve.tensor_tensor(by_tile(kk[:]), by_tile(ps[:]), wide_of["k_k"], ALU.mult)\
                           .then_inc(kk_ready, 1)
                        dve.wait_ge(pack_stored[what], 1 + b * 16)
                        own.done()
                        dve.scalar_tensor_tensor(out=field(what, FK), in0=by_head(scaled[:]), scalar=1.0,
                                                 in1=by_head(ps[:]), op0=ALU.add, op1=ALU.mult)\
                           .then_inc(emptied[s], 1)
                        dve.wait_ge(squared, 1 + b * 2 + what + 1)
                        dve.tensor_reduce(norm[:], by_head(squares[:]), AX.X, ALU.add).then_inc(norm2_ready, 1)
                        dve.wait_ge(norm_ready, 1 + b * 2 + what + 1)
                        own.link(dve.tensor_scalar(norm[:], norm[:], 1e-12, -1.0, ALU.max, ALU.mult))
                        own.link(dve.reciprocal(norm[:], norm[:]))
                        own.link(dve.tensor_tensor(field(what, FA), by_head(kk[:]),
                                                   norm[:].unsqueeze(2).broadcast_to([P, HALF_TILES * HEADS, D]),
                                                   ALU.mult))
                        own.link(dve.scalar_tensor_tensor(out=field(what, FB), in0=field(what, FA), scalar=-1.0,
                                                          in1=by_head(a_sig[what][:]), op0=ALU.mult, op1=ALU.mult))
                    elif stage == "bonus":
                        dve.wait_ge(rr_ready, RR_FIRST + b * 4 + 2 + what + 1)
                        dve.wait_ge(bonus_ready, 1 + b * 2)
                        own.link(dve.tensor_reduce(dots[what][:], by_head(rr[what][:]), AX.X, ALU.add))
                        slots.wait_read(dve, ("v", what))
                        dve.wait_ge(bonus_stored[what], 1 + b * 16)
                        dve.tensor_tensor(by_head(bonus[what][:]), field(what, FV),
                                          dots[what][:].unsqueeze(2).broadcast_to([P, HALF_TILES * HEADS, D]), ALU.mult)\
                           .then_inc(bonus_ready, 1)
                assert b is None or own.n == TURN, own.n

            run(dve, part)


def finish(nc, x_in, o_in, gate_in, bonus_in, gn_weight, gn_bias, w_o, x_out):
    with ExitStack() as ctx:
        def sb(name, shape, dt=F32):
            return ctx.enter_context(nc.sbuf_tensor("fi_" + name, shape, dt))

        sem = ctx.enter_context(semaphores(nc, "fi_"))

        slot = [ctx.enter_context(nc.psum_tensor(f"fi_slot{s}", [P, 2 * BANK], F32)) for s in range(4)]
        w = sb("w", [P, KC, C])
        ident = sb("ident", [P, P])
        wide_w = sb("wide_w", [P, C])
        wide_b = sb("wide_b", [P, C])
        x = [sb(f"x{k}", [P, TILES, C]) for k in range(2)]
        o = [sb(f"o{k}", [P, TILES, C]) for k in range(2)]
        gate = [sb(f"gate{k}", [P, TILES, C]) for k in range(2)]
        bonus = [sb(f"bonus{k}", [P, TILES, C]) for k in range(2)]
        squares = sb("squares", [P, TILES * C])
        mean = sb("mean", [P, TILES * HEADS])
        var = sb("var", [P, TILES * HEADS])
        turned = sb("turned", [P, KC, T])

        loaded = sem("loaded")
        consts = sem("consts")
        in_ready = [sem(f"in_ready{k}") for k in range(2)]
        x_ready = [sem(f"x_ready{k}") for k in range(2)]
        chain = sem("chain")
        centred = sem("centred")
        squared = sem("squared")
        var_ready = sem("var_ready")
        std_ready = sem("std_ready")
        normed = sem("normed")
        with_bias = sem("with_bias")
        gated = sem("gated")
        TURN_MADE = 1 + 2 * KC
        turn_made = sem("turn_made", start=TURN_MADE)
        turn_ready = sem("turn_ready")
        y_made = sem("y_made")
        y_ready = sem("y_ready")
        stored = [sem(f"stored{k}") for k in range(2)]
        nc.all_engine_barrier()
        block = ctx.enter_context(nc.Block())

        @block.sync
        def _(sp):
            sp.dma_start(w[:], w_o.rearrange("(k p) n -> p k n", p=P)).then_inc(loaded, 16)
            sp.dma_start(wide_w[:], spread(gn_weight)).then_inc(loaded, 16)
            sp.dma_start(wide_b[:], spread(gn_bias)).then_inc(loaded, 16)

            def load(i, k):
                b = i * 2 + k
                rows = bass.ds(b * TILES, TILES)
                sp.wait_ge(turn_made, TURN_MADE + (b - 1) * KC)
                sp.nop(nofuse=True)
                for dst, src in ((o, o_in), (gate, gate_in), (bonus, bonus_in)):
                    sp.dma_start(dst[k][:], src[rows].rearrange("n p c -> p n c")).then_inc(in_ready[k], 16)

            def load_x(i, k):
                sp.dma_start(x[k][:], x_in[bass.ds((i * 2 + k) * TILES, TILES)].rearrange("n p c -> p n c"))\
                  .then_inc(x_ready[k], 16)

            def store(i, k):
                b = i * 2 + k
                sp.wait_ge(y_ready, 1 + b * 2 + 2)
                sp.nop(nofuse=True)
                sp.dma_start(x_out[bass.ds(b * TILES, TILES)].rearrange("n p c -> p n c"), x[k][:])\
                  .then_inc(stored[k], 16)
                sp.wait_ge(stored[k], 1 + (i + 1) * 16)
                sp.nop(nofuse=True)

            for k in range(2):
                load(0, k)
                load_x(0, k)
            with sp.Fori(1, BATCH // 2) as i:
                for k in range(2):
                    load(i, k)
                    store(i - 1, k)
                    load_x(i, k)
            for k in range(2):
                store(BATCH // 2 - 1, k)

        @block.gpsimd
        def _(pool):
            own = Tally(pool, consts)
            own.link(pool.memset(ident[:], 0.0))
            own.up(pool.affine_select(out=ident[:], in_=ident[:], compare_op=ALU.not_equal, fill=1.0, base=0,
                                      pattern=[[-1, P]], channel_multiplier=1))
            pool.wait_ge(loaded, 1 + 48)
            bias_wide = wide_b[:].unsqueeze(1).broadcast_to([P, TILES, C])
            with pool.Fori(0, BATCH // 2) as i:
                for k in range(2):
                    b = i * 2 + k
                    pool.wait_ge(in_ready[k], 1 + (i + 1) * 48)
                    pool.tensor_tensor(bonus[k][:], bonus[k][:], bias_wide, ALU.add).then_inc(with_bias, 1)

        @block.tensor
        def _(pe):
            pe.wait_ge(consts, 1 + 2)
            pe.wait_ge(loaded, 1 + 48)
            with pe.Fori(0, BATCH // 2) as i:
                for k in range(2):
                    b = i * 2 + k
                    pe.wait_ge(gated, 1 + b + 1)
                    pe.wait_ge(turn_ready, 1 + b * KC)
                    for c in range(KC):
                        for t in range(TILES):
                            last = pe.transpose(slot[c][:, t * P:(t + 1) * P], o[k][:, t, c * P:(c + 1) * P], ident[:])
                        last.then_inc(turn_made, 1)
                    pe.wait_ge(turn_ready, 1 + b * KC + KC)
                    pe.wait_ge(y_ready, 1 + b * 2)
                    for h in range(2):
                        for n in range(HALF_TILES):
                            t = h * HALF_TILES + n
                            for c in range(KC):
                                last = pe.matmul(slot[2 + h][:, n * C:(n + 1) * C], turned[:, c, t * P:(t + 1) * P],
                                                 w[:, c, :], start=(c == 0), stop=(c == KC - 1))
                        last.then_inc(y_made, 1)

        @block.scalar
        def _(act):
            def root(b, k):
                act.wait_ge(centred, 1 + b + 1)
                act.activation(squares[:], o[k][:].rearrange("p n c -> p (n c)"), ACT.Square).then_inc(squared, 1)
                act.wait_ge(var_ready, 1 + b + 1)
                act.activation(var[:], var[:], ACT.Sqrt).then_inc(std_ready, 1)

            def copy_turned(b):
                act.wait_ge(y_made, 1 + b * 2)
                for c in range(KC):
                    act.wait_ge(turn_made, TURN_MADE + b * KC + c + 1)
                    act.activation(turned[:, c, :], slot[c][:], ACT.Copy).then_inc(turn_ready, 1)

            root(0, 0)
            with act.Fori(0, BATCH // 2 - 1) as i:
                for k in range(2):
                    copy_turned(i * 2 + k)
                    root(i * 2 + k + 1, 1 - k)
            copy_turned(BATCH - 2)
            root(BATCH - 1, 1)
            copy_turned(BATCH - 1)

        @block.vector
        def _(dve):
            dve.wait_ge(loaded, 1 + 48)
            weight_wide = wide_w[:].unsqueeze(1).broadcast_to([P, TILES, C])
            LINKS = 6

            def normalise(i, k, b):
                own = Tally(dve, chain, b * LINKS)
                heads = o[k][:].rearrange("p n (h d) -> p (n h) d", d=D)
                spread_out = lambda ap: ap.unsqueeze(2).broadcast_to([P, TILES * HEADS, D])
                dve.wait_ge(in_ready[k], 1 + (i + 1) * 48)
                own.link(dve.tensor_reduce(mean[:], heads, AX.X, ALU.add))
                own.link(dve.tensor_scalar(mean[:], mean[:], 1.0 / D, None, ALU.mult))
                dve.tensor_tensor(heads, heads, spread_out(mean[:]), ALU.subtract).then_inc(centred, 1)
                dve.wait_ge(squared, 1 + b + 1)
                own.link(dve.tensor_reduce(var[:], squares[:].rearrange("p (n d) -> p n d", d=D), AX.X, ALU.add))
                dve.tensor_scalar(var[:], var[:], 1.0 / D, LN_EPS, ALU.mult, ALU.add).then_inc(var_ready, 1)
                dve.wait_ge(std_ready, 1 + b + 1)
                own.link(dve.reciprocal(var[:], var[:]))
                own.link(dve.tensor_tensor(heads, heads, spread_out(var[:]), ALU.mult))
                own.link(dve.tensor_tensor(o[k][:], o[k][:], weight_wide, ALU.mult))
                dve.wait_ge(with_bias, 1 + b + 1)
                dve.tensor_tensor(o[k][:], o[k][:], bonus[k][:], ALU.add).then_inc(normed, 1)
                dve.wait_ge(normed, 1 + b + 1)
                dve.tensor_tensor(o[k][:], o[k][:], gate[k][:], ALU.mult).then_inc(gated, 1)
                assert own.n == LINKS

            def add_x(i, k, b):
                dve.wait_ge(x_ready[k], 1 + (i + 1) * 16)
                for h in range(2):
                    dve.wait_ge(y_made, 1 + b * 2 + h + 1)
                    t = slice(h * HALF_TILES, (h + 1) * HALF_TILES)
                    dve.tensor_tensor(x[k][:, t, :], slot[2 + h][:].rearrange("p (n c) -> p n c", c=C),
                                      x[k][:, t, :], ALU.add).then_inc(y_ready, 1)

            normalise(0, 0, 0)
            with dve.Fori(0, BATCH // 2 - 1) as i:
                for k in range(2):
                    normalise(i + k, 1 - k, i * 2 + k + 1)
                    add_x(i, k, i * 2 + k)
            last = BATCH // 2 - 1
            normalise(last, 1, BATCH - 1)
            for k in range(2):
                add_x(last, k, BATCH - 2 + k)


def program(nc, a, out):
    def dram(name, shape):
        return nc.dram_tensor(name, shape, F32, kind="Internal").ap()

    def tiles(ap):
        return ap.rearrange("b (n p) c -> (b n) p c", p=P)

    x_attended, x_mixed, x_recurred = (dram(n, (NT, P, C)) for n in ("x_attended", "x_mixed", "x_recurred"))
    slots, results = dram("slots", (KEPT, C)), dram("results", (KEPT, C))
    packed = dram("packed", (NT, P, HEADS * PACK))
    gate, bonus, o = (dram(n, (NT, P, C)) for n in ("gate", "bonus", "o"))
    experts = (a["ffn_gate_weight"], a["ffn_ln_gamma"], a["ffn_ln_beta"], a["ffn_wi"], a["ffn_wo"], slots, results)

    attention(nc, tiles(a["attn_a_x"]), a["attn_a_w_attn"], a["attn_a_b_attn"], a["attn_a_w_proj"],
              a["attn_a_b_proj"], nc.dram_tensor("parts", (2 * KC, 3, P, T), BF16, kind="Internal").ap(), x_attended)
    mixture(nc, 0, x_attended, *experts, x_mixed, clear_slots=True)
    rw = {k.removeprefix("attn_b_"): v for k, v in a.items() if k.startswith("attn_b_")}
    prepare(nc, x_mixed, {m: rw["x_" + m] for m in MIXES}, rw["k_k"], rw["k_a"], rw["r_k"].rearrange("h d -> (h d)"),
            {"r": rw["W_r"], "k": rw["W_k"], "v": rw["W_v"]}, rw["w_lora_a"], rw["w_lora_b"], rw["w_lora_bias"],
            rw["a_lora_a"], rw["a_lora_b"], rw["a_lora_bias"], rw["g_lora_a"], rw["g_lora_b"], rw["g_lora_bias"],
            packed, gate, bonus)
    recurrence(nc, packed.rearrange("(b n) p (h f) -> b (n p) h f", b=BATCH, h=HEADS),
               o.rearrange("(b n) p (h d) -> b (n p) h d", b=BATCH, h=HEADS))
    finish(nc, x_mixed, o, gate, bonus, rw["gn_weight"], rw["gn_bias"], rw["W_o"], x_recurred)
    mixture(nc, 1, x_recurred, *experts, tiles(out), clear_slots=False)


_INS = ["attn_a_x", "attn_a_w_attn", "attn_a_b_attn", "attn_a_w_proj", "attn_a_b_proj",
        "attn_b_x_r", "attn_b_x_w", "attn_b_x_k", "attn_b_x_v", "attn_b_x_a", "attn_b_k_k", "attn_b_k_a",
        "attn_b_r_k", "attn_b_W_r", "attn_b_W_k", "attn_b_W_v", "attn_b_W_o", "attn_b_w_lora_a", "attn_b_w_lora_b",
        "attn_b_w_lora_bias", "attn_b_a_lora_a", "attn_b_a_lora_b", "attn_b_a_lora_bias", "attn_b_g_lora_a",
        "attn_b_g_lora_b", "attn_b_g_lora_bias", "attn_b_gn_weight", "attn_b_gn_bias",
        "ffn_gate_weight", "ffn_ln_gamma", "ffn_ln_beta", "ffn_wi", "ffn_wo"]


def kernel(**inputs):
    import concourse.bacc as _bacc
    from concourse.bass_utils import run_bass_kernel_spmd as _run

    nc = _bacc.Bacc("TRN2", target_bir_lowering=False, num_devices=1)
    arrays, args = {}, {}
    for name in _INS:
        array = np.ascontiguousarray(inputs["L0_" + name])
        arrays[f"in_{name}"] = array
        args[name] = nc.dram_tensor(f"in_{name}", array.shape, mybir.dt.from_np(array.dtype),
                                    kind="ExternalInput").ap()
    out = nc.dram_tensor("out_x", inputs["L0_attn_a_x"].shape, F32, kind="ExternalOutput").ap()
    program(nc, args, out)
    return _run(nc, [arrays], core_ids=[0]).results[0]["out_x"]
```
